# Optimizing a Trainium2 kernel written in Bass

```python
import numpy as np
import jax
import jax.numpy as jnp

def _softmax(x, axis=-1):
    return jax.nn.softmax(x, axis=axis)

def _gelu(x):
    return jax.nn.gelu(x, approximate=True)

def _silu(x):
    return jax.nn.silu(x)

def _sigmoid(x):
    return jax.nn.sigmoid(x)

def _layernorm(x, axis=-1, eps=1e-05):
    m = jnp.mean(x, axis=axis, keepdims=True)
    v = jnp.var(x, axis=axis, keepdims=True)
    return (x - m) / jnp.sqrt(v + eps)

def _scatter_add(tgt, idx, src, axis=0):
    return tgt.at[idx].add(src)

def _segment_sum(src, seg, n):
    return jax.ops.segment_sum(src, seg, n)
kernel_name = 'mk_gnn_resnorm_d4_gnn_r32_c2fb71'

def setup_inputs(seed: int=0):
    np.random.seed(seed)
    _w = jnp.asarray

    def _rec_inputs():
        import jax
        import jax.numpy as jnp
        _gk = jax.random.key(seed)
        x = -0.0003713 + 1 * jax.random.normal(jax.random.fold_in(_gk, 1), (50000, 256), jnp.float32)
        src = jax.random.randint(jax.random.fold_in(_gk, 2), (50000,), 0, 50000, jnp.int32)
        dst = jax.random.randint(jax.random.fold_in(_gk, 3), (50000,), 0, 50000, jnp.int32)
        _o = jnp.argsort(dst, stable=True)
        src = src[_o]
        dst = dst[_o]
        edge_attr_12 = -1.02531e-05 + 0.999808 * jax.random.normal(jax.random.fold_in(_gk, 12), (50000, 12), jnp.float32)
        edge_attr_3 = -1.09012e-05 + 0.99985 * jax.random.normal(jax.random.fold_in(_gk, 13), (50000, 3), jnp.float32)
        edge_weight = jax.random.uniform(jax.random.fold_in(_gk, 15), (50000,), jnp.float32, 0.0, 0.999998)
        return (x, src, dst, edge_attr_12, edge_attr_3, edge_weight)
    x, src, dst, edge_attr_12, edge_attr_3, edge_weight = _rec_inputs()

    def _L0_gnn_setup():
        import jax, jax.numpy as jnp
        import numpy as np
        N_NODES = 50000
        D = 256
        N_EDGES = 9375
        key = jax.random.key(seed)
        ks = jax.random.split(key, 6)
        s = 1.0 / np.sqrt(D)
        x = jax.random.normal(ks[0], (N_NODES, D), dtype=jnp.float32)
        edge_index = jax.random.randint(ks[1], (2, N_EDGES), 0, N_NODES, dtype=jnp.int64)
        W_l = jax.random.normal(ks[2], (D, D), dtype=jnp.float32) * s
        b_l = jnp.zeros((D,), dtype=jnp.float32)
        W_r = jax.random.normal(ks[3], (D, D), dtype=jnp.float32) * s
        W_ln = jax.random.normal(ks[4], (D, D), dtype=jnp.float32) * s
        return {'x': x, 'edge_index': edge_index, 'W_l': W_l, 'b_l': b_l, 'W_r': W_r, 'W_ln': W_ln}
    _L0_gnn_all = _L0_gnn_setup()
    _L0_gnn_in = {k: v for k, v in _L0_gnn_all.items() if k in ('W_l', 'b_l', 'W_r', 'W_ln')}
    del _L0_gnn_all

    def _L1_gnn_setup():
        import jax, jax.numpy as jnp
        import numpy as np
        N = 10000
        E = 9375
        D = 256
        key = jax.random.key(seed)
        k1, k2, k3, k4 = jax.random.split(key, 4)
        x = jax.random.normal(k1, (N, D), dtype=jnp.float32)
        edge_index = jax.random.randint(k2, (2, E), 0, N, dtype=jnp.int32)
        s = 1.0 / np.sqrt(D)
        W1 = jax.random.uniform(k3, (D, D), jnp.float32, -s, s)
        b1 = jnp.zeros((D,), jnp.float32)
        W2 = jax.random.uniform(k4, (D, D), jnp.float32, -s, s)
        b2 = jnp.zeros((D,), jnp.float32)
        return {'x': x, 'W1': W1, 'b1': b1, 'W2': W2, 'b2': b2, 'edge_index': edge_index}
    _L1_gnn_all = _L1_gnn_setup()
    _L1_gnn_in = {k: v for k, v in _L1_gnn_all.items() if k in ('W1', 'b1', 'W2', 'b2')}
    del _L1_gnn_all

    def _L2_gnn_setup():
        import jax, jax.numpy as jnp
        import numpy as np
        PI = float(np.pi)
        CUTOFF = 5.0
        N_NODES = 50000
        N_EDGES = 25000
        HIDDEN = 256
        FILT = 64
        RADIAL = 12
        key = jax.random.key(seed)
        ks = jax.random.split(key, 10)
        x = jax.random.normal(ks[0], (N_NODES, HIDDEN), dtype=jnp.float32)
        rbf = jax.random.normal(ks[1], (N_EDGES, RADIAL), dtype=jnp.float32)
        dists = jax.random.uniform(ks[2], (N_EDGES,), dtype=jnp.float32)
        edge_index = jax.random.randint(ks[3], (2, N_EDGES), 0, N_NODES, dtype=jnp.int64)
        batch = jnp.zeros((N_NODES,), dtype=jnp.int64)
        s = 0.05
        W_node_to_message = jax.random.normal(ks[4], (FILT, HIDDEN), dtype=jnp.float32) * s
        W_radial_to_message = jax.random.normal(ks[5], (FILT, RADIAL), dtype=jnp.float32) * s
        W_lin1 = jax.random.normal(ks[6], (FILT, FILT), dtype=jnp.float32) * s
        W_lin2 = jax.random.normal(ks[7], (FILT, FILT), dtype=jnp.float32) * s
        b_lin2 = jax.random.normal(ks[8], (FILT,), dtype=jnp.float32) * s
        W_message_to_node = jax.random.normal(ks[9], (HIDDEN, FILT), dtype=jnp.float32) * s
        return {'x': x, 'rbf': rbf, 'dists': dists, 'edge_index': edge_index, 'batch': batch, 'W_node_to_message': W_node_to_message, 'W_radial_to_message': W_radial_to_message, 'W_lin1': W_lin1, 'W_lin2': W_lin2, 'b_lin2': b_lin2, 'W_message_to_node': W_message_to_node}
    _L2_gnn_all = _L2_gnn_setup()
    _L2_gnn_in = {k: v for k, v in _L2_gnn_all.items() if k in ('W_node_to_message', 'W_radial_to_message', 'W_lin1', 'W_lin2', 'b_lin2', 'W_message_to_node')}
    del _L2_gnn_all

    def _L3_gnn_setup():
        import jax, jax.numpy as jnp
        import numpy as np
        N = 50000
        E = 12500
        IN = 256
        H = 8
        D = 32
        EF = 3
        key = jax.random.key(seed)
        ks = jax.random.split(key, 8)
        x = jax.random.normal(ks[0], (N, IN), dtype=jnp.float32)
        edge_index = jax.random.randint(ks[1], (2, E), 0, N, dtype=jnp.int64)
        edge_attr = jax.random.normal(ks[2], (E, EF), dtype=jnp.float32)
        W = jax.random.normal(ks[3], (H * D, IN), dtype=jnp.float32) * np.float32(np.sqrt(2.0 / (IN + H * D)))
        a_src = jax.random.normal(ks[4], (H, D), dtype=jnp.float32) * np.float32(np.sqrt(2.0 / (H + D)))
        a_dst = jax.random.normal(ks[5], (H, D), dtype=jnp.float32) * np.float32(np.sqrt(2.0 / (H + D)))
        edge_W = jax.random.normal(ks[6], (H * D, EF), dtype=jnp.float32) * np.float32(np.sqrt(2.0 / (EF + H * D)))
        edge_b = jnp.zeros((H * D,), dtype=jnp.float32)
        bias = jnp.zeros((H * D,), dtype=jnp.float32)
        return {'x': x, 'W': W, 'a_src': a_src, 'a_dst': a_dst, 'edge_W': edge_W, 'edge_b': edge_b, 'bias': bias, 'edge_attr': edge_attr, 'edge_index': edge_index}
    _L3_gnn_all = _L3_gnn_setup()
    _L3_gnn_in = {k: v for k, v in _L3_gnn_all.items() if k in ('W', 'a_src', 'a_dst', 'edge_W', 'edge_b', 'bias')}
    del _L3_gnn_all
    return {'x': x, 'src': src, 'dst': dst, 'edge_attr_12': edge_attr_12, 'edge_attr_3': edge_attr_3, 'edge_weight': edge_weight, 'L0_gnn_W_l': _L0_gnn_in['W_l'], 'L0_gnn_b_l': _L0_gnn_in['b_l'], 'L0_gnn_W_r': _L0_gnn_in['W_r'], 'L0_gnn_W_ln': _L0_gnn_in['W_ln'], 'L1_gnn_W1': _L1_gnn_in['W1'], 'L1_gnn_b1': _L1_gnn_in['b1'], 'L1_gnn_W2': _L1_gnn_in['W2'], 'L1_gnn_b2': _L1_gnn_in['b2'], 'L2_gnn_W_node_to_message': _L2_gnn_in['W_node_to_message'], 'L2_gnn_W_radial_to_message': _L2_gnn_in['W_radial_to_message'], 'L2_gnn_W_lin1': _L2_gnn_in['W_lin1'], 'L2_gnn_W_lin2': _L2_gnn_in['W_lin2'], 'L2_gnn_b_lin2': _L2_gnn_in['b_lin2'], 'L2_gnn_W_message_to_node': _L2_gnn_in['W_message_to_node'], 'L3_gnn_W': _L3_gnn_in['W'], 'L3_gnn_a_src': _L3_gnn_in['a_src'], 'L3_gnn_a_dst': _L3_gnn_in['a_dst'], 'L3_gnn_edge_W': _L3_gnn_in['edge_W'], 'L3_gnn_edge_b': _L3_gnn_in['edge_b'], 'L3_gnn_bias': _L3_gnn_in['bias']}

def reference(x, src, dst, edge_attr_12, edge_attr_3, edge_weight, L0_gnn_W_l, L0_gnn_b_l, L0_gnn_W_r, L0_gnn_W_ln, L1_gnn_W1, L1_gnn_b1, L1_gnn_W2, L1_gnn_b2, L2_gnn_W_node_to_message, L2_gnn_W_radial_to_message, L2_gnn_W_lin1, L2_gnn_W_lin2, L2_gnn_b_lin2, L2_gnn_W_message_to_node, L3_gnn_W, L3_gnn_a_src, L3_gnn_a_dst, L3_gnn_edge_W, L3_gnn_edge_b, L3_gnn_bias):
    import jax
    import jax.numpy as jnp

    def _L0_gnn_ref(x, edge_index, W_l, b_l, W_r, W_ln):
        import jax, jax.numpy as jnp
        import numpy as np
        N_NODES = 50000
        D = 256
        N_EDGES = 9375
        n = x.shape[0]
        src = edge_index[0]
        dst = edge_index[1]
        msg_sum = jax.ops.segment_sum(x[src], dst, num_segments=n)
        cnt = jax.ops.segment_sum(jnp.ones_like(dst, dtype=x.dtype), dst, num_segments=n)
        mean = msg_sum / jnp.maximum(cnt, 1.0)[:, None]
        sage = mean @ W_l.T + b_l + x @ W_r.T
        out = jax.nn.relu(sage)
        out = out @ W_ln.T
        out = out + x
        return jax.nn.relu(out)

    def _L1_gnn_ref(x, W1, b1, W2, b2, edge_index):
        import jax, jax.numpy as jnp
        import numpy as np
        N = 10000
        E = 9375
        D = 256
        n = x.shape[0]
        loops = jnp.arange(n, dtype=edge_index.dtype)
        src = jnp.concatenate([edge_index[0], loops])
        dst = jnp.concatenate([edge_index[1], loops])
        deg = jax.ops.segment_sum(jnp.ones(src.shape[0], x.dtype), dst, num_segments=n)
        dinv = jnp.where(deg > 0, jax.lax.rsqrt(jnp.maximum(deg, 1e-12)), 0.0)
        norm = dinv[src] * dinv[dst]

        def gcn_conv(h, W, b):
            m = (h @ W)[src] * norm[:, None]
            return jax.ops.segment_sum(m, dst, num_segments=n) + b
        x1 = gcn_conv(x, W1, b1)
        x1 = x1 / jnp.maximum(jnp.linalg.norm(x1, axis=-1, keepdims=True), 1e-12)
        x2 = gcn_conv(x1, W2, b2)
        return x2 + x

    def _L2_gnn_ref(x, rbf, dists, edge_index, batch, W_node_to_message, W_radial_to_message, W_lin1, W_lin2, b_lin2, W_message_to_node):
        import jax, jax.numpy as jnp
        import numpy as np
        PI = float(np.pi)
        CUTOFF = 5.0
        N_NODES = 50000
        N_EDGES = 25000
        HIDDEN = 256
        FILT = 64
        RADIAL = 12
        h = x @ W_node_to_message.T
        edge_attr = rbf @ W_radial_to_message.T
        C = 0.5 * (jnp.cos(dists * (PI / CUTOFF)) + 1.0)
        W = edge_attr * C[:, None]
        h = h @ W_lin1.T
        src, dst = (edge_index[0], edge_index[1])
        m = h[src] * W
        agg = jax.ops.segment_sum(m, dst, num_segments=h.shape[0])
        h = agg @ W_lin2.T + b_lin2
        out = h @ W_message_to_node.T
        return out

    def _L3_gnn_ref(x, W, a_src, a_dst, edge_W, edge_b, bias, edge_attr, edge_index):
        import jax, jax.numpy as jnp
        import numpy as np
        N = 50000
        E = 12500
        IN = 256
        H = 8
        D = 32
        EF = 3
        n = x.shape[0]
        h = (x @ W.T).reshape(n, H, D)
        src, dst = (edge_index[0], edge_index[1])
        h_src = h[src]
        h_dst = h[dst]
        alpha = jnp.einsum('ehd,hd->eh', h_src, a_src) + jnp.einsum('ehd,hd->eh', h_dst, a_dst)
        enc = jax.nn.relu(edge_attr @ edge_W.T + edge_b).reshape(-1, H, D)
        alpha = alpha + jnp.sum(enc * h_dst, axis=-1)
        alpha = jnp.where(alpha >= 0, alpha, 0.2 * alpha)
        amax = jax.ops.segment_max(alpha, dst, num_segments=n)
        ex = jnp.exp(alpha - amax[dst])
        denom = jax.ops.segment_sum(ex, dst, num_segments=n)
        attn = ex / jnp.maximum(denom[dst], 1e-10)
        out = jax.ops.segment_sum(h_src * attn[..., None], dst, num_segments=n)
        return out.reshape(n, H * D) + bias
    edge_index = jnp.stack([src, dst])
    batch0 = jnp.zeros((50000,), jnp.int32)
    x = _layernorm(x + _L0_gnn_ref(x, edge_index, L0_gnn_W_l, L0_gnn_b_l, L0_gnn_W_r, L0_gnn_W_ln), axis=-1)
    x = _layernorm(x + _L1_gnn_ref(x, L1_gnn_W1, L1_gnn_b1, L1_gnn_W2, L1_gnn_b2, edge_index), axis=-1)
    x = _layernorm(x + _L2_gnn_ref(x, edge_attr_12, edge_weight, edge_index, batch0, L2_gnn_W_node_to_message, L2_gnn_W_radial_to_message, L2_gnn_W_lin1, L2_gnn_W_lin2, L2_gnn_b_lin2, L2_gnn_W_message_to_node), axis=-1)
    x = _layernorm(x + _L3_gnn_ref(x, L3_gnn_W, L3_gnn_a_src, L3_gnn_a_dst, L3_gnn_edge_W, L3_gnn_edge_b, L3_gnn_bias, edge_attr_3, edge_index), axis=-1)
    return x

_drawn_inputs = setup_inputs


def setup_inputs(seed=0):
    import zlib

    import numpy as np

    out = dict(_drawn_inputs(seed))
    spreads = {'L0_gnn_b_l': (0.0, 0.1),
     'L1_gnn_b1': (0.0, 2.0),
     'L1_gnn_b2': (0.0, 0.1),
     'L3_gnn_edge_b': (0.0, 0.277),
     'L3_gnn_bias': (0.0, 0.1)}
    factors = {'edge_attr_12': 6.659,
     'edge_weight': 8.0,
     'L1_gnn_W1': 2.891,
     'L1_gnn_W2': 2.95,
     'L2_gnn_W_node_to_message': 6.647,
     'L2_gnn_W_radial_to_message': 7.054,
     'L2_gnn_W_lin1': 6.599,
     'L2_gnn_W_lin2': 6.666,
     'L2_gnn_b_lin2': 3.904}
    for name, (base, spread) in spreads.items():
        noise = np.random.default_rng([zlib.crc32(name.encode()), seed]).standard_normal(out[name].shape)
        drawn = base * np.exp(spread * noise) if base else spread * noise
        out[name] = jnp.asarray(drawn.astype(out[name].dtype))
    for name, factor in factors.items():
        out[name] = (out[name] * factor).astype(out[name].dtype)
    return out
```

```python
from contextlib import ExitStack

import concourse.bass as bass
from concourse import mybir

F32 = mybir.dt.float32
I32 = mybir.dt.int32
BF16 = mybir.dt.bfloat16
ALU = mybir.AluOpType
ACT = mybir.ActivationFunctionType
AX_X = mybir.AxisListType.X

N = 50000
E = 50000
D = 256
P = 128
KC = D // P
TN = 96
UNROLL = 8
NT = -(-N // (TN * UNROLL)) * UNROLL
NP = NT * TN
W = 128
ET = -(-(E + W) // (W * UNROLL)) * UNROLL
EP = ET * W
EC = EP // P
PAD_DST = 60000
H, HD = 8, 32
FILT = 64
RAD = 12
HW = D + H
DW = D + 1
TG = 24
NG = NT // TG
NJ = -(-NT // P)
SEG = P // H
SQ = EP // SEG
BIG = 1e30
EPS = 1e-5

assert NG * TG == NT and NT * TN >= N and EC * P == EP and PAD_DST >= NP


class Tile:

    def __init__(self, round8, slot8):
        self.round8, self.slot8 = round8, slot8
        self.t = round8 * 8 + slot8
        self.peeled = isinstance(round8, int)

    def from_(self, n):
        return not self.peeled or self.t >= n

    def ring(self, n):
        return self.slot8 % n, self.round8 * (8 // n) + self.slot8 // n


def sweep(eng, count, stages):
    def step(round8, slot8, only=lambda t: True):
        for lag, stage in stages:
            tile = Tile(round8 + (slot8 - lag) // 8, (slot8 - lag) % 8)
            if not tile.peeled or only(tile.t):
                stage(tile)

    longest = max(lag for lag, _ in stages)
    first = 2 if longest else 1
    for r in range(first):
        for s in range(UNROLL):
            step(r, s, lambda t: t >= 0)
    with eng.Fori(first, count // UNROLL) as r:
        for s in range(UNROLL):
            step(r, s)
    for s in range(longest):
        step(count // UNROLL, s, lambda t: t < count)


class Memory:

    def __init__(self, nc, ctx, name):
        self.nc, self.ctx, self.name, self.semaphores = nc, ctx, name, []

    def sb(self, name, shape, dt=F32):
        return self.ctx.enter_context(self.nc.sbuf_tensor(f"{self.name}_{name}", shape, dt))

    def ps(self, name, shape):
        return self.ctx.enter_context(self.nc.psum_tensor(f"{self.name}_{name}", shape, F32))

    def sem(self, name):
        self.semaphores.append(self.nc.alloc_semaphore(f"{self.name}_{name}"))
        return self.semaphores[-1]

    def sems(self, name, n):
        return [self.sem(f"{name}{i}") for i in range(n)]

    def block(self):
        self.ctx.callback(self.free_semaphores)
        return self.ctx.enter_context(self.nc.Block())

    def free_semaphores(self):
        self.nc.clear_and_free_semaphores(self.semaphores)
        self.nc.all_engine_barrier()


def wait_apart(eng, sem, value, passed):
    eng.wait_ge(sem, value)
    eng.sem_inc(passed, 1)


class Chained:

    def __init__(self, eng, sem):
        self.eng, self.sem, self.n = eng, sem, 0

    def __call__(self, instruction, by=1):
        instruction.then_inc(self.sem, by)
        self.n += by
        self.eng.wait_ge(self.sem, self.n)


def build_setup(nc, keep, dram, ins):
    with ExitStack() as ctx:
        m = Memory(nc, ctx, "setup")
        wn = m.sb("wn", [FILT, D])
        lin1t = m.sb("lin1t", [FILT, FILT])
        lin2b = m.sb("lin2b", [FILT, FILT + 1])
        mnt = m.sb("mnt", [FILT, D])
        w3 = m.sb("w3", [P, KC, D])
        asrc = m.sb("asrc", [P, KC])
        hsel = m.sb("hsel", [P, KC, H])
        ahead = m.sb("ahead", [P, KC, H])
        dst_i = m.sb("dst_i", [P, EC], I32)
        src_i = m.sb("src_i", [P, EC], I32)
        dist = m.sb("dist", [P, EC])
        dstf = m.sb("dstf", [P, EC])
        srcf = m.sb("srcf", [P, EC])
        wraps = m.sb("wraps", [P, EC])
        half_pi = m.sb("half_pi", [P, 1])
        edge_pads = m.sb("edge_pads", [1, 2])
        dst_e = m.sb("dst_e", [P, ET], I32)
        group_start = m.sb("group_start", [P, NG + 1])
        tile_start = m.sb("tile_start", [P, TG + 1])
        past_group = m.sb("past_group", [P, EC, NG + 1], BF16)
        in_group = m.sb("in_group", [P, EC, NG], BF16)
        group_no = m.sb("group_no", [P, EC])
        rest = m.sb("rest", [P, EC])
        before_tile = m.sb("before_tile", [P, EC, TG + 1], BF16)
        radial_rows = m.sb("radial_rows", [P, NJ, RAD, W])
        iota_g = m.sb("iota_g", [NG, NG])
        part_g = m.sb("part_g", [NG, 1])
        earlier = m.sb("earlier", [NG, NG])
        within = m.sb("within", [NG, TG + 1])
        starts = m.sb("starts", [NG, TG])
        starts_i = m.sb("starts_i", [NG, TG], I32)
        zero_i = m.sb("zero_i", [1, NJ * P], I32)
        row = m.sb("row", [1, NT], I32)
        rowf = m.sb("rowf", [1, NT])
        cnt = m.sb("cnt", [1, NT])
        cnt_i = m.sb("cnt_i", [1, NT], I32)
        over_i = m.sb("over_i", [1, NT], I32)
        start_cols = m.sb("start_cols", [P, NJ], I32)
        window_rows = m.sb("window_rows", [P, 3, NJ, W])
        ident = keep["ident"]
        ps_fold = m.ps("ps_fold", [P, 512])
        ps_fold2 = m.ps("ps_fold2", [P, 512])
        ps_cnt = m.ps("ps_cnt", [P, 512])
        ps_base = m.ps("ps_base", [P, 512])
        ps_win = [m.ps(f"ps_win{i}", [P, W]) for i in range(2)]

        weights_in, edges_in, pads_out = m.sem("weights_in"), m.sem("edges_in"), m.sem("pads_out")
        kept_in = m.sem("kept_in")
        iotas_done, consts_done = m.sem("iotas_done"), m.sem("consts_done")
        dve_chain, act_chain = m.sem("dve_chain"), m.sem("act_chain")
        heads_ready, fold1, fold2, folds_copied = (m.sem(x) for x in ("heads_ready", "fold1", "fold2", "folds_copied"))
        wraps_ready, cutoff_ready = m.sem("wraps_ready"), m.sem("cutoff_ready")
        flat_ready, flat_out = m.sem("flat_ready"), m.sem("flat_out")
        onehots_ready, counted, within_ready, based = (m.sem(x) for x in ("onehots_ready", "counted", "within_ready", "based"))
        starts_ready, starts_out, starts_back = m.sem("starts_ready"), m.sem("starts_out"), m.sem("starts_back")
        index_ready, windows_in = m.sem("index_ready"), m.sem("windows_in")
        radial_in, radial_out = m.sems("radial_in", NJ), m.sem("radial_out")
        ident_zeroed, ident_ready = m.sem("ident_zeroed"), m.sem("ident_ready")
        turned, turned_used = m.sem("turned"), m.sem("turned_used")

        block = m.block()

        @block.sync
        def _(sp):
            n = 0
            for name, src in (("wl", "L0_wlt"), ("wr", "L0_wrt"), ("wln", "L0_wlnt"), ("w1", "L1_w1"), ("w2", "L1_w2")):
                sp.dma_start(keep[name][:], ins[src].rearrange("(c p) o -> p c o", p=P)).then_inc(kept_in, 16)
                n += 1
            sp.dma_start(keep["w3"][:, :, 0:D], ins["L3_wt"].rearrange("(c p) o -> p c o", p=P)).then_inc(kept_in, 16)
            sp.dma_start(keep["bl"][:], ins["L0_bl"]).then_inc(kept_in, 16)
            sp.dma_start(keep["wrad"][:], ins["L2_wradt"]).then_inc(kept_in, 16)
            sp.dma_start(keep["wedge"][:], ins["L3_wedge"]).then_inc(kept_in, 16)
            for name, src in (("b1", "L1_b1"), ("b2", "L1_b2"), ("bias3", "L3_bias"), ("adst", "L3_adst")):
                sp.dma_start(keep[name][:], ins[src].partition_broadcast(P)).then_inc(kept_in, 16)
            sp.dma_start(keep["src_e"][:], ins["src_by_tile"]).then_inc(kept_in, 16)
            for dst_, src in ((wn, "L2_wn"), (lin1t, "L2_lin1t"), (lin2b, "L2_lin2b"), (mnt, "L2_mnt")):
                sp.dma_start(dst_[:], ins[src]).then_inc(weights_in, 16)
            sp.dma_start(w3[:], ins["L3_w"].rearrange("(c p) k -> p c k", p=P)).then_inc(weights_in, 16)
            sp.dma_start(asrc[:], ins["L3_asrc"]).then_inc(weights_in, 16)
            sp.wait_ge(flat_ready, 3)
            sp.wait_ge(cutoff_ready, 1)
            sp.dma_start(dram["dst_f"].rearrange("(p c) -> p c", p=P), dstf[:]).then_inc(flat_out, 16)
            sp.dma_start(dram["src_f"].rearrange("(p c) -> p c", p=P), srcf[:]).then_inc(flat_out, 16)
            sp.dma_start(dram["cut_f"].rearrange("(p c) -> p c", p=P), dist[:]).then_inc(flat_out, 16)
            sp.dma_start(dram["dst_ext"][1:EP + 1].rearrange("(p c) -> p c", p=P), dstf[:]).then_inc(flat_out, 16)
            sp.dma_start(dram["dst_ext"][0:1].unsqueeze(0), edge_pads[:, 0:1]).then_inc(flat_out, 16)
            sp.dma_start(dram["dst_ext"][EP + 1:EP + 2].unsqueeze(0), edge_pads[:, 1:2]).then_inc(flat_out, 16)
            sp.wait_ge(starts_ready, 1)
            sp.dma_start(dram["starts"][0:NT].rearrange("(g t) -> g t", t=TG), starts_i[:]).then_inc(starts_out, 16)
            sp.dma_start(dram["starts"][NT:NJ * P].unsqueeze(0), zero_i[:, NT:NJ * P]).then_inc(starts_out, 16)
            sp.wait_ge(starts_out, 32)
            sp.dma_start(keep["starts"][:], dram["starts"][0:NT].unsqueeze(0)).then_inc(starts_back, 16)
            sp.dma_start(row[:], dram["starts"][0:NT].unsqueeze(0)).then_inc(starts_back, 16)
            sp.dma_start(start_cols[:], dram["starts"].rearrange("(j p) -> p j", p=P),
                         allow_slow_non_contiguous=True).then_inc(starts_back, 16)
            for j in range(NJ):
                sp.wait_ge(radial_in[j], 16 * RAD)
                sp.dma_start(dram["radial"][j * P:(j + 1) * P, :, :], radial_rows[:, j, :, :]).then_inc(radial_out, 16)
            sp.wait_ge(radial_out, NJ * 16)
            sp.wait_ge(flat_out, 6 * 16)
            sp.wait_ge(kept_in, 14 * 16)

        @block.scalar
        def _(act):
            act.dma_start(dst_i[:], ins["dst_flat"].rearrange("(p c) -> p c", p=P)).then_inc(edges_in, 16)
            act.dma_start(src_i[:], ins["src_flat"].rearrange("(p c) -> p c", p=P)).then_inc(edges_in, 16)
            act.dma_start(dist[:], ins["dist_flat"].rearrange("(p c) -> p c", p=P)).then_inc(edges_in, 16)
            act.dma_start(dst_e[:], ins["dst_by_tile"]).then_inc(edges_in, 16)
            chain = Chained(act, act_chain)
            act.wait_ge(wraps_ready, 1)
            act.wait_ge(consts_done, 1)
            chain(nc.scalar.activation(wraps[:], wraps[:], ACT.Sin, bias=half_pi[:], scale=-3.14159265358979))
            nc.scalar.activation(dist[:], wraps[:], ACT.Square).then_inc(cutoff_ready, 1)

        @block.gpsimd
        def _(pool):
            nc.gpsimd.iota(keep["iota"][:], pattern=[[1, TN]], base=0, channel_multiplier=0,
                           allow_small_or_imprecise_dtypes=True).then_inc(iotas_done, 1)
            nc.gpsimd.iota(keep["base"][:], pattern=[[TN, NT]], base=0, channel_multiplier=0,
                           allow_small_or_imprecise_dtypes=True).then_inc(iotas_done, 1)
            nc.gpsimd.iota(group_start[:], pattern=[[TN * TG, NG + 1]], base=0, channel_multiplier=0,
                           allow_small_or_imprecise_dtypes=True).then_inc(iotas_done, 1)
            nc.gpsimd.iota(tile_start[:], pattern=[[TN, TG + 1]], base=0, channel_multiplier=0,
                           allow_small_or_imprecise_dtypes=True).then_inc(iotas_done, 1)
            nc.gpsimd.iota(iota_g[:], pattern=[[1, NG]], base=0, channel_multiplier=0,
                           allow_small_or_imprecise_dtypes=True).then_inc(iotas_done, 1)
            nc.gpsimd.iota(part_g[:], pattern=[[0, 1]], base=0, channel_multiplier=1,
                           allow_small_or_imprecise_dtypes=True).then_inc(iotas_done, 1)
            nc.gpsimd.memset(ident[:], 0.0).then_inc(ident_zeroed, 1)
            pool.wait_ge(ident_zeroed, 1)
            nc.gpsimd.affine_select(out=ident[:], in_=ident[:], compare_op=ALU.not_equal, fill=1.0, base=0,
                                    pattern=[[-1, P]], channel_multiplier=1).then_inc(ident_ready, 1)
            pool.wait_ge(index_ready, 1)
            pool.wait_ge(flat_out, 6 * 16)
            for j in range(NJ):
                for k, name in enumerate(("dst_f", "src_f", "cut_f")):
                    pool.indirect_dma_start(
                        out=window_rows[:, k, j, :], out_offset=None, in_=dram[name].unsqueeze(1),
                        in_offset=bass.IndirectOffsetOnAxis(ap=start_cols[:, j:j + 1], axis=0)).then_inc(windows_in, 16)
            for j in range(NJ):
                for k in range(RAD):
                    pool.indirect_dma_start(
                        out=radial_rows[:, j, k, :], out_offset=None, in_=ins["radial_flat"].unsqueeze(1),
                        in_offset=bass.IndirectOffsetOnAxis(ap=keep["start_cols"][:, k, j:j + 1], axis=0),
                    ).then_inc(radial_in[j], 16)

        @block.vector
        def _(dve):
            chain = Chained(dve, dve_chain)
            nc.vector.memset(half_pi[:], 1.5707963267949).then_inc(consts_done, 1)
            chain(nc.vector.memset(keep["eps"][:], EPS))
            chain(nc.vector.memset(keep["ones"][:], 1.0))
            chain(nc.vector.memset(zero_i[:], 0))
            chain(nc.vector.memset(edge_pads[:, 0:1], -1.0))
            chain(nc.vector.memset(edge_pads[:, 1:2], -1.0))
            dve.wait_ge(edges_in, 4 * 16)
            nc.vector.tensor_copy(srcf[:], src_i[:]).then_inc(flat_ready, 1)
            nc.vector.tensor_scalar(keep["dst_e"][:], dst_e[:], float(N - 1), None, ALU.min).then_inc(flat_ready, 1)
            chain(nc.vector.tensor_scalar(rest[:], dist[:], 0.1, None, ALU.mult))
            chain(nc.vector.tensor_scalar(wraps[:], rest[:], 12582912.0, None, ALU.add))
            chain(nc.vector.tensor_scalar(wraps[:], wraps[:], 12582912.0, None, ALU.subtract))
            chain(nc.vector.tensor_tensor(wraps[:], rest[:], wraps[:], ALU.subtract))
            nc.vector.scalar_tensor_tensor(out=wraps[:], in0=wraps[:], scalar=-1.0, in1=wraps[:],
                                           op0=ALU.mult, op1=ALU.max).then_inc(wraps_ready, 1)
            dve.wait_ge(wraps_ready, 1)
            chain(nc.vector.tensor_copy(dstf[:], dst_i[:]))
            dve.sem_inc(flat_ready, 1)
            dve.wait_ge(iotas_done, 6)
            chain(nc.vector.tensor_tensor(
                past_group[:], dstf[:].unsqueeze(2).broadcast_to([P, EC, NG + 1]),
                group_start[:].unsqueeze(1).broadcast_to([P, EC, NG + 1]), ALU.is_ge))
            chain(nc.vector.tensor_tensor(in_group[:], past_group[:, :, 0:NG], past_group[:, :, 1:NG + 1], ALU.subtract))
            chain(nc.vector.tensor_reduce(group_no[:], past_group[:, :, 1:NG + 1], AX_X, ALU.add))
            chain(nc.vector.scalar_tensor_tensor(rest[:], group_no[:], -float(TN * TG), dstf[:], ALU.mult, ALU.add))
            nc.vector.tensor_tensor(
                before_tile[:], rest[:].unsqueeze(2).broadcast_to([P, EC, TG + 1]),
                tile_start[:].unsqueeze(1).broadcast_to([P, EC, TG + 1]), ALU.is_lt).then_inc(onehots_ready, 1)
            chain(nc.vector.tensor_scalar(earlier[:], iota_g[:], part_g[:], None, ALU.is_gt))
            dve.wait_ge(weights_in, 6 * 16)
            chain(nc.vector.memset(hsel[:], 0.0))
            for c in range(KC):
                for g in range(P // HD):
                    h = c * (P // HD) + g
                    chain(nc.vector.memset(hsel[g * HD:(g + 1) * HD, c, h:h + 1], 1.0))
            for c in range(KC):
                nc.vector.tensor_scalar(ahead[:, c, :], hsel[:, c, :], asrc[:, c:c + 1], None, ALU.mult).then_inc(heads_ready, 1)
            dve.wait_ge(fold1, 1)
            chain(nc.vector.tensor_copy(keep["wc"][:], ps_fold[:, 0:KC * FILT].rearrange("p (c o) -> p c o", c=KC)))
            chain(nc.vector.tensor_copy(keep["w3"][:, :, D:HW], ps_fold[:, 128:128 + KC * H].rearrange("p (c o) -> p c o", c=KC)))
            chain(nc.vector.tensor_copy(keep["m2"][:], ps_fold2[0:FILT + 1, 0:D]))
            dve.wait_ge(counted, 1)
            nc.vector.tensor_copy(within[:], ps_cnt[0:NG, 0:TG + 1]).then_inc(within_ready, 1)
            dve.wait_ge(based, 1)
            dve.wait_ge(within_ready, 1)
            chain(nc.vector.tensor_scalar(starts[:], within[:, 0:TG], ps_base[0:NG, 0:1], None, ALU.add))
            nc.vector.tensor_copy(starts_i[:], starts[:]).then_inc(starts_ready, 1)
            dve.wait_ge(starts_back, 48)
            chain(nc.vector.tensor_copy(rowf[:], row[:]))
            chain(nc.vector.memset(cnt[:], 0.0))
            chain(nc.vector.tensor_tensor(cnt[:, 0:NT - 1], rowf[:, 1:NT], rowf[:, 0:NT - 1], ALU.subtract))
            chain(nc.vector.tensor_scalar(cnt_i[:], cnt[:], -1.0, 0.0, ALU.add, ALU.max))
            chain(nc.vector.tensor_scalar(over_i[:], cnt_i[:], 7, None, ALU.arith_shift_right))
            chain(nc.vector.tensor_copy(keep["over"][:, 0:NT], over_i[:]))
            chain(nc.vector.tensor_reduce(cnt[:, 0:1], over_i[:], AX_X, ALU.max))
            chain(nc.vector.tensor_copy(keep["over"][:, NT:NT + 1], cnt[:, 0:1]))
            for k in range(RAD):
                chain(nc.vector.tensor_scalar(keep["start_cols"][:, k, :], start_cols[:], float(k * EP), None, ALU.add))
            dve.sem_inc(index_ready, 1)
            n = 0
            for j in range(NJ):
                w = min(P, NT - j * P)
                for k in range(3):
                    dve.wait_ge(turned, n + 1)
                    at = slice(j * P, j * P + w)
                    if k == 0:
                        op = nc.vector.tensor_tensor(keep["drel"][:, at], ps_win[n % 2][:, 0:w], keep["base"][:, at], ALU.subtract)
                    elif k == 1:
                        op = nc.vector.tensor_copy(keep["src"][:, at], ps_win[n % 2][:, 0:w])
                    else:
                        op = nc.vector.tensor_copy(keep["cut"][:, at], ps_win[n % 2][:, 0:w])
                    op.then_inc(turned_used, 1)
                    n += 1
            dve.wait_ge(turned_used, n)

        @block.tensor
        def _(pe):
            pe.wait_ge(weights_in, 6 * 16)
            for c in range(KC):
                nc.tensor.matmul(ps_fold[:, c * FILT:(c + 1) * FILT], wn[:, c * P:(c + 1) * P], lin1t[:], start=True, stop=True)
            pe.wait_ge(heads_ready, KC)
            for c in range(KC):
                for o in range(KC):
                    nc.tensor.matmul(ps_fold[:, 128 + c * H:128 + (c + 1) * H], w3[:, o, c * P:(c + 1) * P], ahead[:, o, :],
                                     start=(o == 0), stop=(o == KC - 1))
            nc.tensor.matmul(ps_fold2[0:FILT + 1, 0:D], lin2b[:], mnt[:], start=True, stop=True).then_inc(fold1, 1)
            pe.wait_ge(onehots_ready, 1)
            for c in range(EC):
                last = nc.tensor.matmul(ps_cnt[0:NG, 0:TG + 1], in_group[:, c, :], before_tile[:, c, :],
                                        start=(c == 0), stop=(c == EC - 1))
            last.then_inc(counted, 1)
            pe.wait_ge(within_ready, 1)
            nc.tensor.matmul(ps_base[0:NG, 0:1], earlier[:], within[:, TG:TG + 1], start=True, stop=True).then_inc(based, 1)
            n = 0
            pe.wait_ge(ident_ready, 1)
            for j in range(NJ):
                pe.wait_ge(windows_in, 16 * 3 * NJ)
                for k in range(3):
                    if n >= 2:
                        pe.wait_ge(turned_used, n - 1)
                    nc.tensor.transpose(ps_win[n % 2][:, 0:W], window_rows[:, k, j, :], ident[:]).then_inc(turned, 1)
                    n += 1


class Further:

    def __init__(self, eng, keep, name):
        self.eng, self.keep = eng, keep
        self.any_over = eng.value_load(keep["over"][0:1, NT:NT + 1], min_val=0, max_val=ET)
        self.done = eng.alloc_register(f"{name}_chunks_done")
        eng.reg_mov(self.done, 0)

    def chunks(self, tile, body):
        eng = self.eng
        with eng.If(self.any_over > 0):
            count = eng.value_load(self.keep["over"][0:1, bass.ds(tile.t, 1)], min_val=0, max_val=ET)
            with eng.If(count > 0):
                with eng.Fori(0, count) as k:
                    eng.reg_add(self.done, self.done, 1)
                    body(k, eng.snap(self.done, min_val=1, max_val=60000))


class WindowSweep:

    def __init__(self, nc, ctx, keep, dram, ins, name, table, width, columns=()):
        self.nc, self.keep, self.dram, self.ins = nc, keep, dram, ins
        self.table, self.width, self.columns = table, width, columns
        m = self.m = Memory(nc, ctx, name)
        self.index = m.sb("index", [P, 8], I32)
        self.rows = m.sb("rows", [P, 8, width])
        self.sel = m.sb("sel", [P, 8, TN])
        self.index_ready = m.sem("index_ready")
        self.gathered = m.sems("gathered", 8)
        self.sel_ready = m.sem("sel_ready")
        self.summed = m.sem("summed")
        self.x_src = m.sb("x_src", [P, 1], I32)
        self.x_dst = m.sb("x_dst", [P, 1])
        self.x_cut = m.sb("x_cut", [P, 1])
        self.x_rel = m.sb("x_rel", [P, 1])
        self.x_rows = m.sb("x_rows", [P, width])
        self.x_sel = m.sb("x_sel", [P, TN])
        self.x_cols = m.sb("x_cols", [16, W])
        self.x_loaded = m.sem("x_loaded")
        self.x_gathered = m.sem("x_gathered")
        self.x_rel_ready = m.sem("x_rel_ready")
        self.x_sel_ready = m.sem("x_sel_ready")
        self.x_summed = m.sem("x_summed")
        self.passed = m.sems("passed", 4)
        self.x_loads = 3 + len(columns)
        self.w = m.sb("w", [TN, 4, D])
        self.stats = m.sb("stats", [TN, 4, 6])
        self.mv = m.sb("mv", [TN, 4, 2])
        self.sd = m.sb("sd", [TN, 4, 1])
        self.rstd = m.sb("rstd", [TN, 4, 1])
        self.shift = m.sb("shift", [TN, 4, 1])
        self.w_ready, self.stats_ready, self.mv_ready, self.sd_ready, self.rstd_ready, self.shift_ready = (
            m.sem(x) for x in ("w_ready", "stats_ready", "mv_ready", "sd_ready", "rstd_ready", "shift_ready"))

    def gather(self, pool, rows_free=None):
        further = Further(pool, self.keep, self.m.name)
        rows_free = rows_free or self.summed

        def stage(tile):
            slot, round_ = tile.ring(8)
            if slot % 4 == 0:
                if tile.from_(8):
                    pool.wait_ge(rows_free, tile.t - 4)
                self.nc.gpsimd.tensor_copy(self.index[:, slot:slot + 4], self.keep["src"][:, bass.ds(tile.t, 4)]).then_inc(
                    self.index_ready, 1)
                wait_apart(pool, self.index_ready, round_ * 2 + slot // 4 + 1, self.passed[1])
            pool.indirect_dma_start(
                out=self.rows[:, slot, :], out_offset=None, in_=self.table,
                in_offset=bass.IndirectOffsetOnAxis(ap=self.index[:, slot:slot + 1], axis=0)).then_inc(self.gathered[slot], 16)

            def chunk(k, n):
                wait_apart(pool, self.x_loaded, n * (16 * self.x_loads), self.passed[1])
                pool.indirect_dma_start(
                    out=self.x_rows[:], out_offset=None, in_=self.table,
                    in_offset=bass.IndirectOffsetOnAxis(ap=self.x_src[:, 0:1], axis=0)).then_inc(self.x_gathered, 16)

            further.chunks(tile, chunk)

        sweep(pool, NT, [(0, stage)])

    def load_chunks(self, sp, further, tile):
        def chunk(k, n):
            start = sp.value_load(self.keep["starts"][0:1, bass.ds(tile.t, 1)], min_val=0, max_val=N)
            at = self.nc.s_assert_within(start + k * W + W, 0, N)
            sp.dma_start(self.x_src[:], self.ins["src_flat"][bass.ds(at, W)].unsqueeze(1)).then_inc(self.x_loaded, 16)
            sp.dma_start(self.x_dst[:], self.dram["dst_f"][bass.ds(at, W)].unsqueeze(1)).then_inc(self.x_loaded, 16)
            sp.dma_start(self.x_cut[:], self.dram["cut_f"][bass.ds(at, W)].unsqueeze(1)).then_inc(self.x_loaded, 16)
            for source, n_rows in self.columns:
                sp.dma_start(self.x_cols[0:n_rows, :], source[:, bass.ds(at, W)]).then_inc(self.x_loaded, 16)
            wait_apart(sp, self.x_summed, n, self.passed[2])

        further.chunks(tile, chunk)

    def select(self, dve, tile, scale=None):
        slot, _ = tile.ring(8)
        if tile.from_(8):
            dve.wait_ge(self.summed, tile.t - 7)
        s2, op1 = (scale(slot, tile), ALU.mult) if scale else (None, ALU.bypass)
        self.nc.vector.tensor_scalar(self.sel[:, slot, :], self.keep["iota"][:], self.keep["drel"][:, bass.ds(tile.t, 1)],
                                     s2, ALU.is_equal, op1).then_inc(self.sel_ready, 1)

    def select_chunk(self, dve, tile, n, scale=None):
        dve.wait_ge(self.x_gathered, n * 16)
        self.nc.vector.tensor_tensor(self.x_rel[:], self.x_dst[:], self.keep["base"][:, bass.ds(tile.t, 1)],
                                     ALU.subtract).then_inc(self.x_rel_ready, 1)
        dve.wait_ge(self.x_rel_ready, n)
        s2, op1 = (scale, ALU.mult) if scale is not None else (None, ALU.bypass)
        self.nc.vector.tensor_scalar(self.x_sel[:], self.keep["iota"][:], self.x_rel[:, 0:1], s2,
                                     ALU.is_equal, op1).then_inc(self.x_sel_ready, 1)

    def moments(self, dve, tile):
        slot, _ = tile.ring(4)
        dve.wait_ge(self.w_ready, tile.t + 1)
        self.nc.vector.bn_stats(self.stats[:, slot, :], self.w[:, slot, :]).then_inc(self.stats_ready, 1)
        wait_apart(dve, self.stats_ready, tile.t + 1, self.passed[0])
        self.nc.vector.bn_aggr(self.mv[:, slot, :], self.stats[:, slot, :]).then_inc(self.mv_ready, 1)

    def deviation(self, act, tile):
        slot, _ = tile.ring(4)
        act.wait_ge(self.mv_ready, tile.t + 1)
        self.nc.scalar.activation(self.sd[:, slot, :], self.mv[:, slot, 1:2], ACT.Sqrt,
                                  bias=self.keep["eps"][0:TN, :]).then_inc(self.sd_ready, 1)

    def factor(self, dve, tile):
        slot, _ = tile.ring(4)
        dve.wait_ge(self.sd_ready, tile.t + 1)
        self.nc.vector.reciprocal(self.rstd[:, slot, :], self.sd[:, slot, :]).then_inc(self.rstd_ready, 1)
        dve.wait_ge(self.rstd_ready, tile.t + 1)
        self.nc.vector.scalar_tensor_tensor(out=self.shift[:, slot, :], in0=self.mv[:, slot, 0:1], scalar=-1.0,
                                            in1=self.rstd[:, slot, :], op0=ALU.mult, op1=ALU.mult).then_inc(self.shift_ready, 1)


def node_rows(table, tile, width=D, count=2):
    return table[bass.ds(tile.t * TN, count * TN), 0:width].rearrange("(k p) f -> p k f", p=TN)


def build_sage(nc, keep, dram, ins):
    with ExitStack() as ctx:
        s = WindowSweep(nc, ctx, keep, dram, ins, "sage", ins["x"], D)
        m = s.m
        x = m.sb("x", [TN, 8, D])
        xt = m.sb("xt", [P, 4, KC, 2 * TN])
        count_inv = m.sb("count_inv", [P, 4, TN])
        mean_t = m.sb("mean_t", [P, 4, KC, TN])
        hid_t = m.sb("hid_t", [P, 4, KC, TN])
        deg = m.sb("deg", [TN, 4, 1])
        deg_root = m.sb("deg_root", [TN, 4, 1])
        y = m.sb("y", [TN, 4, D])
        out = m.sb("out", [TN, 8, DW])
        sum_ps = [m.ps(f"sum_ps{i}", [P, 512]) for i in range(2)]
        hid_ps = [m.ps(f"hid_ps{i}", [P, 512]) for i in range(2)]
        out_ps = [m.ps(f"out_ps{i}", [P, 512]) for i in range(2)]
        loaded, stored = m.sems("loaded", 4), m.sems("stored", 4)
        (clamped, inverted, mean_ready, deg_ready, root_ready, dinv_ready, hid_summed, hid_ready, out_summed, y_ready,
         out_ready) = (m.sem(n) for n in ("clamped", "inverted", "mean_ready", "deg_ready", "root_ready", "dinv_ready",
                                          "hid_summed", "hid_ready", "out_summed", "y_ready", "out_ready"))
        CNT = KC * TN
        block = m.block()

        @block.gpsimd
        def _(pool):
            s.gather(pool)

        @block.sync
        def _(sp):
            further = Further(sp, keep, s.m.name)

            def load(tile):
                if tile.slot8 % 2:
                    return
                pair, _ = tile.ring(8)
                pair //= 2
                if tile.from_(8):
                    sp.wait_ge(s.w_ready, tile.t - 6)
                    sp.wait_ge(hid_summed, tile.t - 6)
                sp.dma_start(x[:, 2 * pair:2 * pair + 2, :], node_rows(ins["x"], tile)).then_inc(loaded[pair], 16)
                sp.dma_start(xt[:, pair, :, :], ins["xt"][:, bass.ds(tile.t * TN, 2 * TN)].rearrange(
                    "(c p) n -> p c n", p=P)).then_inc(loaded[pair], 16)

            def store(tile):
                if tile.slot8 % 2:
                    return
                slot, _ = tile.ring(8)
                sp.wait_ge(out_ready, tile.t + 2)
                sp.wait_ge(dinv_ready, tile.t + 2)
                sp.dma_start(node_rows(dram["x1"], tile, DW), out[:, slot:slot + 2, :]).then_inc(stored[slot // 2], 16)

            sweep(sp, NT, [(0, load), (6, store), (0, lambda tile: s.load_chunks(sp, further, tile))])
            for q in stored:
                sp.wait_ge(q, 16 * (NT // 8))

        @block.vector
        def _(dve):
            further = Further(dve, keep, s.m.name)

            def select(tile):
                s.select(dve, tile)
                further.chunks(tile, lambda k, n: s.select_chunk(dve, tile, n))

            def mean(tile):
                slot, _ = tile.ring(4)
                ps = sum_ps[slot % 2]
                dve.wait_ge(s.summed, tile.t + 1)
                if tile.from_(4):
                    dve.wait_ge(root_ready, tile.t - 3)
                nc.vector.tensor_copy(deg[:, slot, :], ps[0:TN, CNT + TN:CNT + TN + 1]).then_inc(deg_ready, 1)
                nc.vector.tensor_scalar(count_inv[:, slot, :], ps[:, CNT:CNT + TN], 1.0, None, ALU.max).then_inc(clamped, 1)
                dve.wait_ge(clamped, tile.t + 1)
                nc.vector.reciprocal(count_inv[:, slot, :], count_inv[:, slot, :]).then_inc(inverted, 1)
                dve.wait_ge(inverted, tile.t + 1)
                if tile.from_(4):
                    dve.wait_ge(hid_summed, tile.t - 3)
                nc.vector.tensor_tensor(
                    mean_t[:, slot, :, :], ps[:, 0:CNT].rearrange("p (c n) -> p c n", c=KC),
                    count_inv[:, slot:slot + 1, :].broadcast_to([P, KC, TN]), ALU.mult).then_inc(mean_ready, 1)

            def residual(tile):
                slot, _ = tile.ring(4)
                slot8, round8 = tile.ring(8)
                dve.wait_ge(out_summed, tile.t + 1)
                if slot8 % 2 == 0:
                    dve.wait_ge(loaded[slot8 // 2], (round8 + 1) * 32)
                nc.vector.tensor_tensor(y[:, slot, :], out_ps[slot % 2][0:TN, 0:D], x[:, slot8, :], ALU.add).then_inc(y_ready, 1)
                dve.wait_ge(y_ready, tile.t + 1)
                if tile.from_(4):
                    dve.wait_ge(out_ready, tile.t - 3)
                nc.vector.scalar_tensor_tensor(out=s.w[:, slot, :], in0=y[:, slot, :], scalar=0.0, in1=x[:, slot8, :],
                                               op0=ALU.max, op1=ALU.add).then_inc(s.w_ready, 1)
                s.moments(dve, tile)

            def factor(tile):
                slot, _ = tile.ring(4)
                slot8, round8 = tile.ring(8)
                s.factor(dve, tile)
                dve.wait_ge(root_ready, tile.t + 1)
                if tile.from_(8):
                    dve.wait_ge(stored[slot8 // 2], round8 * 16)
                nc.vector.reciprocal(out[:, slot8, D:DW], deg_root[:, slot, :]).then_inc(dinv_ready, 1)

            sweep(dve, NT, [(0, select), (1, mean), (3, residual), (4, factor)])

        @block.scalar
        def _(act):
            def hidden(tile):
                slot, _ = tile.ring(4)
                act.wait_ge(hid_summed, tile.t + 1)
                if tile.from_(4):
                    act.wait_ge(out_summed, tile.t - 3)
                for o in range(KC):
                    last = nc.scalar.activation(hid_t[:, slot, o, :], hid_ps[slot % 2][:, o * TN:(o + 1) * TN], ACT.Relu,
                                                bias=keep["bl"][:, o:o + 1])
                last.then_inc(hid_ready, 1)

            def roots(tile):
                slot, _ = tile.ring(4)
                act.wait_ge(deg_ready, tile.t + 1)
                if tile.from_(4):
                    act.wait_ge(dinv_ready, tile.t - 3)
                nc.scalar.activation(deg_root[:, slot, :], deg[:, slot, :], ACT.Sqrt, bias=keep["ones"][0:TN, 0:1]).then_inc(root_ready, 1)
                s.deviation(act, tile)

            def normal(tile):
                slot, _ = tile.ring(4)
                slot8, round8 = tile.ring(8)
                act.wait_ge(s.shift_ready, tile.t + 1)
                if tile.from_(8):
                    act.wait_ge(stored[slot8 // 2], round8 * 16)
                nc.scalar.activation(out[:, slot8, 0:D], s.w[:, slot, :], ACT.Identity, bias=s.shift[:, slot, :],
                                     scale=s.rstd[:, slot, :]).then_inc(out_ready, 1)

            sweep(act, NT, [(1, hidden), (3, roots), (4, normal)])

        @block.tensor
        def _(pe):
            further = Further(pe, keep, s.m.name)

            def sums(tile):
                slot, round8 = tile.ring(8)
                ps = sum_ps[slot % 2]
                pe.wait_ge(s.sel_ready, tile.t + 1)
                pe.wait_ge(s.gathered[slot], (round8 + 1) * 16)
                if tile.from_(2):
                    pe.wait_ge(mean_ready, tile.t - 1)

                def add(rows, sel, part, start=False):
                    if part < KC:
                        return nc.tensor.matmul(ps[:, part * TN:(part + 1) * TN], rows[:, part * P:(part + 1) * P], sel,
                                                start=start, stop=True, skip_group_check=True)
                    if part == KC:
                        return nc.tensor.matmul(ps[:, CNT:CNT + TN], keep["ones"][:], sel, start=False, stop=True,
                                                skip_group_check=True)
                    return nc.tensor.matmul(ps[0:TN, CNT + TN:CNT + TN + 1], sel, keep["ones"][:, 0:1], start=False, stop=True,
                                            skip_group_check=True)

                add(s.rows[:, slot, :], s.sel[:, slot, :], 0, start=True)

                def chunk(k, n):
                    pe.wait_ge(s.x_sel_ready, n)
                    for part in range(KC + 2):
                        last = add(s.x_rows[:], s.x_sel[:], part)
                    last.then_inc(s.x_summed, 1)

                further.chunks(tile, chunk)
                for part in range(1, KC + 2):
                    last = add(s.rows[:, slot, :], s.sel[:, slot, :], part)
                last.then_inc(s.summed, 1)

            def hidden(tile):
                slot, _ = tile.ring(4)
                slot8, round8 = tile.ring(8)
                pair, half = slot8 // 2, slot8 % 2
                ps = hid_ps[slot % 2]
                if half == 0:
                    pe.wait_ge(loaded[pair], (round8 + 1) * 32)
                if tile.from_(2):
                    pe.wait_ge(hid_ready, tile.t - 1)
                for o in range(KC):
                    at = slice(o * TN, (o + 1) * TN)
                    for c in range(KC):
                        nc.tensor.matmul(ps[:, at], keep["wr"][:, c, o * P:(o + 1) * P], xt[:, pair, c, half * TN:(half + 1) * TN],
                                         start=(o == 0 and c == 0), stop=True, skip_group_check=True)
                pe.wait_ge(mean_ready, tile.t + 1)
                for o in range(KC):
                    at = slice(o * TN, (o + 1) * TN)
                    for c in range(KC):
                        last = nc.tensor.matmul(ps[:, at], keep["wl"][:, c, o * P:(o + 1) * P], mean_t[:, slot, c, :],
                                                start=False, stop=True, skip_group_check=True)
                last.then_inc(hid_summed, 1)

            def output(tile):
                slot, _ = tile.ring(4)
                pe.wait_ge(hid_ready, tile.t + 1)
                if tile.from_(2):
                    pe.wait_ge(y_ready, tile.t - 1)
                for c in range(KC):
                    last = nc.tensor.matmul(out_ps[slot % 2][0:TN, 0:D], hid_t[:, slot, c, :], keep["wln"][:, c, :],
                                            start=(c == 0), stop=(c == KC - 1))
                last.then_inc(out_summed, 1)

            sweep(pe, NT, [(0, sums), (1, hidden), (2, output)])


class Projection:

    def __init__(self, s, name, matrix, width, n_turn_banks, n_out_banks):
        self.s, self.nc, self.matrix, self.width = s, s.nc, matrix, width
        m = s.m
        self.out = m.sb("out", [TN, 8, D])
        self.turned = m.sb("turned", [P, 4, KC * TN])
        self.proj = m.sb("proj", [TN, 8, width])
        self.turn_ps = [m.ps(f"turn_ps{i}", [P, 512]) for i in range(n_turn_banks)]
        self.proj_ps = [m.ps(f"proj_ps{i}", [P, 512]) for i in range(n_out_banks)]
        self.out_ready, self.turn_done, self.turned_ready, self.proj_done, self.proj_ready = (
            m.sem(n) for n in ("out_ready", "turn_done", "turned_ready", "proj_done", "proj_ready"))
        self.stored, self.proj_stored = m.sems("stored", 4), m.sems("proj_stored", 4)

    def normal(self, act, tile):
        s = self.s
        slot, _ = tile.ring(4)
        slot8, round8 = tile.ring(8)
        act.wait_ge(s.shift_ready, tile.t + 1)
        if tile.from_(8):
            act.wait_ge(self.stored[slot8 // 2], round8 * 16)
            act.wait_ge(self.turn_done, tile.t - 7)
        self.nc.scalar.activation(self.out[:, slot8, :], s.w[:, slot, :], ACT.Identity, bias=s.shift[:, slot, :],
                                  scale=s.rstd[:, slot, :]).then_inc(self.out_ready, 1)

    def turn(self, pe, tile):
        slot8, _ = tile.ring(8)
        banks = len(self.turn_ps)
        pe.wait_ge(self.out_ready, tile.t + 1)
        if tile.from_(banks):
            pe.wait_ge(self.turned_ready, tile.t + 1 - banks)
        for c in range(KC):
            last = self.nc.tensor.transpose(self.turn_ps[slot8 % banks][:, c * TN:(c + 1) * TN],
                                            self.out[:, slot8, c * P:(c + 1) * P], self.s.keep["ident"][0:TN, 0:TN])
        last.then_inc(self.turn_done, 1)

    def copy_turned(self, act, tile):
        slot, _ = tile.ring(4)
        act.wait_ge(self.turn_done, tile.t + 1)
        if tile.from_(4):
            act.wait_ge(self.proj_done, tile.t - 3)
        self.nc.scalar.copy(self.turned[:, slot, :], self.turn_ps[slot % len(self.turn_ps)][:, 0:KC * TN]).then_inc(self.turned_ready, 1)

    def project(self, pe, tile):
        slot, _ = tile.ring(4)
        banks = len(self.proj_ps)
        pe.wait_ge(self.turned_ready, tile.t + 1)
        if tile.from_(banks):
            pe.wait_ge(self.proj_ready, tile.t + 1 - banks)
        for c in range(KC):
            last = self.nc.tensor.matmul(self.proj_ps[slot % banks][0:TN, 0:self.width],
                                         self.turned[:, slot, c * TN:(c + 1) * TN], self.matrix[:, c, :],
                                         start=(c == 0), stop=(c == KC - 1))
        last.then_inc(self.proj_done, 1)

    def copy_projected(self, dve, tile):
        slot8, round8 = tile.ring(8)
        dve.wait_ge(self.proj_done, tile.t + 1)
        if tile.from_(8):
            dve.wait_ge(self.proj_stored[slot8 // 2], round8 * 16 * self.proj_stores)
        self.nc.vector.tensor_copy(self.proj[:, slot8, :], self.proj_ps[slot8 % len(self.proj_ps)][0:TN, 0:self.width]).then_inc(
            self.proj_ready, 1)

    proj_stores = 1

    def store(self, sp, tile, rows_table, *proj_tables):
        if tile.slot8 % 2:
            return
        slot, _ = tile.ring(8)
        self.proj_stores = len(proj_tables)
        sp.wait_ge(self.out_ready, tile.t + 2)
        sp.dma_start(node_rows(rows_table, tile), self.out[:, slot:slot + 2, :]).then_inc(self.stored[slot // 2], 16)
        sp.wait_ge(self.proj_ready, tile.t + 2)
        for table, a, b in proj_tables:
            sp.dma_start(node_rows(table, tile, b - a), self.proj[:, slot:slot + 2, a:b]).then_inc(
                self.proj_stored[slot // 2], 16)

    def stores_done(self, sp):
        for q in range(4):
            sp.wait_ge(self.stored[q], 16 * (NT // 8))
            sp.wait_ge(self.proj_stored[q], 16 * self.proj_stores * (NT // 8))


class GcnFront:

    def __init__(self, s, weight):
        self.s, self.nc, self.weight = s, s.nc, weight
        m = s.m
        self.own = m.sb("own", [TN, 8, DW])
        self.diag = m.sb("diag", [TN, 4, TN])
        self.sum_t = m.sb("sum_t", [P, 4, KC * TN])
        self.sum_ps = [m.ps(f"sum_ps{i}", [P, 512]) for i in range(2)]
        self.conv_ps = [m.ps(f"conv_ps{i}", [P, 512]) for i in range(2)]
        self.own_loaded = m.sems("own_loaded", 4)
        self.diag_ready, self.sum_ready, self.conv_done, self.conv_used = (
            m.sem(n) for n in ("diag_ready", "sum_ready", "conv_done", "conv_used"))

    def select(self, dve, tile, further):
        s = self.s
        slot8, round8 = tile.ring(8)
        dve.wait_ge(s.gathered[slot8], (round8 + 1) * 16)
        s.select(dve, tile, scale=lambda slot, _: s.rows[:, slot, D:DW])
        further.chunks(tile, lambda k, n: s.select_chunk(dve, tile, n, scale=s.x_rows[:, D:DW]))

    def diagonal(self, act, tile):
        slot, _ = tile.ring(4)
        slot8, round8 = tile.ring(8)
        act.wait_ge(self.own_loaded[slot8 // 2], (round8 + 1) * self.own_loads * 16)
        if tile.from_(4):
            act.wait_ge(self.s.summed, tile.t - 3)
        self.nc.scalar.activation(self.diag[:, slot, :], self.s.keep["ident"][0:TN, 0:TN], ACT.Identity,
                                  scale=self.own[:, slot8, D:DW]).then_inc(self.diag_ready, 1)

    own_loads = 1

    def sums(self, pe, tile, further):
        s = self.s
        slot, _ = tile.ring(4)
        slot8, _ = tile.ring(8)
        ps = self.sum_ps[slot % 2]
        pe.wait_ge(s.sel_ready, tile.t + 1)
        if tile.from_(2):
            pe.wait_ge(self.sum_ready, tile.t - 1)

        def add(rows, sel, c, start=False):
            return self.nc.tensor.matmul(ps[:, c * TN:(c + 1) * TN], rows[:, c * P:(c + 1) * P], sel, start=start, stop=True,
                                         skip_group_check=True)

        add(s.rows[:, slot8, :], s.sel[:, slot8, :], 0, start=True)

        def chunk(k, n):
            pe.wait_ge(s.x_sel_ready, n)
            for c in range(KC):
                last = add(s.x_rows[:], s.x_sel[:], c)
            last.then_inc(s.x_summed, 1)

        further.chunks(tile, chunk)
        add(s.rows[:, slot8, :], s.sel[:, slot8, :], 1)
        pe.wait_ge(self.diag_ready, tile.t + 1)
        for c in range(KC):
            last = add(self.own[:, slot8, :], self.diag[:, slot, :], c)
        last.then_inc(s.summed, 1)

    def copy_sum(self, act, tile):
        slot, _ = tile.ring(4)
        act.wait_ge(self.s.summed, tile.t + 1)
        if tile.from_(4):
            act.wait_ge(self.conv_done, tile.t - 3)
        self.nc.scalar.copy(self.sum_t[:, slot, :], self.sum_ps[slot % 2][:, 0:KC * TN]).then_inc(self.sum_ready, 1)

    def convolve(self, pe, tile):
        slot, _ = tile.ring(4)
        pe.wait_ge(self.sum_ready, tile.t + 1)
        if tile.from_(2):
            pe.wait_ge(self.conv_used, tile.t - 1)
        for c in range(KC):
            last = self.nc.tensor.matmul(self.conv_ps[slot % 2][0:TN, 0:D], self.sum_t[:, slot, c * TN:(c + 1) * TN],
                                         self.weight[:, c, :], start=(c == 0), stop=(c == KC - 1))
        last.then_inc(self.conv_done, 1)


def build_gcn_first(nc, keep, dram, ins):
    with ExitStack() as ctx:
        s = WindowSweep(nc, ctx, keep, dram, ins, "gcn1", dram["x1"], DW)
        g = GcnFront(s, keep["w1"])
        m = s.m
        z = m.sb("z", [TN, 4, D])
        squares = m.sb("squares", [TN, 4, 1])
        length = m.sb("length", [TN, 4, 1])
        inverse = m.sb("inverse", [TN, 4, 1])
        out = m.sb("out", [TN, 8, DW])
        stored = m.sems("stored", 4)
        squares_ready, length_ready, clamped, inverse_ready, dinv_ready, out_ready = (
            m.sem(n) for n in ("squares_ready", "length_ready", "clamped", "inverse_ready", "dinv_ready", "out_ready"))
        block = m.block()

        @block.gpsimd
        def _(pool):
            s.gather(pool)

        @block.sync
        def _(sp):
            further = Further(sp, keep, s.m.name)

            def load(tile):
                if tile.slot8 % 2:
                    return
                slot, _ = tile.ring(8)
                if tile.from_(8):
                    sp.wait_ge(dinv_ready, tile.t - 6)
                sp.dma_start(g.own[:, slot:slot + 2, :], node_rows(dram["x1"], tile, DW)).then_inc(g.own_loaded[slot // 2], 16)

            def store(tile):
                if tile.slot8 % 2:
                    return
                slot, _ = tile.ring(8)
                sp.wait_ge(out_ready, tile.t + 2)
                sp.dma_start(node_rows(dram["z1"], tile, DW), out[:, slot:slot + 2, :]).then_inc(stored[slot // 2], 16)

            sweep(sp, NT, [(0, load), (6, store), (0, lambda tile: s.load_chunks(sp, further, tile))])
            for q in stored:
                sp.wait_ge(q, 16 * (NT // 8))

        @block.vector
        def _(dve):
            further = Further(dve, keep, s.m.name)

            def scale_and_bias(tile):
                slot, _ = tile.ring(4)
                slot8, _ = tile.ring(8)
                dve.wait_ge(g.conv_done, tile.t + 1)
                if tile.from_(4):
                    dve.wait_ge(out_ready, tile.t - 3)
                nc.vector.scalar_tensor_tensor(out=z[:, slot, :], in0=g.conv_ps[slot % 2][0:TN, 0:D], scalar=g.own[:, slot8, D:DW],
                                               in1=keep["b1"][0:TN, :], op0=ALU.mult, op1=ALU.add).then_inc(g.conv_used, 1)

            def inverse_length(tile):
                slot, _ = tile.ring(4)
                slot8, round8 = tile.ring(8)
                dve.wait_ge(length_ready, tile.t + 1)
                nc.vector.tensor_scalar(length[:, slot, :], length[:, slot, :], 1e-12, None, ALU.max).then_inc(clamped, 1)
                if tile.from_(8):
                    dve.wait_ge(stored[slot8 // 2], round8 * 16)
                nc.vector.tensor_copy(out[:, slot8, D:DW], g.own[:, slot8, D:DW]).then_inc(dinv_ready, 1)
                dve.wait_ge(clamped, tile.t + 1)
                nc.vector.reciprocal(inverse[:, slot, :], length[:, slot, :]).then_inc(inverse_ready, 1)

            sweep(dve, NT, [(0, lambda tile: g.select(dve, tile, further)), (2, scale_and_bias), (3, inverse_length)])

        @block.scalar
        def _(act):
            def lengths(tile):
                slot, _ = tile.ring(4)
                slot8, round8 = tile.ring(8)
                act.wait_ge(g.conv_used, tile.t + 1)
                if tile.from_(8):
                    act.wait_ge(stored[slot8 // 2], round8 * 16)
                nc.scalar.activation(out[:, slot8, 0:D], z[:, slot, :], ACT.Square,
                                     accum_out=squares[:, slot, :]).then_inc(squares_ready, 1)
                act.wait_ge(squares_ready, tile.t + 1)
                nc.scalar.activation(length[:, slot, :], squares[:, slot, :], ACT.Sqrt).then_inc(length_ready, 1)

            def unit(tile):
                slot, _ = tile.ring(4)
                slot8, _ = tile.ring(8)
                act.wait_ge(inverse_ready, tile.t + 1)
                nc.scalar.activation(out[:, slot8, 0:D], z[:, slot, :], ACT.Identity, scale=inverse[:, slot, :]).then_inc(out_ready, 1)

            sweep(act, NT, [(0, lambda tile: g.diagonal(act, tile)), (1, lambda tile: g.copy_sum(act, tile)),
                            (2, lengths), (3, unit)])

        @block.tensor
        def _(pe):
            further = Further(pe, keep, s.m.name)
            sweep(pe, NT, [(0, lambda tile: g.sums(pe, tile, further)), (1, lambda tile: g.convolve(pe, tile))])


def build_gcn_second(nc, keep, dram, ins):
    with ExitStack() as ctx:
        s = WindowSweep(nc, ctx, keep, dram, ins, "gcn2", dram["z1"], DW)
        g = GcnFront(s, keep["w2"])
        p = Projection(s, "proj", keep["wc"], FILT, 2, 2)
        m = s.m
        x1 = m.sb("x1", [TN, 8, D])
        v = m.sb("v", [TN, 4, D])
        g.own_loads = 2
        block = m.block()

        @block.gpsimd
        def _(pool):
            s.gather(pool)

        @block.sync
        def _(sp):
            further = Further(sp, keep, s.m.name)

            def load(tile):
                if tile.slot8 % 2:
                    return
                slot, _ = tile.ring(8)
                if tile.from_(8):
                    sp.wait_ge(s.w_ready, tile.t - 6)
                sp.dma_start(g.own[:, slot:slot + 2, :], node_rows(dram["z1"], tile, DW)).then_inc(g.own_loaded[slot // 2], 16)
                sp.dma_start(x1[:, slot:slot + 2, :], node_rows(dram["x1"], tile)).then_inc(g.own_loaded[slot // 2], 16)

            sweep(sp, NT, [(0, load), (8, lambda tile: p.store(sp, tile, dram["x2"], (dram["h2"], 0, FILT))),
                           (0, lambda tile: s.load_chunks(sp, further, tile))])
            p.stores_done(sp)

        @block.vector
        def _(dve):
            further = Further(dve, keep, s.m.name)

            def residual(tile):
                slot, _ = tile.ring(4)
                slot8, _ = tile.ring(8)
                dve.wait_ge(g.conv_done, tile.t + 1)
                nc.vector.scalar_tensor_tensor(out=v[:, slot, :], in0=g.conv_ps[slot % 2][0:TN, 0:D], scalar=g.own[:, slot8, D:DW],
                                               in1=keep["b2"][0:TN, :], op0=ALU.mult, op1=ALU.add).then_inc(g.conv_used, 1)
                dve.wait_ge(g.conv_used, tile.t + 1)
                if tile.from_(4):
                    dve.wait_ge(p.out_ready, tile.t - 3)
                nc.vector.scalar_tensor_tensor(out=s.w[:, slot, :], in0=x1[:, slot8, :], scalar=2.0, in1=v[:, slot, :],
                                               op0=ALU.mult, op1=ALU.add).then_inc(s.w_ready, 1)
                s.moments(dve, tile)

            sweep(dve, NT, [(0, lambda tile: g.select(dve, tile, further)), (2, residual), (3, lambda tile: s.factor(dve, tile)),
                            (5, lambda tile: p.copy_projected(dve, tile))])

        @block.scalar
        def _(act):
            sweep(act, NT, [(0, lambda tile: g.diagonal(act, tile)), (1, lambda tile: g.copy_sum(act, tile)),
                            (2, lambda tile: s.deviation(act, tile)), (3, lambda tile: p.normal(act, tile)),
                            (4, lambda tile: p.copy_turned(act, tile))])

        @block.tensor
        def _(pe):
            further = Further(pe, keep, s.m.name)
            sweep(pe, NT, [(0, lambda tile: g.sums(pe, tile, further)), (1, lambda tile: g.convolve(pe, tile)),
                           (4, lambda tile: p.turn(pe, tile)), (5, lambda tile: p.project(pe, tile))])


def build_filter(nc, keep, dram, ins):
    with ExitStack() as ctx:
        s = WindowSweep(nc, ctx, keep, dram, ins, "filter", dram["h2"], FILT,
                        columns=((ins["radial_flat"].rearrange("(r e) -> r e", r=RAD), RAD),))
        p = Projection(s, "proj", keep["w3"], HW, 1, 1)
        m = s.m
        x2 = m.sb("x2", [TN, 8, D])
        radial = m.sb("radial", [RAD, 8, W])
        message = m.sb("message", [P, 4, FILT])
        x_message = m.sb("x_message", [P, FILT])
        agg_t = m.sb("agg_t", [FILT + 1, 4, TN])
        radial_ps = m.ps("radial_ps", [P, 512])
        x_radial_ps = m.ps("x_radial_ps", [P, 512])
        agg_ps = [m.ps(f"agg_ps{i}", [P, 512]) for i in range(2)]
        out_ps = [m.ps(f"out_ps{i}", [P, 512]) for i in range(2)]
        loaded = m.sems("loaded", 4)
        ones_ready, radial_done, message_ready, x_radial_done, x_message_ready, agg_ready, out_done = (
            m.sem(n) for n in ("ones_ready", "radial_done", "message_ready", "x_radial_done", "x_message_ready", "agg_ready",
                               "out_done"))
        block = m.block()

        @block.gpsimd
        def _(pool):
            s.gather(pool, rows_free=message_ready)

        @block.sync
        def _(sp):
            further = Further(sp, keep, s.m.name)

            def load(tile):
                if tile.slot8 % 2:
                    return
                slot, _ = tile.ring(8)
                if tile.from_(8):
                    sp.wait_ge(s.w_ready, tile.t - 6)
                sp.dma_start(x2[:, slot:slot + 2, :], node_rows(dram["x2"], tile)).then_inc(loaded[slot // 2], 16)
                sp.dma_start(radial[:, slot:slot + 2, :], dram["radial"][bass.ds(tile.t, 2), :, :].rearrange(
                    "k r e -> r k e")).then_inc(loaded[slot // 2], 16)

            sweep(sp, NT, [(0, load), (8, lambda tile: p.store(sp, tile, dram["x3"], (dram["h3"], 0, HW), (dram["a_src"], D, HW))),
                           (0, lambda tile: s.load_chunks(sp, further, tile))])
            p.stores_done(sp)

        @block.vector
        def _(dve):
            further = Further(dve, keep, s.m.name)
            p.proj_stores = 2
            nc.vector.memset(agg_t[FILT:FILT + 1, :, :], 1.0).then_inc(ones_ready, 1)

            def messages(tile):
                slot, _ = tile.ring(4)
                slot8, round8 = tile.ring(8)
                s.select(dve, tile, scale=lambda slot_, tile_: keep["cut"][:, bass.ds(tile_.t, 1)])
                dve.wait_ge(s.gathered[slot8], (round8 + 1) * 16)
                dve.wait_ge(radial_done, tile.t + 1)
                if tile.from_(4):
                    dve.wait_ge(s.summed, tile.t - 3)
                nc.vector.tensor_tensor(message[:, slot, :], s.rows[:, slot8, :], radial_ps[:, 0:FILT], ALU.mult).then_inc(message_ready, 1)

                def chunk(k, n):
                    dve.wait_ge(x_radial_done, n)
                    dve.wait_ge(s.x_gathered, n * 16)
                    nc.vector.tensor_tensor(x_message[:], s.x_rows[:], x_radial_ps[:, 0:FILT], ALU.mult).then_inc(x_message_ready, 1)
                    s.select_chunk(dve, tile, n, scale=s.x_cut[:, 0:1])

                further.chunks(tile, chunk)

            def residual(tile):
                slot, _ = tile.ring(4)
                slot8, round8 = tile.ring(8)
                dve.wait_ge(out_done, tile.t + 1)
                if slot8 % 2 == 0:
                    dve.wait_ge(loaded[slot8 // 2], (round8 + 1) * 32)
                if tile.from_(4):
                    dve.wait_ge(p.out_ready, tile.t - 3)
                nc.vector.tensor_tensor(s.w[:, slot, :], out_ps[slot % 2][0:TN, 0:D], x2[:, slot8, :], ALU.add).then_inc(s.w_ready, 1)
                s.moments(dve, tile)

            sweep(dve, NT, [(0, messages), (3, residual), (4, lambda tile: s.factor(dve, tile)),
                            (6, lambda tile: p.copy_projected(dve, tile))])

        @block.scalar
        def _(act):
            def copy_sum(tile):
                slot, _ = tile.ring(4)
                act.wait_ge(s.summed, tile.t + 1)
                if tile.from_(4):
                    act.wait_ge(out_done, tile.t - 3)
                nc.scalar.copy(agg_t[0:FILT, slot, :], agg_ps[slot % 2][0:FILT, 0:TN]).then_inc(agg_ready, 1)

            sweep(act, NT, [(1, copy_sum), (3, lambda tile: s.deviation(act, tile)), (4, lambda tile: p.normal(act, tile)),
                            (5, lambda tile: p.copy_turned(act, tile))])

        @block.tensor
        def _(pe):
            further = Further(pe, keep, s.m.name)
            pe.wait_ge(ones_ready, 1)

            def filters(tile):
                slot8, round8 = tile.ring(8)
                if slot8 % 2 == 0:
                    pe.wait_ge(loaded[slot8 // 2], (round8 + 1) * 32)
                if tile.from_(1):
                    pe.wait_ge(message_ready, tile.t)
                nc.tensor.matmul(radial_ps[:, 0:FILT], radial[:, slot8, :], keep["wrad"][:], start=True, stop=True).then_inc(radial_done, 1)

            def sums(tile):
                slot, _ = tile.ring(4)
                slot8, _ = tile.ring(8)
                pe.wait_ge(message_ready, tile.t + 1)
                pe.wait_ge(s.sel_ready, tile.t + 1)
                if tile.from_(2):
                    pe.wait_ge(agg_ready, tile.t - 1)
                ps = agg_ps[slot % 2][0:FILT, :]
                half = TN // 2

                def add(msg, sel, a, b, start=False):
                    return nc.tensor.matmul(ps[:, a:b], msg, sel[:, a:b], start=start, stop=True, skip_group_check=True)

                add(message[:, slot, :], s.sel[:, slot8, :], 0, half, start=True)

                def chunk(k, n):
                    pe.wait_ge(s.x_loaded, n * (16 * s.x_loads))
                    nc.tensor.matmul(x_radial_ps[:, 0:FILT], s.x_cols[0:RAD, :], keep["wrad"][:], start=True, stop=True).then_inc(
                        x_radial_done, 1)
                    pe.wait_ge(s.x_sel_ready, n)
                    pe.wait_ge(x_message_ready, n)
                    add(x_message[:], s.x_sel[:], 0, TN).then_inc(s.x_summed, 1)

                further.chunks(tile, chunk)
                add(message[:, slot, :], s.sel[:, slot8, :], half, TN).then_inc(s.summed, 1)

            def output(tile):
                slot, _ = tile.ring(4)
                pe.wait_ge(agg_ready, tile.t + 1)
                if tile.from_(2):
                    pe.wait_ge(s.w_ready, tile.t - 1)
                nc.tensor.matmul(out_ps[slot % 2][0:TN, 0:D], agg_t[:, slot, :], keep["m2"][:], start=True, stop=True).then_inc(out_done, 1)

            sweep(pe, NT, [(0, filters), (1, sums), (2, output), (5, lambda tile: p.turn(pe, tile)),
                           (6, lambda tile: p.project(pe, tile))])


def build_scores(nc, keep, dram, ins):
    with ExitStack() as ctx:
        m = Memory(nc, ctx, "score")
        index = m.sb("index", [P, 2, 8], I32)
        rows = m.sb("rows", [P, 8, HW])
        src_score = m.sb("src_score", [P, 8, H])
        attr = m.sb("attr", [4, 8, W])
        factor = m.sb("factor", [P, 4, D])
        prod = m.sb("prod", [P, 4, D])
        dot = m.sb("dot", [P, 4, H])
        total = m.sb("total", [P, 4, H])
        leaky = m.sb("leaky", [P, 4, H])
        alpha_t = m.sb("alpha_t", [H, 8, W])
        enc_ps = [m.ps(f"enc_ps{i}", [P, 512]) for i in range(2)]
        alpha_ps = [m.ps(f"alpha_ps{i}", [P, 512]) for i in range(2)]
        index_ready, passed = m.sem("index_ready"), m.sem("passed")
        gathered, loaded, stored = m.sems("gathered", 8), m.sems("loaded", 4), m.sems("stored", 4)
        enc_done, factor_ready, prod_ready, dot_ready, total_ready, leaky_ready, turned, alpha_ready = (
            m.sem(n) for n in ("enc_done", "factor_ready", "prod_ready", "dot_ready", "total_ready", "leaky_ready", "turned",
                               "alpha_ready"))
        block = m.block()

        @block.gpsimd
        def _(pool):
            def gather(tile):
                slot, round_ = tile.ring(8)
                if slot % 4 == 0:
                    if tile.from_(8):
                        pool.wait_ge(total_ready, tile.t - 4)
                    for k, name in enumerate(("dst_e", "src_e")):
                        last = nc.gpsimd.tensor_copy(index[:, k, slot:slot + 4], keep[name][:, bass.ds(tile.t, 4)])
                    last.then_inc(index_ready, 1)
                    wait_apart(pool, index_ready, round_ * 2 + slot // 4 + 1, passed)
                pool.indirect_dma_start(out=rows[:, slot, :], out_offset=None, in_=dram["h3"],
                                        in_offset=bass.IndirectOffsetOnAxis(ap=index[:, 0, slot:slot + 1], axis=0)).then_inc(gathered[slot], 16)
                pool.indirect_dma_start(out=src_score[:, slot, :], out_offset=None, in_=dram["a_src"],
                                        in_offset=bass.IndirectOffsetOnAxis(ap=index[:, 1, slot:slot + 1], axis=0)).then_inc(gathered[slot], 16)

            sweep(pool, ET, [(0, gather)])

        @block.sync
        def _(sp):
            def load(tile):
                if tile.slot8 % 2:
                    return
                slot, _ = tile.ring(8)
                if tile.from_(8):
                    sp.wait_ge(enc_done, tile.t - 6)
                sp.dma_start(attr[:, slot:slot + 2, :], ins["attr3t"][:, bass.ds(tile.t * W, 2 * W)].rearrange(
                    "r (k e) -> r k e", k=2)).then_inc(loaded[slot // 2], 16)

            def store(tile):
                if tile.slot8 % 2:
                    return
                slot, _ = tile.ring(8)
                sp.wait_ge(alpha_ready, tile.t + 2)
                sp.dma_start(dram["alpha"][:, bass.ds(tile.t * W, 2 * W)].rearrange("h (k e) -> h k e", k=2),
                             alpha_t[:, slot:slot + 2, :]).then_inc(stored[slot // 2], 16)

            sweep(sp, ET, [(0, load), (6, store)])
            for q in stored:
                sp.wait_ge(q, 16 * (ET // 8))

        @block.tensor
        def _(pe):
            def encode(tile):
                slot8, round8 = tile.ring(8)
                if slot8 % 2 == 0:
                    pe.wait_ge(loaded[slot8 // 2], (round8 + 1) * 16)
                if tile.from_(2):
                    pe.wait_ge(factor_ready, tile.t - 1)
                nc.tensor.matmul(enc_ps[slot8 % 2][:, 0:D], attr[:, slot8, :], keep["wedge"][:], start=True, stop=True).then_inc(enc_done, 1)

            def turn(tile):
                slot, _ = tile.ring(4)
                pe.wait_ge(leaky_ready, tile.t + 1)
                if tile.from_(2):
                    pe.wait_ge(alpha_ready, tile.t - 1)
                nc.tensor.transpose(alpha_ps[slot % 2][0:H, 0:W], leaky[:, slot, :], keep["ident"][:]).then_inc(turned, 1)

            sweep(pe, ET, [(0, encode), (2, turn)])

        @block.vector
        def _(dve):
            def factors(tile):
                slot, _ = tile.ring(4)
                dve.wait_ge(enc_done, tile.t + 1)
                nc.vector.scalar_tensor_tensor(out=factor[:, slot, :], in0=enc_ps[slot % 2][:, 0:D], scalar=0.0, in1=keep["adst"][:],
                                               op0=ALU.max, op1=ALU.add).then_inc(factor_ready, 1)

            def scores(tile):
                slot, _ = tile.ring(4)
                slot8, round8 = tile.ring(8)
                dve.wait_ge(gathered[slot8], (round8 + 1) * 32)
                dve.wait_ge(factor_ready, tile.t + 1)
                nc.vector.tensor_tensor(prod[:, slot, :], factor[:, slot, :], rows[:, slot8, 0:D], ALU.mult).then_inc(prod_ready, 1)
                dve.wait_ge(prod_ready, tile.t + 1)
                nc.vector.tensor_reduce(dot[:, slot, :], prod[:, slot, :].rearrange("p (h d) -> p h d", h=H), AX_X, ALU.add).then_inc(dot_ready, 1)
                dve.wait_ge(dot_ready, tile.t + 1)
                nc.vector.tensor_tensor(total[:, slot, :], dot[:, slot, :], src_score[:, slot8, :], ALU.add).then_inc(total_ready, 1)
                dve.wait_ge(total_ready, tile.t + 1)
                if tile.from_(4):
                    dve.wait_ge(turned, tile.t - 3)
                nc.vector.scalar_tensor_tensor(out=leaky[:, slot, :], in0=total[:, slot, :], scalar=0.2, in1=total[:, slot, :],
                                               op0=ALU.mult, op1=ALU.max).then_inc(leaky_ready, 1)

            sweep(dve, ET, [(0, factors), (1, scores)])

        @block.scalar
        def _(act):
            def copy_alpha(tile):
                slot, _ = tile.ring(4)
                slot8, round8 = tile.ring(8)
                act.wait_ge(turned, tile.t + 1)
                if tile.from_(8):
                    act.wait_ge(stored[slot8 // 2], round8 * 16)
                nc.scalar.copy(alpha_t[:, slot8, :], alpha_ps[slot % 2][0:H, 0:W]).then_inc(alpha_ready, 1)

            sweep(act, ET, [(2, copy_alpha)])


def build_softmax(nc, keep, dram, ins):
    with ExitStack() as ctx:
        m = Memory(nc, ctx, "softmax")
        alpha = m.sb("alpha", [P, SQ])
        dst = m.sb("dst", [P, SQ + 2])
        start = m.sb("start", [P, SQ])
        inside = m.sb("inside", [P, SQ])
        reset = m.sb("reset", [P, SQ])
        end = m.sb("end", [P, SQ])
        before_end = m.sb("before_end", [P, SQ])
        run = m.sb("run", [P, SQ])
        last = m.sb("last", [P, SQ])
        seg = m.sb("seg", [P, SQ])
        col = m.sb("col", [P, 5])
        flags = m.sb("flags", [H, 2, SEG])
        no_start, no_end, start_reset = m.sb("no_start", [H, SEG]), m.sb("no_end", [H, SEG]), m.sb("start_reset", [H, SEG])
        piece = m.sb("piece", [H, SEG])
        piece_sum = m.sb("piece_sum", [H, SEG])
        carry = m.sb("carry", [H, SEG])
        carry_in = m.sb("carry_in", [P, 1])
        windows = m.sb("windows", [P, NJ, H, W])
        loaded, chain_sem, exp_ready, shifted = m.sem("loaded"), m.sem("chain"), m.sem("exp_ready"), m.sem("shifted")
        flags_ready, flags_out, flags_back = m.sem("flags_ready"), m.sem("flags_out"), m.sem("flags_back")
        outcome_ready, outcome_out, outcome_back = m.sem("outcome_ready"), m.sem("outcome_out"), m.sem("outcome_back")
        carry_ready, carry_out, carry_back = m.sem("carry_ready"), m.sem("carry_out"), m.sem("carry_back")
        attn_ready, attn_out = m.sem("attn_ready"), m.sem("attn_out")
        window_in, window_out = m.sems("window_in", NJ), m.sem("window_out")
        flat = lambda t: t.rearrange("h (s q) -> (h s) q", s=SEG)
        SCANS = 4
        block = m.block()

        @block.sync
        def _(sp):
            sp.dma_start(alpha[:], flat(dram["alpha"])).then_inc(loaded, 16)
            for h in range(H):
                sp.dma_start(dst[h * SEG:(h + 1) * SEG, :], bass.AP(tensor=dram["dst_ext"].tensor, offset=0,
                             ap=[[SQ, SEG], [1, SQ + 2]])).then_inc(loaded, 16)
            carry_d = dram["carry"]
            sp.wait_ge(flags_ready, 1)
            for k in range(2):
                sp.dma_start(carry_d[k].unsqueeze(1), col[:, k:k + 1]).then_inc(flags_out, 16)
            sp.wait_ge(flags_out, 32)
            for k in range(2):
                sp.dma_start(flags[:, k, :], carry_d[k].rearrange("(h s) -> h s", h=H)).then_inc(flags_back, 16)
            for n in range(SCANS):
                sp.wait_ge(outcome_ready, n + 1)
                sp.dma_start(carry_d[2].unsqueeze(1), col[:, 2:3]).then_inc(outcome_out, 16)
                sp.wait_ge(outcome_out, 16 * (n + 1))
                sp.dma_start(piece[:], carry_d[2].rearrange("(h s) -> h s", h=H)).then_inc(outcome_back, 16)
                sp.wait_ge(carry_ready, n + 1)
                sp.dma_start(carry_d[3].rearrange("(h s) -> h s", h=H), carry[:]).then_inc(carry_out, 16)
                sp.wait_ge(carry_out, 16 * (n + 1))
                sp.dma_start(carry_in[:], carry_d[3].unsqueeze(1)).then_inc(carry_back, 16)
            sp.wait_ge(attn_ready, 1)
            sp.dma_start(flat(dram["attn"]), seg[:]).then_inc(attn_out, 16)
            for j in range(NJ):
                sp.wait_ge(window_in[j], 16 * H)
                sp.dma_start(dram["attn_windows"][j * P:(j + 1) * P, :, :], windows[:, j, :, :]).then_inc(window_out, 16)
            sp.wait_ge(window_out, 16 * NJ)

        @block.gpsimd
        def _(pool):
            pool.wait_ge(attn_out, 16)
            attn = dram["attn"].rearrange("h e -> (h e)").unsqueeze(1)
            for j in range(NJ):
                for h in range(H):
                    pool.indirect_dma_start(out=windows[:, j, h, :], out_offset=None, in_=attn,
                                            in_offset=bass.IndirectOffsetOnAxis(ap=keep["start_cols"][:, h, j:j + 1], axis=0),
                                            ).then_inc(window_in[j], 16)

        @block.scalar
        def _(act):
            act.wait_ge(shifted, 1)
            nc.scalar.activation(alpha[:], alpha[:], ACT.Exp).then_inc(exp_ready, 1)

        @block.vector
        def _(dve):
            chain = Chained(dve, chain_sem)
            dve.wait_ge(loaded, 16 * (H + 1))
            chain(nc.vector.tensor_tensor(start[:], dst[:, 1:SQ + 1], dst[:, 0:SQ], ALU.not_equal))
            chain(nc.vector.tensor_tensor(end[:], dst[:, 1:SQ + 1], dst[:, 2:SQ + 2], ALU.not_equal))
            chain(nc.vector.tensor_scalar(inside[:], start[:], -1.0, 1.0, ALU.mult, ALU.add))
            chain(nc.vector.tensor_scalar(reset[:], start[:], -BIG, None, ALU.mult))
            chain(nc.vector.tensor_scalar(before_end[:], end[:], -1.0, 1.0, ALU.mult, ALU.add))
            chain(nc.vector.tensor_reduce(col[:, 0:1], start[:], AX_X, ALU.max))
            chain(nc.vector.tensor_reduce(col[:, 1:2], end[:], AX_X, ALU.max))
            dve.sem_inc(flags_ready, 1)
            dve.wait_ge(flags_back, 32)
            chain(nc.vector.tensor_scalar(no_start[:], flags[:, 0, :], -1.0, 1.0, ALU.mult, ALU.add))
            chain(nc.vector.tensor_scalar(no_end[:], flags[:, 1, :], -1.0, 1.0, ALU.mult, ALU.add))
            chain(nc.vector.tensor_scalar(start_reset[:], flags[:, 0, :], -BIG, None, ALU.mult))
            scans = [0]

            def carried_scan(out, keep_, add, ops, piece_keep, empty, backward=False):
                flip = (lambda t: t[:, ::-1]) if backward else (lambda t: t[:, :])
                final = out[:, 0:1] if backward else out[:, SQ - 1:SQ]
                n = scans[0] = scans[0] + 1
                chain(nc.vector.tensor_tensor_scan(flip(out), flip(keep_), flip(add), empty, ops[0], ops[1]))
                chain(nc.vector.tensor_copy(col[:, 2:3], final))
                dve.sem_inc(outcome_ready, 1)
                dve.wait_ge(outcome_back, 16 * n)
                chain(nc.vector.tensor_tensor_scan(flip(piece_sum), flip(piece_keep), flip(piece), empty, ops[0], ops[1]))
                chain(nc.vector.memset(carry[:], empty))
                to, of = (carry[:, 0:SEG - 1], piece_sum[:, 1:SEG]) if backward else (carry[:, 1:SEG], piece_sum[:, 0:SEG - 1])
                chain(nc.vector.tensor_copy(to, of))
                dve.sem_inc(carry_ready, 1)
                dve.wait_ge(carry_back, 16 * n)
                chain(nc.vector.tensor_tensor_scan(flip(out), flip(keep_), flip(add), carry_in[:, 0:1], ops[0], ops[1]))

            def spread_last(out, value):
                chain(nc.vector.tensor_tensor(last[:], value[:], end[:], ALU.mult))
                carried_scan(out, before_end, last, (ALU.mult, ALU.add), no_end, 0.0, backward=True)

            carried_scan(run, reset, alpha, (ALU.add, ALU.max), start_reset, -BIG)
            spread_last(seg, run)
            nc.vector.tensor_tensor(alpha[:], alpha[:], seg[:], ALU.subtract).then_inc(shifted, 1)
            dve.wait_ge(exp_ready, 1)
            carried_scan(run, inside, alpha, (ALU.mult, ALU.add), no_start, 0.0)
            spread_last(seg, run)
            chain(nc.vector.tensor_scalar(seg[:], seg[:], 1e-10, None, ALU.max))
            chain(nc.vector.reciprocal(seg[:], seg[:]))
            nc.vector.tensor_tensor(seg[:], seg[:], alpha[:], ALU.mult).then_inc(attn_ready, 1)


def build_gat(nc, keep, dram, ins, out):
    with ExitStack() as ctx:
        s = WindowSweep(nc, ctx, keep, dram, ins, "gat", dram["h3"], HW, columns=((dram["attn"], H),))
        m = s.m
        x3 = m.sb("x3", [TN, 8, D])
        attn = m.sb("attn", [H, 8, W])
        message = m.sb("message", [P, 4, D])
        x_message = m.sb("x_message", [P, D])
        v = m.sb("v", [TN, 4, D])
        normed = m.sb("normed", [TN, 8, D])
        attn_ps = [m.ps(f"attn_ps{i}", [P, 512]) for i in range(2)]
        x_attn_ps = m.ps("x_attn_ps", [P, 512])
        sum_ps = [m.ps(f"sum_ps{i}", [P, 512]) for i in range(2)]
        loaded, stored = m.sems("loaded", 4), m.sems("stored", 4)
        turned, message_ready, x_turned, x_message_ready, v_ready, out_ready = (
            m.sem(n) for n in ("turned", "message_ready", "x_turned", "x_message_ready", "v_ready", "out_ready"))
        block = m.block()

        @block.gpsimd
        def _(pool):
            s.gather(pool, rows_free=message_ready)

        @block.sync
        def _(sp):
            further = Further(sp, keep, s.m.name)

            def load(tile):
                if tile.slot8 % 2:
                    return
                slot, _ = tile.ring(8)
                if tile.from_(8):
                    sp.wait_ge(s.w_ready, tile.t - 6)
                sp.dma_start(x3[:, slot:slot + 2, :], node_rows(dram["x3"], tile)).then_inc(loaded[slot // 2], 16)
                sp.dma_start(attn[:, slot:slot + 2, :], dram["attn_windows"][bass.ds(tile.t, 2), :, :].rearrange(
                    "k h e -> h k e")).then_inc(loaded[slot // 2], 16)

            def store(tile):
                if tile.slot8 % 2:
                    return
                slot, _ = tile.ring(8)
                sp.wait_ge(out_ready, tile.t + 2)
                sp.dma_start(node_rows(out, tile), normed[:, slot:slot + 2, :]).then_inc(stored[slot // 2], 16)

            sweep(sp, NT, [(0, load), (6, store), (0, lambda tile: s.load_chunks(sp, further, tile))])
            for q in stored:
                sp.wait_ge(q, 16 * (NT // 8))

        @block.vector
        def _(dve):
            further = Further(dve, keep, s.m.name)
            heads = lambda rows: rows[:, 0:D].rearrange("p (h d) -> p h d", h=H)
            weights = lambda ps: ps[:, 0:H].unsqueeze(2).broadcast_to([P, H, HD])

            def messages(tile):
                slot, _ = tile.ring(4)
                slot8, round8 = tile.ring(8)
                s.select(dve, tile)
                dve.wait_ge(s.gathered[slot8], (round8 + 1) * 16)
                dve.wait_ge(turned, tile.t + 1)
                if tile.from_(4):
                    dve.wait_ge(s.summed, tile.t - 3)
                nc.vector.tensor_tensor(heads(message[:, slot, :]), heads(s.rows[:, slot8, :]), weights(attn_ps[slot % 2]),
                                        ALU.mult).then_inc(message_ready, 1)

                def chunk(k, n):
                    dve.wait_ge(x_turned, n)
                    dve.wait_ge(s.x_gathered, n * 16)
                    nc.vector.tensor_tensor(heads(x_message[:]), heads(s.x_rows[:]), weights(x_attn_ps), ALU.mult).then_inc(x_message_ready, 1)
                    s.select_chunk(dve, tile, n)

                further.chunks(tile, chunk)

            def residual(tile):
                slot, _ = tile.ring(4)
                slot8, round8 = tile.ring(8)
                dve.wait_ge(s.summed, tile.t + 1)
                nc.vector.tensor_tensor(v[:, slot, :], sum_ps[slot % 2][0:TN, 0:D], keep["bias3"][0:TN, :], ALU.add).then_inc(v_ready, 1)
                if slot8 % 2 == 0:
                    dve.wait_ge(loaded[slot8 // 2], (round8 + 1) * 32)
                dve.wait_ge(v_ready, tile.t + 1)
                if tile.from_(4):
                    dve.wait_ge(out_ready, tile.t - 3)
                nc.vector.tensor_tensor(s.w[:, slot, :], v[:, slot, :], x3[:, slot8, :], ALU.add).then_inc(s.w_ready, 1)
                s.moments(dve, tile)

            sweep(dve, NT, [(0, messages), (2, residual), (3, lambda tile: s.factor(dve, tile))])

        @block.scalar
        def _(act):
            def normal(tile):
                slot, _ = tile.ring(4)
                slot8, round8 = tile.ring(8)
                act.wait_ge(s.shift_ready, tile.t + 1)
                if tile.from_(8):
                    act.wait_ge(stored[slot8 // 2], round8 * 16)
                nc.scalar.activation(normed[:, slot8, :], s.w[:, slot, :], ACT.Identity, bias=s.shift[:, slot, :],
                                     scale=s.rstd[:, slot, :]).then_inc(out_ready, 1)

            sweep(act, NT, [(2, lambda tile: s.deviation(act, tile)), (3, normal)])

        @block.tensor
        def _(pe):
            further = Further(pe, keep, s.m.name)

            def turn(tile):
                slot8, round8 = tile.ring(8)
                if slot8 % 2 == 0:
                    wait_apart(pe, loaded[slot8 // 2], (round8 + 1) * 32, s.passed[3])
                if tile.from_(2):
                    wait_apart(pe, message_ready, tile.t - 1, s.passed[3])
                nc.tensor.transpose(attn_ps[slot8 % 2][:, 0:H], attn[:, slot8, :], keep["ident"][0:H, 0:H]).then_inc(turned, 1)

            def sums(tile):
                slot, _ = tile.ring(4)
                slot8, _ = tile.ring(8)
                pe.wait_ge(message_ready, tile.t + 1)
                pe.wait_ge(s.sel_ready, tile.t + 1)
                if tile.from_(2):
                    pe.wait_ge(s.w_ready, tile.t - 1)
                ps = sum_ps[slot % 2][0:TN, :]
                half = D // 2

                def add(msg, sel, a, b, start=False):
                    return nc.tensor.matmul(ps[:, a:b], sel, msg[:, a:b], start=start, stop=True, skip_group_check=True)

                add(message[:, slot, :], s.sel[:, slot8, :], 0, half, start=True)

                def chunk(k, n):
                    wait_apart(pe, s.x_loaded, n * (16 * s.x_loads), s.passed[3])
                    nc.tensor.transpose(x_attn_ps[:, 0:H], s.x_cols[0:H, :], keep["ident"][0:H, 0:H]).then_inc(x_turned, 1)
                    pe.wait_ge(s.x_sel_ready, n)
                    pe.wait_ge(x_message_ready, n)
                    add(x_message[:], s.x_sel[:], 0, D).then_inc(s.x_summed, 1)

                further.chunks(tile, chunk)
                add(message[:, slot, :], s.sel[:, slot8, :], half, D).then_inc(s.summed, 1)

            sweep(pe, NT, [(0, turn), (1, sums)])


def build(nc, ins, out, last="gat"):
    def scratch(name, shape):
        return nc.dram_tensor(name, shape, F32, kind="Internal").ap()

    dram = {
        "dst_f": scratch("dst_f", [EP]), "src_f": scratch("src_f", [EP]), "cut_f": scratch("cut_f", [EP]),
        "dst_ext": scratch("dst_ext", [EP + 2]),
        "starts": nc.dram_tensor("tile_starts", [NJ * P], I32, kind="Internal").ap(),
        "radial": scratch("radial_windows", [NJ * P, RAD, W]),
        "x1": scratch("x1", [NP, DW]), "z1": scratch("z1", [NP, DW]), "x2": scratch("x2", [NP, D]),
        "h2": scratch("h2", [NP, FILT]), "x3": scratch("x3", [NP, D]), "h3": scratch("h3", [NP, HW]),
        "a_src": scratch("a_src_h", [NP, H]), "alpha": scratch("alpha", [H, EP]), "attn": scratch("attn", [H, EP]),
        "attn_windows": scratch("attn_windows", [NJ * P, H, W]), "carry": scratch("carry", [4, P]),
    }
    with ExitStack() as ctx:
        m = Memory(nc, ctx, "keep")
        keep = {
            "wl": m.sb("wl", [P, KC, D]), "wr": m.sb("wr", [P, KC, D]), "wln": m.sb("wln", [P, KC, D]),
            "w1": m.sb("w1", [P, KC, D]), "w2": m.sb("w2", [P, KC, D]), "w3": m.sb("w3", [P, KC, HW]),
            "bl": m.sb("bl", [P, KC]), "wrad": m.sb("wrad", [RAD, FILT]), "wedge": m.sb("wedge", [4, D]),
            "b1": m.sb("b1", [P, D]), "b2": m.sb("b2", [P, D]), "bias3": m.sb("bias3", [P, D]), "adst": m.sb("adst", [P, D]),
            "wc": m.sb("wc", [P, KC, FILT]), "m2": m.sb("m2", [FILT + 1, D]),
            "ident": m.sb("ident", [P, P]), "ones": m.sb("ones", [P, P]), "eps": m.sb("eps", [P, 1]),
            "iota": m.sb("iota", [P, TN]), "base": m.sb("base", [P, NT]),
            "src_e": m.sb("src_e", [P, ET], I32), "dst_e": m.sb("dst_e", [P, ET], I32),
            "src": m.sb("src", [P, NT], I32), "drel": m.sb("drel", [P, NT]), "cut": m.sb("cut", [P, NT]),
            "starts": m.sb("starts", [1, NT], I32), "over": m.sb("over", [1, NT + 1], I32),
            "start_cols": m.sb("start_cols", [P, RAD, NJ], I32),
        }
        build_setup(nc, keep, dram, ins)
        build_sage(nc, keep, dram, ins)
        if last == "sage":
            return
        build_gcn_first(nc, keep, dram, ins)
        if last == "gcn1":
            return
        build_gcn_second(nc, keep, dram, ins)
        if last == "gcn2":
            return
        build_filter(nc, keep, dram, ins)
        if last == "filter":
            return
        build_scores(nc, keep, dram, ins)
        build_softmax(nc, keep, dram, ins)
        if last == "softmax":
            return
        build_gat(nc, keep, dram, ins, out)


def layouts(inputs):
    import numpy as np

    a = {k: np.asarray(v) for k, v in inputs.items()}
    rows = lambda v, n: np.concatenate([v, np.zeros((n - v.shape[0],) + v.shape[1:], v.dtype)])
    x = rows(a["x"], NP)
    src, dst = rows(a["src"], EP), np.concatenate([a["dst"], np.full(EP - E, PAD_DST, a["dst"].dtype)])
    attr3 = np.concatenate([rows(a["edge_attr_3"], EP), np.ones((EP, 1), a["edge_attr_3"].dtype)], axis=1)
    radial = np.ascontiguousarray(rows(a["edge_attr_12"], EP).T)
    column = lambda v: np.ascontiguousarray(v.reshape(KC, P).T)
    t = lambda name: np.ascontiguousarray(a[name].T)
    return {
        "x": x, "xt": np.ascontiguousarray(x.T), "src_flat": src, "dst_flat": dst,
        "src_by_tile": np.ascontiguousarray(src.reshape(ET, W).T), "dst_by_tile": np.ascontiguousarray(dst.reshape(ET, W).T),
        "dist_flat": rows(a["edge_weight"], EP), "radial_flat": radial.reshape(-1),
        "attr3t": np.ascontiguousarray(attr3.T),
        "L0_wlt": t("L0_gnn_W_l"), "L0_wrt": t("L0_gnn_W_r"), "L0_wlnt": t("L0_gnn_W_ln"), "L0_bl": column(a["L0_gnn_b_l"]),
        "L1_w1": a["L1_gnn_W1"], "L1_w2": a["L1_gnn_W2"], "L1_b1": a["L1_gnn_b1"], "L1_b2": a["L1_gnn_b2"],
        "L2_wn": a["L2_gnn_W_node_to_message"], "L2_wradt": t("L2_gnn_W_radial_to_message"), "L2_lin1t": t("L2_gnn_W_lin1"),
        "L2_lin2b": np.concatenate([a["L2_gnn_W_lin2"], a["L2_gnn_b_lin2"][:, None]], axis=1),
        "L2_mnt": t("L2_gnn_W_message_to_node"),
        "L3_wt": t("L3_gnn_W"), "L3_w": a["L3_gnn_W"], "L3_asrc": column(a["L3_gnn_a_src"].reshape(-1)),
        "L3_adst": a["L3_gnn_a_dst"].reshape(-1), "L3_bias": a["L3_gnn_bias"],
        "L3_wedge": np.concatenate([t("L3_gnn_edge_W"), a["L3_gnn_edge_b"][None]], axis=0),
    }


def kernel(**inputs):
    import numpy as np
    import concourse.bacc as bacc
    from concourse.bass_utils import run_bass_kernel_spmd

    nc = bacc.Bacc("TRN2", target_bir_lowering=False, num_devices=1)
    arrays = layouts(inputs)
    ins = {k: nc.dram_tensor(f"in_{k}", v.shape, mybir.dt.from_np(v.dtype), kind="ExternalInput").ap() for k, v in arrays.items()}
    out = nc.dram_tensor("out", (NP, D), F32, kind="ExternalOutput").ap()
    build(nc, ins, out)
    r = run_bass_kernel_spmd(nc, [{f"in_{k}": v for k, v in arrays.items()}], core_ids=[0])
    return r.results[0]["out"][:N]
```

```python
from contextlib import ExitStack

import concourse.bass as bass
from concourse import mybir

F32 = mybir.dt.float32
I32 = mybir.dt.int32
BF16 = mybir.dt.bfloat16
ALU = mybir.AluOpType
ACT = mybir.ActivationFunctionType
AX_X = mybir.AxisListType.X

N = 50000
E = 50000
D = 256
P = 128
KC = D // P
TN = 96
UNROLL = 8
NT = -(-N // (TN * UNROLL)) * UNROLL
NP = NT * TN
W = 128
ET = -(-(E + W) // (W * UNROLL)) * UNROLL
EP = ET * W
EC = EP // P
PAD_DST = 60000
H, HD = 8, 32
FILT = 64
RAD = 12
HW = D + H
DW = D + 1
TG = 24
NG = NT // TG
NJ = -(-NT // P)
SEG = P // H
SQ = EP // SEG
BIG = 1e30
EPS = 1e-5

assert NG * TG == NT and NT * TN >= N and EC * P == EP and PAD_DST >= NP


class Tile:

    def __init__(self, round8, slot8):
        self.round8, self.slot8 = round8, slot8
        self.t = round8 * 8 + slot8
        self.peeled = isinstance(round8, int)

    def from_(self, n):
        return not self.peeled or self.t >= n

    def ring(self, n):
        return self.slot8 % n, self.round8 * (8 // n) + self.slot8 // n


def sweep(eng, count, stages):
    def step(round8, slot8, only=lambda t: True):
        for lag, stage in stages:
            tile = Tile(round8 + (slot8 - lag) // 8, (slot8 - lag) % 8)
            if not tile.peeled or only(tile.t):
                stage(tile)

    longest = max(lag for lag, _ in stages)
    first = 1 + -(-longest // UNROLL)
    for r in range(first):
        for s in range(UNROLL):
            step(r, s, lambda t: t >= 0)
    with eng.Fori(first, count // UNROLL) as r:
        for s in range(UNROLL):
            step(r, s)
    for s in range(longest):
        step(count // UNROLL, s, lambda t: t < count)


class Memory:

    def __init__(self, nc, ctx, name):
        self.nc, self.ctx, self.name, self.semaphores = nc, ctx, name, []

    def sb(self, name, shape, dt=F32):
        return self.ctx.enter_context(self.nc.sbuf_tensor(f"{self.name}_{name}", shape, dt))

    def ps(self, name, shape):
        return self.ctx.enter_context(self.nc.psum_tensor(f"{self.name}_{name}", shape, F32))

    def sem(self, name):
        self.semaphores.append(self.nc.alloc_semaphore(f"{self.name}_{name}"))
        return self.semaphores[-1]

    def sems(self, name, n):
        return [self.sem(f"{name}{i}") for i in range(n)]

    def block(self):
        self.ctx.callback(self.free_semaphores)
        return self.ctx.enter_context(self.nc.Block())

    def free_semaphores(self):
        self.nc.clear_and_free_semaphores(self.semaphores)
        self.nc.all_engine_barrier()


def wait_apart(eng, sem, value, passed):
    eng.wait_ge(sem, value)
    eng.sem_inc(passed, 1)


class Chained:

    def __init__(self, eng, sem):
        self.eng, self.sem, self.n = eng, sem, 0

    def __call__(self, instruction, by=1):
        instruction.then_inc(self.sem, by)
        self.n += by
        self.eng.wait_ge(self.sem, self.n)


def build_setup(nc, keep, dram, ins):
    with ExitStack() as ctx:
        m = Memory(nc, ctx, "setup")
        wn = m.sb("wn", [FILT, D])
        lin1t = m.sb("lin1t", [FILT, FILT])
        lin2b = m.sb("lin2b", [FILT, FILT + 1])
        mnt = m.sb("mnt", [FILT, D])
        w3 = m.sb("w3", [P, KC, D])
        asrc = m.sb("asrc", [P, KC])
        hsel = m.sb("hsel", [P, KC, H])
        ahead = m.sb("ahead", [P, KC, H])
        dst_x = m.sb("dst_x", [P, EC + 2], I32)
        src_i = m.sb("src_i", [P, EC], I32)
        dist = m.sb("dist", [P, EC])
        dstf = m.sb("dstf", [P, EC])
        srcf = m.sb("srcf", [P, EC])
        wraps = m.sb("wraps", [P, EC])
        half_pi = m.sb("half_pi", [P, 1])
        ones_e = m.sb("ones_e", [P, EC])
        same = m.sb("same", [P, EC])
        run = m.sb("run", [P, EC])
        count_e = m.sb("count_e", [P, EC])
        count_inv = m.sb("count_inv", [P, EC])
        piece_col = m.sb("piece_col", [P, 2])
        piece_row = m.sb("piece_row", [1, 2, P])
        piece_run = m.sb("piece_run", [1, P])
        carry_row = m.sb("carry_row", [1, P])
        carry_in = m.sb("carry_in", [P, 1])
        dst_e = m.sb("dst_e", [P, ET], I32)
        group_start = m.sb("group_start", [P, NG + 1])
        tile_start = m.sb("tile_start", [P, TG + 1])
        past_group = m.sb("past_group", [P, EC, NG + 1], BF16)
        in_group = m.sb("in_group", [P, EC, NG], BF16)
        group_no = m.sb("group_no", [P, EC])
        rest = m.sb("rest", [P, EC])
        before_tile = m.sb("before_tile", [P, EC, TG + 1], BF16)
        radial_rows = m.sb("radial_rows", [P, NJ, RAD, W])
        iota_g = m.sb("iota_g", [NG, NG])
        part_g = m.sb("part_g", [NG, 1])
        earlier = m.sb("earlier", [NG, NG])
        within = m.sb("within", [NG, TG + 1])
        starts = m.sb("starts", [NG, TG])
        starts_i = m.sb("starts_i", [NG, TG], I32)
        zero_i = m.sb("zero_i", [1, NJ * P], I32)
        row = m.sb("row", [1, NT], I32)
        rowf = m.sb("rowf", [1, NT])
        cnt = m.sb("cnt", [1, NT])
        cnt_i = m.sb("cnt_i", [1, NT], I32)
        over_i = m.sb("over_i", [1, NT], I32)
        start_cols = m.sb("start_cols", [P, NJ], I32)
        window_rows = m.sb("window_rows", [P, 4, NJ, W])
        ident = keep["ident"]
        ps_fold = m.ps("ps_fold", [P, 512])
        ps_fold2 = m.ps("ps_fold2", [P, 512])
        ps_cnt = m.ps("ps_cnt", [P, 512])
        ps_base = m.ps("ps_base", [P, 512])
        ps_win = [m.ps(f"ps_win{i}", [P, W]) for i in range(2)]

        weights_in, edges_in, pads_out = m.sem("weights_in"), m.sem("edges_in"), m.sem("pads_out")
        kept_in = m.sem("kept_in")
        iotas_done, consts_done = m.sem("iotas_done"), m.sem("consts_done")
        dve_chain, act_chain = m.sem("dve_chain"), m.sem("act_chain")
        heads_ready, fold1, fold2, folds_copied = (m.sem(x) for x in ("heads_ready", "fold1", "fold2", "folds_copied"))
        wraps_ready, cutoff_ready = m.sem("wraps_ready"), m.sem("cutoff_ready")
        flat_ready, flat_out = m.sem("flat_ready"), m.sem("flat_out")
        onehots_ready, counted, within_ready, based = (m.sem(x) for x in ("onehots_ready", "counted", "within_ready", "based"))
        starts_ready, starts_out, starts_back = m.sem("starts_ready"), m.sem("starts_out"), m.sem("starts_back")
        index_ready, windows_in = m.sem("index_ready"), m.sem("windows_in")
        radial_in, radial_out = m.sems("radial_in", NJ), m.sem("radial_out")
        piece_ready, piece_turned, carry_ready, carry_turned = (m.sem(x) for x in ("piece_ready", "piece_turned", "carry_ready", "carry_turned"))
        count_ready, count_out, counts_in = m.sem("count_ready"), m.sem("count_out"), m.sem("counts_in")
        ident_zeroed, ident_ready = m.sem("ident_zeroed"), m.sem("ident_ready")
        turned, turned_used = m.sem("turned"), m.sem("turned_used")

        turns = [(j, k) for j in range(NJ) for k in range(3)] + [(j, 3) for j in range(NJ)]
        block = m.block()

        @block.sync
        def _(sp):
            n = 0
            for name, src in (("wl", "L0_wlt"), ("wr", "L0_wrt"), ("wln", "L0_wlnt"), ("w1", "L1_w1"), ("w2", "L1_w2")):
                sp.dma_start(keep[name][:], ins[src].rearrange("(c p) o -> p c o", p=P)).then_inc(kept_in, 16)
                n += 1
            sp.dma_start(keep["w3"][:, :, 0:D], ins["L3_wt"].rearrange("(c p) o -> p c o", p=P)).then_inc(kept_in, 16)
            sp.dma_start(keep["bl"][:], ins["L0_bl"]).then_inc(kept_in, 16)
            sp.dma_start(keep["wrad"][:], ins["L2_wradt"]).then_inc(kept_in, 16)
            sp.dma_start(keep["wedge"][:], ins["L3_wedge"]).then_inc(kept_in, 16)
            for name, src in (("b1", "L1_b1"), ("b2", "L1_b2"), ("adst", "L3_adst")):
                sp.dma_start(keep[name][:], ins[src].partition_broadcast(P)).then_inc(kept_in, 16)
            sp.dma_start(keep["bias3"][:], ins["L3_bias"].unsqueeze(0)).then_inc(kept_in, 16)
            sp.dma_start(keep["src_e"][:], ins["src_by_tile"]).then_inc(kept_in, 16)
            for dst_, src in ((wn, "L2_wn"), (lin1t, "L2_lin1t"), (lin2b, "L2_lin2b"), (mnt, "L2_mnt")):
                sp.dma_start(dst_[:], ins[src]).then_inc(weights_in, 16)
            sp.dma_start(w3[:], ins["L3_w"].rearrange("(c p) k -> p c k", p=P)).then_inc(weights_in, 16)
            sp.dma_start(asrc[:], ins["L3_asrc"]).then_inc(weights_in, 16)
            sp.wait_ge(flat_ready, 3)
            sp.wait_ge(cutoff_ready, 1)
            sp.dma_start(dram["dst_f"].rearrange("(p c) -> p c", p=P), dstf[:]).then_inc(flat_out, 16)
            sp.dma_start(dram["src_f"].rearrange("(p c) -> p c", p=P), srcf[:]).then_inc(flat_out, 16)
            sp.dma_start(dram["cut_f"].rearrange("(p c) -> p c", p=P), dist[:]).then_inc(flat_out, 16)
            sp.wait_ge(starts_ready, 1)
            sp.dma_start(dram["starts"][0:NT].rearrange("(g t) -> g t", t=TG), starts_i[:]).then_inc(starts_out, 16)
            sp.dma_start(dram["starts"][NT:NJ * P].unsqueeze(0), zero_i[:, NT:NJ * P]).then_inc(starts_out, 16)
            sp.wait_ge(starts_out, 32)
            sp.dma_start(keep["starts"][:], dram["starts"][0:NT].unsqueeze(0)).then_inc(starts_back, 16)
            sp.dma_start(row[:], dram["starts"][0:NT].unsqueeze(0)).then_inc(starts_back, 16)
            sp.dma_start(start_cols[:], dram["starts"].rearrange("(j p) -> p j", p=P),
                         allow_slow_non_contiguous=True).then_inc(starts_back, 16)
            sp.wait_ge(count_ready, 1)
            sp.dma_start(dram["cnt_f"].rearrange("(p c) -> p c", p=P), count_e[:]).then_inc(count_out, 16)
            sp.dma_start(dram["icnt_f"].rearrange("(p c) -> p c", p=P), count_inv[:]).then_inc(count_out, 16)
            for j in range(NJ):
                sp.wait_ge(radial_in[j], 16 * RAD)
                sp.dma_start(dram["radial"][j * P:(j + 1) * P, :, :], radial_rows[:, j, :, :]).then_inc(radial_out, 16)
            sp.wait_ge(radial_out, NJ * 16)
            sp.wait_ge(count_out, 2 * 16)
            sp.wait_ge(flat_out, 3 * 16)
            sp.wait_ge(kept_in, 14 * 16)

        @block.scalar
        def _(act):
            act.dma_start(dst_x[:], bass.AP(tensor=ins["dst_ext"].tensor, offset=0, ap=[[EC, P], [1, EC + 2]])).then_inc(edges_in, 16)
            act.dma_start(src_i[:], ins["src_flat"].rearrange("(p c) -> p c", p=P)).then_inc(edges_in, 16)
            act.dma_start(dist[:], ins["dist_flat"].rearrange("(p c) -> p c", p=P)).then_inc(edges_in, 16)
            act.dma_start(dst_e[:], ins["dst_by_tile"]).then_inc(edges_in, 16)
            chain = Chained(act, act_chain)
            act.wait_ge(wraps_ready, 1)
            act.wait_ge(consts_done, 1)
            chain(nc.scalar.activation(wraps[:], wraps[:], ACT.Sin, bias=half_pi[:], scale=-3.14159265358979))
            nc.scalar.activation(dist[:], wraps[:], ACT.Square).then_inc(cutoff_ready, 1)

        @block.gpsimd
        def _(pool):
            nc.gpsimd.iota(keep["iota"][:], pattern=[[1, TN]], base=0, channel_multiplier=0,
                           allow_small_or_imprecise_dtypes=True).then_inc(iotas_done, 1)
            nc.gpsimd.iota(keep["base"][:], pattern=[[TN, NT]], base=0, channel_multiplier=0,
                           allow_small_or_imprecise_dtypes=True).then_inc(iotas_done, 1)
            nc.gpsimd.iota(group_start[:], pattern=[[TN * TG, NG + 1]], base=0, channel_multiplier=0,
                           allow_small_or_imprecise_dtypes=True).then_inc(iotas_done, 1)
            nc.gpsimd.iota(tile_start[:], pattern=[[TN, TG + 1]], base=0, channel_multiplier=0,
                           allow_small_or_imprecise_dtypes=True).then_inc(iotas_done, 1)
            nc.gpsimd.iota(iota_g[:], pattern=[[1, NG]], base=0, channel_multiplier=0,
                           allow_small_or_imprecise_dtypes=True).then_inc(iotas_done, 1)
            nc.gpsimd.iota(part_g[:], pattern=[[0, 1]], base=0, channel_multiplier=1,
                           allow_small_or_imprecise_dtypes=True).then_inc(iotas_done, 1)
            nc.gpsimd.memset(ident[:], 0.0).then_inc(ident_zeroed, 1)
            pool.wait_ge(ident_zeroed, 1)
            nc.gpsimd.affine_select(out=ident[:], in_=ident[:], compare_op=ALU.not_equal, fill=1.0, base=0,
                                    pattern=[[-1, P]], channel_multiplier=1).then_inc(ident_ready, 1)
            pool.wait_ge(index_ready, 1)
            pool.wait_ge(flat_out, 3 * 16)
            for j in range(NJ):
                for k, name in enumerate(("dst_f", "src_f", "cut_f")):
                    pool.indirect_dma_start(
                        out=window_rows[:, k, j, :], out_offset=None, in_=dram[name].unsqueeze(1),
                        in_offset=bass.IndirectOffsetOnAxis(ap=start_cols[:, j:j + 1], axis=0)).then_inc(windows_in, 16)
            for j in range(NJ):
                for k in range(RAD):
                    pool.indirect_dma_start(
                        out=radial_rows[:, j, k, :], out_offset=None, in_=ins["radial_flat"].unsqueeze(1),
                        in_offset=bass.IndirectOffsetOnAxis(ap=keep["start_cols"][:, k, j:j + 1], axis=0),
                    ).then_inc(radial_in[j], 16)
            pool.wait_ge(count_out, 2 * 16)
            for j in range(NJ):
                pool.indirect_dma_start(
                    out=window_rows[:, 3, j, :], out_offset=None, in_=dram["cnt_f"].unsqueeze(1),
                    in_offset=bass.IndirectOffsetOnAxis(ap=start_cols[:, j:j + 1], axis=0)).then_inc(counts_in, 16)

        @block.vector
        def _(dve):
            chain = Chained(dve, dve_chain)
            nc.vector.memset(half_pi[:], 1.5707963267949).then_inc(consts_done, 1)
            chain(nc.vector.memset(keep["eps"][:], EPS))
            chain(nc.vector.memset(keep["ones"][:], 1.0))
            chain(nc.vector.memset(zero_i[:], 0))
            chain(nc.vector.memset(ones_e[:], 1.0))
            dve.wait_ge(edges_in, 4 * 16)
            nc.vector.tensor_copy(srcf[:], src_i[:]).then_inc(flat_ready, 1)
            nc.vector.tensor_scalar(keep["dst_e"][:], dst_e[:], float(N - 1), None, ALU.min).then_inc(flat_ready, 1)
            chain(nc.vector.tensor_scalar(rest[:], dist[:], 0.1, None, ALU.mult))
            chain(nc.vector.tensor_scalar(wraps[:], rest[:], 12582912.0, None, ALU.add))
            chain(nc.vector.tensor_scalar(wraps[:], wraps[:], 12582912.0, None, ALU.subtract))
            chain(nc.vector.tensor_tensor(wraps[:], rest[:], wraps[:], ALU.subtract))
            nc.vector.scalar_tensor_tensor(out=wraps[:], in0=wraps[:], scalar=-1.0, in1=wraps[:],
                                           op0=ALU.mult, op1=ALU.max).then_inc(wraps_ready, 1)
            dve.wait_ge(wraps_ready, 1)
            chain(nc.vector.tensor_copy(dstf[:], dst_x[:, 1:EC + 1]))
            dve.sem_inc(flat_ready, 1)
            dve.wait_ge(iotas_done, 6)
            chain(nc.vector.tensor_tensor(
                past_group[:], dstf[:].unsqueeze(2).broadcast_to([P, EC, NG + 1]),
                group_start[:].unsqueeze(1).broadcast_to([P, EC, NG + 1]), ALU.is_ge))
            chain(nc.vector.tensor_tensor(in_group[:], past_group[:, :, 0:NG], past_group[:, :, 1:NG + 1], ALU.subtract))
            chain(nc.vector.tensor_reduce(group_no[:], past_group[:, :, 1:NG + 1], AX_X, ALU.add))
            chain(nc.vector.scalar_tensor_tensor(rest[:], group_no[:], -float(TN * TG), dstf[:], ALU.mult, ALU.add))
            nc.vector.tensor_tensor(
                before_tile[:], rest[:].unsqueeze(2).broadcast_to([P, EC, TG + 1]),
                tile_start[:].unsqueeze(1).broadcast_to([P, EC, TG + 1]), ALU.is_lt).then_inc(onehots_ready, 1)
            chain(nc.vector.tensor_scalar(earlier[:], iota_g[:], part_g[:], None, ALU.is_gt))
            dve.wait_ge(weights_in, 6 * 16)
            chain(nc.vector.memset(hsel[:], 0.0))
            for c in range(KC):
                for g in range(P // HD):
                    h = c * (P // HD) + g
                    chain(nc.vector.memset(hsel[g * HD:(g + 1) * HD, c, h:h + 1], 1.0))
            for c in range(KC):
                nc.vector.tensor_scalar(ahead[:, c, :], hsel[:, c, :], asrc[:, c:c + 1], None, ALU.mult).then_inc(heads_ready, 1)
            dve.wait_ge(fold1, 1)
            chain(nc.vector.tensor_copy(keep["wc"][:], ps_fold[:, 0:KC * FILT].rearrange("p (c o) -> p c o", c=KC)))
            chain(nc.vector.tensor_copy(keep["w3"][:, :, D:HW], ps_fold[:, 128:128 + KC * H].rearrange("p (c o) -> p c o", c=KC)))
            chain(nc.vector.tensor_copy(keep["m2"][:], ps_fold2[0:FILT + 1, 0:D]))
            dve.wait_ge(counted, 1)
            nc.vector.tensor_copy(within[:], ps_cnt[0:NG, 0:TG + 1]).then_inc(within_ready, 1)
            dve.wait_ge(based, 1)
            dve.wait_ge(within_ready, 1)
            chain(nc.vector.tensor_scalar(starts[:], within[:, 0:TG], ps_base[0:NG, 0:1], None, ALU.add))
            nc.vector.tensor_copy(starts_i[:], starts[:]).then_inc(starts_ready, 1)
            dve.wait_ge(starts_back, 48)
            chain(nc.vector.tensor_copy(rowf[:], row[:]))
            chain(nc.vector.memset(cnt[:], 0.0))
            chain(nc.vector.tensor_tensor(cnt[:, 0:NT - 1], rowf[:, 1:NT], rowf[:, 0:NT - 1], ALU.subtract))
            chain(nc.vector.tensor_scalar(cnt_i[:], cnt[:], -1.0, 0.0, ALU.add, ALU.max))
            chain(nc.vector.tensor_scalar(over_i[:], cnt_i[:], 7, None, ALU.arith_shift_right))
            chain(nc.vector.tensor_copy(keep["over"][:, 0:NT], over_i[:]))
            chain(nc.vector.tensor_reduce(cnt[:, 0:1], over_i[:], AX_X, ALU.max))
            chain(nc.vector.tensor_copy(keep["over"][:, NT:NT + 1], cnt[:, 0:1]))
            for k in range(RAD):
                chain(nc.vector.tensor_scalar(keep["start_cols"][:, k, :], start_cols[:], float(k * EP), None, ALU.add))
            dve.sem_inc(index_ready, 1)

            def carried_scan(n, out, add, backward):
                flip = (lambda t: t[:, ::-1]) if backward else (lambda t: t[:, :])
                final = out[:, 0:1] if backward else out[:, EC - 1:EC]
                chain(nc.vector.tensor_tensor_scan(flip(out), flip(same), flip(add), 0.0, ALU.mult, ALU.add))
                chain(nc.vector.tensor_copy(piece_col[:, 0:1], final))
                nc.vector.tensor_reduce(piece_col[:, 1:2], same[:], AX_X, ALU.min).then_inc(piece_ready, 1)
                dve.wait_ge(piece_turned, n)
                chain(nc.vector.tensor_copy(piece_row[:], ps_base[0:1, 128:128 + 2 * P].rearrange("p (k c) -> p k c", k=2)))
                chain(nc.vector.tensor_tensor_scan(flip(piece_run), flip(piece_row[:, 1, :]), flip(piece_row[:, 0, :]), 0.0,
                                                   ALU.mult, ALU.add))
                chain(nc.vector.memset(carry_row[:], 0.0))
                to, of = ((carry_row[:, 0:P - 1], piece_run[:, 1:P]) if backward else
                          (carry_row[:, 1:P], piece_run[:, 0:P - 1]))
                nc.vector.tensor_copy(to, of).then_inc(carry_ready, 1)
                dve.wait_ge(carry_turned, n)
                chain(nc.vector.tensor_copy(carry_in[:], ps_base[:, 64:65]))
                chain(nc.vector.tensor_tensor_scan(flip(out), flip(same), flip(add), carry_in[:, 0:1], ALU.mult, ALU.add))

            chain(nc.vector.tensor_tensor(same[:], dst_x[:, 1:EC + 1], dst_x[:, 0:EC], ALU.is_equal))
            carried_scan(1, run, ones_e, backward=False)
            chain(nc.vector.tensor_tensor(same[:], dst_x[:, 1:EC + 1], dst_x[:, 2:EC + 2], ALU.is_equal))
            chain(nc.vector.tensor_tensor(rest[:], run[:], same[:], ALU.mult))
            chain(nc.vector.tensor_tensor(run[:], run[:], rest[:], ALU.subtract))
            carried_scan(2, count_e, run, backward=True)
            nc.vector.reciprocal(count_inv[:], count_e[:]).then_inc(count_ready, 1)
            for n, (j, k) in enumerate(turns):
                w = min(P, NT - j * P)
                at = slice(j * P, j * P + w)
                dve.wait_ge(turned, n + 1)
                if k == 0:
                    op = nc.vector.tensor_tensor(keep["drel"][:, at], ps_win[n % 2][:, 0:w], keep["base"][:, at], ALU.subtract)
                elif k == 3:
                    chain(nc.vector.tensor_copy(keep["cnt"][:, at], ps_win[n % 2][:, 0:w]))
                    op = nc.vector.reciprocal(keep["icnt"][:, at], keep["cnt"][:, at])
                else:
                    op = nc.vector.tensor_copy(keep["src" if k == 1 else "cut"][:, at], ps_win[n % 2][:, 0:w])
                op.then_inc(turned_used, 1)
            dve.wait_ge(turned_used, len(turns))

        @block.tensor
        def _(pe):
            pe.wait_ge(weights_in, 6 * 16)
            for c in range(KC):
                nc.tensor.matmul(ps_fold[:, c * FILT:(c + 1) * FILT], wn[:, c * P:(c + 1) * P], lin1t[:], start=True, stop=True)
            pe.wait_ge(heads_ready, KC)
            for c in range(KC):
                for o in range(KC):
                    nc.tensor.matmul(ps_fold[:, 128 + c * H:128 + (c + 1) * H], w3[:, o, c * P:(c + 1) * P], ahead[:, o, :],
                                     start=(o == 0), stop=(o == KC - 1))
            nc.tensor.matmul(ps_fold2[0:FILT + 1, 0:D], lin2b[:], mnt[:], start=True, stop=True).then_inc(fold1, 1)
            pe.wait_ge(onehots_ready, 1)
            for c in range(EC):
                last = nc.tensor.matmul(ps_cnt[0:NG, 0:TG + 1], in_group[:, c, :], before_tile[:, c, :],
                                        start=(c == 0), stop=(c == EC - 1))
            last.then_inc(counted, 1)
            pe.wait_ge(within_ready, 1)
            nc.tensor.matmul(ps_base[0:NG, 0:1], earlier[:], within[:, TG:TG + 1], start=True, stop=True).then_inc(based, 1)
            pe.wait_ge(ident_ready, 1)
            for n in range(1, 3):
                pe.wait_ge(piece_ready, n)
                for k in range(2):
                    last = nc.tensor.transpose(ps_base[0:1, 128 + k * P:128 + (k + 1) * P], piece_col[:, k:k + 1], ident[:])
                last.then_inc(piece_turned, 1)
                pe.wait_ge(carry_ready, n)
                nc.tensor.matmul(ps_base[:, 64:65], carry_row[:], keep["ones"][0:1, 0:1], start=True, stop=True).then_inc(
                    carry_turned, 1)
            for n, (j, k) in enumerate(turns):
                pe.wait_ge(windows_in if k < 3 else counts_in, 16 * NJ * (3 if k < 3 else 1))
                if n >= 2:
                    pe.wait_ge(turned_used, n - 1)
                nc.tensor.transpose(ps_win[n % 2][:, 0:W], window_rows[:, k, j, :], ident[:]).then_inc(turned, 1)


class Further:

    def __init__(self, eng, keep, name):
        self.eng, self.keep = eng, keep
        self.any_over = eng.value_load(keep["over"][0:1, NT:NT + 1], min_val=0, max_val=ET)
        self.done = eng.alloc_register(f"{name}_chunks_done")
        eng.reg_mov(self.done, 0)

    def chunks(self, tile, body):
        eng = self.eng
        with eng.If(self.any_over > 0):
            count = eng.value_load(self.keep["over"][0:1, bass.ds(tile.t, 1)], min_val=0, max_val=ET)
            with eng.If(count > 0):
                with eng.Fori(0, count) as k:
                    eng.reg_add(self.done, self.done, 1)
                    body(k, eng.snap(self.done, min_val=1, max_val=60000))


class WindowSweep:

    def __init__(self, nc, ctx, keep, dram, ins, name, table, width, values=(), columns=()):
        self.nc, self.keep, self.dram, self.ins = nc, keep, dram, ins
        self.table, self.width, self.values, self.columns = table, width, values, columns
        m = self.m = Memory(nc, ctx, name)
        self.index = m.sb("index", [P, 8], I32)
        self.rows = m.sb("rows", [P, 8, width])
        self.sel = m.sb("sel", [P, 8, TN])
        self.index_ready = m.sem("index_ready")
        self.gathered = m.sems("gathered", 8)
        self.sel_ready = m.sem("sel_ready")
        self.summed = m.sem("summed")
        self.x_src = m.sb("x_src", [P, 1], I32)
        self.x_dst = m.sb("x_dst", [P, 1])
        self.x_values = m.sb("x_values", [P, 2])
        self.x_rel = m.sb("x_rel", [P, 1])
        self.x_rows = m.sb("x_rows", [P, width])
        self.x_sel = m.sb("x_sel", [P, TN])
        self.x_cols = m.sb("x_cols", [16, W])
        self.x_loaded = m.sem("x_loaded")
        self.x_gathered = m.sem("x_gathered")
        self.x_rel_ready = m.sem("x_rel_ready")
        self.x_sel_ready = m.sem("x_sel_ready")
        self.x_summed = m.sem("x_summed")
        self.passed = m.sems("passed", 4)
        self.x_loads = 2 + len(values) + len(columns)
        self.w = m.sb("w", [TN, 8, D])
        self.stats = m.sb("stats", [TN, 8, 6])
        self.mv = m.sb("mv", [TN, 8, 2])
        self.sd = m.sb("sd", [TN, 8, 1])
        self.rstd = m.sb("rstd", [TN, 8, 1])
        self.shift = m.sb("shift", [TN, 8, 1])
        self.w_ready, self.stats_ready, self.mv_ready, self.sd_ready, self.rstd_ready, self.shift_ready = (
            m.sem(x) for x in ("w_ready", "stats_ready", "mv_ready", "sd_ready", "rstd_ready", "shift_ready"))

    def gather(self, pool, rows_free=None):
        further = Further(pool, self.keep, self.m.name)
        rows_free = rows_free or self.summed

        def stage(tile):
            slot, round_ = tile.ring(8)
            if slot % 4 == 0:
                if tile.from_(8):
                    pool.wait_ge(rows_free, tile.t - 4)
                self.nc.gpsimd.tensor_copy(self.index[:, slot:slot + 4], self.keep["src"][:, bass.ds(tile.t, 4)]).then_inc(
                    self.index_ready, 1)
                wait_apart(pool, self.index_ready, round_ * 2 + slot // 4 + 1, self.passed[1])
            pool.indirect_dma_start(
                out=self.rows[:, slot, :], out_offset=None, in_=self.table,
                in_offset=bass.IndirectOffsetOnAxis(ap=self.index[:, slot:slot + 1], axis=0)).then_inc(self.gathered[slot], 16)

            def chunk(k, n):
                wait_apart(pool, self.x_loaded, n * (16 * self.x_loads), self.passed[1])
                pool.indirect_dma_start(
                    out=self.x_rows[:], out_offset=None, in_=self.table,
                    in_offset=bass.IndirectOffsetOnAxis(ap=self.x_src[:, 0:1], axis=0)).then_inc(self.x_gathered, 16)

            further.chunks(tile, chunk)

        sweep(pool, NT, [(0, stage)])

    def load_chunks(self, sp, further, tile):
        def chunk(k, n):
            start = sp.value_load(self.keep["starts"][0:1, bass.ds(tile.t, 1)], min_val=0, max_val=N)
            at = self.nc.s_assert_within(start + k * W + W, 0, N)
            sp.dma_start(self.x_src[:], self.ins["src_flat"][bass.ds(at, W)].unsqueeze(1)).then_inc(self.x_loaded, 16)
            sp.dma_start(self.x_dst[:], self.dram["dst_f"][bass.ds(at, W)].unsqueeze(1)).then_inc(self.x_loaded, 16)
            for i, value in enumerate(self.values):
                sp.dma_start(self.x_values[:, i:i + 1], value[bass.ds(at, W)].unsqueeze(1)).then_inc(self.x_loaded, 16)
            for source, n_rows in self.columns:
                sp.dma_start(self.x_cols[0:n_rows, :], source[:, bass.ds(at, W)]).then_inc(self.x_loaded, 16)
            wait_apart(sp, self.x_summed, n, self.passed[2])

        further.chunks(tile, chunk)

    def select(self, dve, tile, scale=None):
        slot, _ = tile.ring(8)
        s2, op1 = (scale(slot, tile), ALU.mult) if scale else (None, ALU.bypass)
        self.nc.vector.tensor_scalar(self.sel[:, slot, :], self.keep["iota"][:], self.keep["drel"][:, bass.ds(tile.t, 1)],
                                     s2, ALU.is_equal, op1).then_inc(self.sel_ready, 1)

    def select_chunk(self, dve, tile, n, scale=None):
        dve.wait_ge(self.x_gathered, n * 16)
        self.nc.vector.tensor_tensor(self.x_rel[:], self.x_dst[:], self.keep["base"][:, bass.ds(tile.t, 1)],
                                     ALU.subtract).then_inc(self.x_rel_ready, 1)
        dve.wait_ge(self.x_rel_ready, n)
        s2, op1 = (scale, ALU.mult) if scale is not None else (None, ALU.bypass)
        self.nc.vector.tensor_scalar(self.x_sel[:], self.keep["iota"][:], self.x_rel[:, 0:1], s2,
                                     ALU.is_equal, op1).then_inc(self.x_sel_ready, 1)

    def row_stats(self, dve, tile):
        slot, _ = tile.ring(8)
        dve.wait_ge(self.w_ready, tile.t + 1)
        self.nc.vector.bn_stats(self.stats[:, slot, :], self.w[:, slot, :]).then_inc(self.stats_ready, 1)

    def moments(self, dve, tile):
        slot, _ = tile.ring(8)
        wait_apart(dve, self.stats_ready, tile.t + 1, self.passed[0])
        self.nc.vector.bn_aggr(self.mv[:, slot, :], self.stats[:, slot, :]).then_inc(self.mv_ready, 1)

    def deviation(self, act, tile):
        if tile.slot8 % 2:
            pair = slice(tile.slot8 - 1, tile.slot8 + 1)
            act.wait_ge(self.mv_ready, tile.t + 1)
            self.nc.scalar.activation(self.sd[:, pair, :], self.mv[:, pair, 1:2], ACT.Sqrt,
                                      bias=self.keep["eps"][0:TN, :]).then_inc(self.sd_ready, 2)

    def factor(self, dve, tile):
        if tile.slot8 % 2:
            pair = slice(tile.slot8 - 1, tile.slot8 + 1)
            dve.wait_ge(self.sd_ready, tile.t + 1)
            self.nc.vector.reciprocal(self.rstd[:, pair, :], self.sd[:, pair, :]).then_inc(self.rstd_ready, 2)

    def offset(self, dve, tile):
        if tile.slot8 % 2:
            pair = slice(tile.slot8 - 1, tile.slot8 + 1)
            dve.wait_ge(self.rstd_ready, tile.t + 1)
            self.nc.vector.scalar_tensor_tensor(out=self.shift[:, pair, :], in0=self.mv[:, pair, 0:1], scalar=-1.0,
                                                in1=self.rstd[:, pair, :], op0=ALU.mult, op1=ALU.mult).then_inc(self.shift_ready, 2)


def node_rows(table, tile, width=D, count=2):
    return table[bass.ds(tile.t * TN, count * TN), 0:width].rearrange("(k p) f -> p k f", p=TN)


def build_sage(nc, keep, dram, ins):
    with ExitStack() as ctx:
        s = WindowSweep(nc, ctx, keep, dram, ins, "sage", ins["x"], D, values=(dram["icnt_f"], dram["cnt_f"]))
        m = s.m
        x = m.sb("x", [TN, 8, D])
        xt = m.sb("xt", [P, 4, KC, 2 * TN])
        mean_t = m.sb("mean_t", [P, 8, KC * TN])
        hid_t = m.sb("hid_t", [P, 8, KC, TN])
        deg_root = m.sb("deg_root", [TN, 8, 1])
        dinv = m.sb("dinv", [TN, 8, 1])
        y = m.sb("y", [TN, 8, D])
        out = m.sb("out", [TN, 8, DW])
        sum_ps = [m.ps(f"sum_ps{i}", [P, 512]) for i in range(2)]
        hid_ps = [m.ps(f"hid_ps{i}", [P, 512]) for i in range(2)]
        out_ps = [m.ps(f"out_ps{i}", [P, 512]) for i in range(4)]
        loaded, stored = m.sems("loaded", 4), m.sems("stored", 4)
        mean_ready, inverted, dinv_ready, hid_summed, hid_ready, out_summed, y_ready, out_ready = (
            m.sem(n) for n in ("mean_ready", "inverted", "dinv_ready", "hid_summed", "hid_ready", "out_summed", "y_ready", "out_ready"))
        CNT = KC * TN
        block = m.block()

        @block.gpsimd
        def _(pool):
            s.gather(pool)

        @block.sync
        def _(sp):
            further = Further(sp, keep, s.m.name)

            def load(tile):
                if tile.slot8 % 2:
                    return
                pair = tile.slot8 // 2
                if tile.from_(8):
                    sp.wait_ge(s.w_ready, tile.t - 6)
                sp.dma_start(x[:, 2 * pair:2 * pair + 2, :], node_rows(ins["x"], tile)).then_inc(loaded[pair], 16)
                sp.dma_start(xt[:, pair, :, :], ins["xt"][:, bass.ds(tile.t * TN, 2 * TN)].rearrange(
                    "(c p) n -> p c n", p=P)).then_inc(loaded[pair], 16)

            def store(tile):
                if tile.slot8 % 2:
                    return
                slot, _ = tile.ring(8)
                sp.wait_ge(out_ready, tile.t + 2)
                sp.dma_start(node_rows(dram["x1"], tile, DW), out[:, slot:slot + 2, :]).then_inc(stored[slot // 2], 16)

            sweep(sp, NT, [(0, load), (0, lambda tile: s.load_chunks(sp, further, tile)), (12, store)])
            for q in stored:
                sp.wait_ge(q, 16 * (NT // 8))

        @block.vector
        def _(dve):
            further = Further(dve, keep, s.m.name)

            def select(tile):
                s.select(dve, tile, scale=lambda slot, tile_: keep["icnt"][:, bass.ds(tile_.t, 1)])
                further.chunks(tile, lambda k, n: s.select_chunk(dve, tile, n, scale=s.x_values[:, 0:1]))

            def skip(tile):
                slot, _ = tile.ring(8)
                dve.wait_ge(out_summed, tile.t + 1)
                nc.vector.tensor_tensor(y[:, slot, :], out_ps[slot % 4][0:TN, 0:D], x[:, slot, :], ALU.add).then_inc(y_ready, 1)

            def residual(tile):
                slot, _ = tile.ring(8)
                dve.wait_ge(y_ready, tile.t + 1)
                if tile.from_(8):
                    dve.wait_ge(out_ready, tile.t - 7)
                nc.vector.scalar_tensor_tensor(out=s.w[:, slot, :], in0=y[:, slot, :], scalar=0.0, in1=x[:, slot, :],
                                               op0=ALU.max, op1=ALU.add).then_inc(s.w_ready, 1)

            def degrees(tile):
                if tile.slot8 % 2:
                    pair = slice(tile.slot8 - 1, tile.slot8 + 1)
                    dve.wait_ge(mean_ready, tile.t + 1)
                    nc.vector.reciprocal(dinv[:, pair, :], deg_root[:, pair, :]).then_inc(inverted, 2)

            def place_degrees(tile):
                if tile.slot8 % 2:
                    pair = slice(tile.slot8 - 1, tile.slot8 + 1)
                    if tile.from_(8):
                        dve.wait_ge(stored[tile.slot8 // 2], tile.round8 * 16)
                    dve.wait_ge(inverted, tile.t + 1)
                    nc.vector.tensor_copy(out[:, pair, D:DW], dinv[:, pair, :]).then_inc(dinv_ready, 2)

            sweep(dve, NT, [(9, lambda tile: s.factor(dve, tile)), (7, lambda tile: s.row_stats(dve, tile)), (6, skip),
                            (9, place_degrees), (4, degrees), (0, select), (7, lambda tile: s.moments(dve, tile)), (6, residual),
                            (9, lambda tile: s.offset(dve, tile))])

        @block.scalar
        def _(act):
            def means(tile):
                slot, _ = tile.ring(8)
                ps = sum_ps[slot % 2]
                act.wait_ge(s.summed, tile.t + 1)
                nc.scalar.activation(deg_root[:, slot, :], ps[0:TN, CNT:CNT + 1], ACT.Sqrt, bias=keep["ones"][0:TN, 0:1])
                nc.scalar.copy(mean_t[:, slot, :], ps[:, 0:CNT]).then_inc(mean_ready, 1)

            def hidden(tile):
                slot, _ = tile.ring(8)
                act.wait_ge(hid_summed, tile.t + 1)
                for o in range(KC):
                    last = nc.scalar.activation(hid_t[:, slot, o, :], hid_ps[slot % 2][:, o * TN:(o + 1) * TN], ACT.Relu,
                                                bias=keep["bl"][:, o:o + 1])
                last.then_inc(hid_ready, 1)

            def normal(tile):
                slot, round8 = tile.ring(8)
                act.wait_ge(s.shift_ready, tile.t + 1)
                if tile.from_(8):
                    act.wait_ge(stored[slot // 2], round8 * 16)
                nc.scalar.activation(out[:, slot, 0:D], s.w[:, slot, :], ACT.Identity, bias=s.shift[:, slot, :],
                                     scale=s.rstd[:, slot, :]).then_inc(out_ready, 1)

            sweep(act, NT, [(2, means), (4, hidden), (8, lambda tile: s.deviation(act, tile)), (11, normal)])

        @block.tensor
        def _(pe):
            further = Further(pe, keep, s.m.name)

            def sums(tile):
                slot, round8 = tile.ring(8)
                ps = sum_ps[slot % 2]
                pe.wait_ge(s.sel_ready, tile.t + 1)
                pe.wait_ge(s.gathered[slot], (round8 + 1) * 16)

                def add(rows, sel, count, part, start=False):
                    if part < KC:
                        return nc.tensor.matmul(ps[:, part * TN:(part + 1) * TN], rows[:, part * P:(part + 1) * P], sel,
                                                start=start, stop=True, skip_group_check=True)
                    return nc.tensor.matmul(ps[0:TN, CNT:CNT + 1], sel, count, start=False, stop=True, skip_group_check=True)

                window = (s.rows[:, slot, :], s.sel[:, slot, :], keep["cnt"][:, bass.ds(tile.t, 1)])
                add(*window, 0, start=True)

                def chunk(k, n):
                    pe.wait_ge(s.x_sel_ready, n)
                    for part in range(KC + 1):
                        last = add(s.x_rows[:], s.x_sel[:], s.x_values[:, 1:2], part)
                    last.then_inc(s.x_summed, 1)

                further.chunks(tile, chunk)
                for part in range(1, KC + 1):
                    last = add(*window, part)
                last.then_inc(s.summed, 1)

            def hidden(tile):
                slot8, round8 = tile.ring(8)
                pair, half = slot8 // 2, slot8 % 2
                ps = hid_ps[slot8 % 2]
                if half == 0:
                    pe.wait_ge(loaded[pair], (round8 + 1) * 32)
                for o in range(KC):
                    at = slice(o * TN, (o + 1) * TN)
                    for c in range(KC):
                        nc.tensor.matmul(ps[:, at], keep["wr"][:, c, o * P:(o + 1) * P], xt[:, pair, c, half * TN:(half + 1) * TN],
                                         start=(o == 0 and c == 0), stop=True, skip_group_check=True)
                pe.wait_ge(mean_ready, tile.t + 1)
                for o in range(KC):
                    at = slice(o * TN, (o + 1) * TN)
                    for c in range(KC):
                        last = nc.tensor.matmul(ps[:, at], keep["wl"][:, c, o * P:(o + 1) * P], mean_t[:, slot8, c * TN:(c + 1) * TN],
                                                start=False, stop=True, skip_group_check=True)
                last.then_inc(hid_summed, 1)

            def output(tile):
                slot, _ = tile.ring(8)
                pe.wait_ge(hid_ready, tile.t + 1)
                if tile.from_(4):
                    pe.wait_ge(y_ready, tile.t - 3)
                for c in range(KC):
                    last = nc.tensor.matmul(out_ps[slot % 4][0:TN, 0:D], hid_t[:, slot, c, :], keep["wln"][:, c, :],
                                            start=(c == 0), stop=(c == KC - 1))
                last.then_inc(out_summed, 1)

            sweep(pe, NT, [(5, output), (3, hidden), (1, sums)])


class Projection:

    def __init__(self, s, matrix, width, proj_banks):
        self.s, self.nc, self.matrix, self.width = s, s.nc, matrix, width
        m = s.m
        self.out = m.sb("out", [TN, 8, D])
        self.turned = m.sb("turned", [P, 8, KC * TN])
        self.proj = m.sb("proj", [TN, 8, width])
        self.turn_ps = [m.ps(f"turn_ps{i}", [P, 512]) for i in range(2)]
        self.proj_ps = [m.ps(f"proj_ps{i}", [P, 512]) for i in range(proj_banks)]
        self.out_ready, self.turn_done, self.turned_ready, self.proj_done, self.proj_ready = (
            m.sem(n) for n in ("out_ready", "turn_done", "turned_ready", "proj_done", "proj_ready"))
        self.stored, self.proj_stored = m.sems("stored", 4), m.sems("proj_stored", 4)
        self.proj_stores = 1

    def normal(self, act, tile):
        s = self.s
        slot, round8 = tile.ring(8)
        act.wait_ge(s.shift_ready, tile.t + 1)
        if tile.from_(8):
            act.wait_ge(self.stored[slot // 2], round8 * 16)
        self.nc.scalar.activation(self.out[:, slot, :], s.w[:, slot, :], ACT.Identity, bias=s.shift[:, slot, :],
                                  scale=s.rstd[:, slot, :]).then_inc(self.out_ready, 1)

    def turn(self, pe, tile):
        slot, _ = tile.ring(8)
        pe.wait_ge(self.out_ready, tile.t + 1)
        if tile.from_(2):
            pe.wait_ge(self.turned_ready, tile.t - 1)
        for c in range(KC):
            last = self.nc.tensor.transpose(self.turn_ps[slot % 2][:, c * TN:(c + 1) * TN],
                                            self.out[:, slot, c * P:(c + 1) * P], self.s.keep["ident"][0:TN, 0:TN])
        last.then_inc(self.turn_done, 1)

    def copy_turned(self, act, tile):
        slot, _ = tile.ring(8)
        act.wait_ge(self.turn_done, tile.t + 1)
        if tile.from_(8):
            act.wait_ge(self.proj_done, tile.t - 7)
        self.nc.scalar.copy(self.turned[:, slot, :], self.turn_ps[slot % 2][:, 0:KC * TN]).then_inc(self.turned_ready, 1)

    def project(self, pe, tile):
        slot, _ = tile.ring(8)
        banks = len(self.proj_ps)
        pe.wait_ge(self.turned_ready, tile.t + 1)
        if tile.from_(banks):
            pe.wait_ge(self.proj_ready, tile.t + 1 - banks)
        for c in range(KC):
            last = self.nc.tensor.matmul(self.proj_ps[slot % len(self.proj_ps)][0:TN, 0:self.width],
                                         self.turned[:, slot, c * TN:(c + 1) * TN], self.matrix[:, c, :],
                                         start=(c == 0), stop=(c == KC - 1))
        last.then_inc(self.proj_done, 1)

    def copy_projected(self, dve, tile):
        slot, round8 = tile.ring(8)
        dve.wait_ge(self.proj_done, tile.t + 1)
        if tile.from_(8):
            dve.wait_ge(self.proj_stored[slot // 2], round8 * 16 * self.proj_stores)
        self.nc.vector.tensor_copy(self.proj[:, slot, :], self.proj_ps[slot % len(self.proj_ps)][0:TN, 0:self.width]).then_inc(
            self.proj_ready, 1)

    def store(self, sp, tile, rows_table, *proj_tables):
        if tile.slot8 % 2:
            return
        slot, _ = tile.ring(8)
        sp.wait_ge(self.out_ready, tile.t + 2)
        sp.dma_start(node_rows(rows_table, tile), self.out[:, slot:slot + 2, :]).then_inc(self.stored[slot // 2], 16)
        sp.wait_ge(self.proj_ready, tile.t + 2)
        for table, a, b in proj_tables:
            sp.dma_start(node_rows(table, tile, b - a), self.proj[:, slot:slot + 2, a:b]).then_inc(
                self.proj_stored[slot // 2], 16)

    def stores_done(self, sp):
        for q in range(4):
            sp.wait_ge(self.stored[q], 16 * (NT // 8))
            sp.wait_ge(self.proj_stored[q], 16 * self.proj_stores * (NT // 8))


class GcnFront:

    def __init__(self, s, weight):
        self.s, self.nc, self.weight = s, s.nc, weight
        m = s.m
        self.own = m.sb("own", [TN, 8, DW])
        self.diag = m.sb("diag", [TN, 8, TN])
        self.sum_t = m.sb("sum_t", [P, 8, KC * TN])
        self.sum_ps = [m.ps(f"sum_ps{i}", [P, 512]) for i in range(2)]
        self.conv_ps = [m.ps(f"conv_ps{i}", [P, 512]) for i in range(2)]
        self.own_loaded = m.sems("own_loaded", 4)
        self.own_loads = 1
        self.diag_ready, self.sum_ready, self.conv_done, self.conv_used = (
            m.sem(n) for n in ("diag_ready", "sum_ready", "conv_done", "conv_used"))

    def select(self, dve, tile, further):
        s = self.s
        slot, round8 = tile.ring(8)
        dve.wait_ge(s.gathered[slot], (round8 + 1) * 16)
        s.select(dve, tile, scale=lambda slot, _: s.rows[:, slot, D:DW])
        further.chunks(tile, lambda k, n: s.select_chunk(dve, tile, n, scale=s.x_rows[:, D:DW]))

    def diagonal(self, act, tile):
        slot, round8 = tile.ring(8)
        if slot % 2 == 0:
            act.wait_ge(self.own_loaded[slot // 2], (round8 + 1) * self.own_loads * 16)
        self.nc.scalar.activation(self.diag[:, slot, :], self.s.keep["ident"][0:TN, 0:TN], ACT.Identity,
                                  scale=self.own[:, slot, D:DW]).then_inc(self.diag_ready, 1)

    def sums(self, pe, tile, further):
        s = self.s
        slot, _ = tile.ring(8)
        ps = self.sum_ps[slot % 2]

        def add(rows, sel, c, start=False):
            return self.nc.tensor.matmul(ps[:, c * TN:(c + 1) * TN], rows[:, c * P:(c + 1) * P], sel, start=start, stop=True,
                                         skip_group_check=True)

        pe.wait_ge(self.diag_ready, tile.t + 1)
        for c in range(KC):
            add(self.own[:, slot, :], self.diag[:, slot, :], c, start=(c == 0))
        pe.wait_ge(s.sel_ready, tile.t + 1)
        add(s.rows[:, slot, :], s.sel[:, slot, :], 0)

        def chunk(k, n):
            pe.wait_ge(s.x_sel_ready, n)
            for c in range(KC):
                last = add(s.x_rows[:], s.x_sel[:], c)
            last.then_inc(s.x_summed, 1)

        further.chunks(tile, chunk)
        add(s.rows[:, slot, :], s.sel[:, slot, :], 1).then_inc(s.summed, 1)

    def copy_sum(self, act, tile):
        slot, _ = tile.ring(8)
        act.wait_ge(self.s.summed, tile.t + 1)
        self.nc.scalar.copy(self.sum_t[:, slot, :], self.sum_ps[slot % 2][:, 0:KC * TN]).then_inc(self.sum_ready, 1)

    def convolve(self, pe, tile):
        slot, _ = tile.ring(8)
        pe.wait_ge(self.sum_ready, tile.t + 1)
        if tile.from_(2):
            pe.wait_ge(self.conv_used, tile.t - 1)
        for c in range(KC):
            last = self.nc.tensor.matmul(self.conv_ps[slot % 2][0:TN, 0:D], self.sum_t[:, slot, c * TN:(c + 1) * TN],
                                         self.weight[:, c, :], start=(c == 0), stop=(c == KC - 1))
        last.then_inc(self.conv_done, 1)


def build_gcn_first(nc, keep, dram, ins):
    with ExitStack() as ctx:
        s = WindowSweep(nc, ctx, keep, dram, ins, "gcn1", dram["x1"], DW)
        g = GcnFront(s, keep["w1"])
        m = s.m
        z = m.sb("z", [TN, 8, D])
        squares = m.sb("squares", [TN, 8, 1])
        length = m.sb("length", [TN, 8, 1])
        inverse = m.sb("inverse", [TN, 8, 1])
        out = m.sb("out", [TN, 8, DW])
        stored = m.sems("stored", 4)
        squares_ready, length_ready, clamped, inverse_ready, dinv_ready, out_ready = (
            m.sem(n) for n in ("squares_ready", "length_ready", "clamped", "inverse_ready", "dinv_ready", "out_ready"))
        block = m.block()

        @block.gpsimd
        def _(pool):
            s.gather(pool)

        @block.sync
        def _(sp):
            further = Further(sp, keep, s.m.name)

            def load(tile):
                if tile.slot8 % 2:
                    return
                slot, _ = tile.ring(8)
                if tile.from_(8):
                    sp.wait_ge(dinv_ready, tile.t - 6)
                sp.dma_start(g.own[:, slot:slot + 2, :], node_rows(dram["x1"], tile, DW)).then_inc(g.own_loaded[slot // 2], 16)

            def store(tile):
                if tile.slot8 % 2:
                    return
                slot, _ = tile.ring(8)
                sp.wait_ge(out_ready, tile.t + 2)
                sp.dma_start(node_rows(dram["z1"], tile, DW), out[:, slot:slot + 2, :]).then_inc(stored[slot // 2], 16)

            sweep(sp, NT, [(0, load), (0, lambda tile: s.load_chunks(sp, further, tile)), (10, store)])
            for q in stored:
                sp.wait_ge(q, 16 * (NT // 8))

        @block.vector
        def _(dve):
            further = Further(dve, keep, s.m.name)

            def scale_and_bias(tile):
                slot, _ = tile.ring(8)
                dve.wait_ge(g.conv_done, tile.t + 1)
                if tile.from_(8):
                    dve.wait_ge(out_ready, tile.t - 7)
                nc.vector.scalar_tensor_tensor(out=z[:, slot, :], in0=g.conv_ps[slot % 2][0:TN, 0:D], scalar=g.own[:, slot, D:DW],
                                               in1=keep["b1"][0:TN, :], op0=ALU.mult, op1=ALU.add).then_inc(g.conv_used, 1)

            def place_degrees(tile):
                if tile.slot8 % 2:
                    pair = slice(tile.slot8 - 1, tile.slot8 + 1)
                    if tile.from_(8):
                        dve.wait_ge(stored[tile.slot8 // 2], tile.round8 * 16)
                    nc.vector.tensor_copy(out[:, pair, D:DW], g.own[:, pair, D:DW]).then_inc(dinv_ready, 2)

            def clamp(tile):
                if tile.slot8 % 2:
                    pair = slice(tile.slot8 - 1, tile.slot8 + 1)
                    dve.wait_ge(length_ready, tile.t + 1)
                    nc.vector.tensor_scalar(length[:, pair, :], length[:, pair, :], 1e-12, None, ALU.max).then_inc(clamped, 2)

            def invert(tile):
                if tile.slot8 % 2:
                    pair = slice(tile.slot8 - 1, tile.slot8 + 1)
                    dve.wait_ge(clamped, tile.t + 1)
                    nc.vector.reciprocal(inverse[:, pair, :], length[:, pair, :]).then_inc(inverse_ready, 2)

            sweep(dve, NT, [(7, clamp), (4, scale_and_bias), (0, lambda tile: g.select(dve, tile, further)), (4, place_degrees),
                            (7, invert)])

        @block.scalar
        def _(act):
            def square(tile):
                slot, round8 = tile.ring(8)
                act.wait_ge(g.conv_used, tile.t + 1)
                if tile.from_(8):
                    act.wait_ge(stored[slot // 2], round8 * 16)
                nc.scalar.activation(out[:, slot, 0:D], z[:, slot, :], ACT.Square, accum_out=squares[:, slot, :]).then_inc(squares_ready, 1)

            def lengths(tile):
                if tile.slot8 % 2:
                    pair = slice(tile.slot8 - 1, tile.slot8 + 1)
                    act.wait_ge(squares_ready, tile.t + 1)
                    nc.scalar.activation(length[:, pair, :], squares[:, pair, :], ACT.Sqrt).then_inc(length_ready, 2)

            def unit(tile):
                slot, _ = tile.ring(8)
                act.wait_ge(inverse_ready, tile.t + 1)
                nc.scalar.activation(out[:, slot, 0:D], z[:, slot, :], ACT.Identity, scale=inverse[:, slot, :]).then_inc(out_ready, 1)

            sweep(act, NT, [(2, lambda tile: g.copy_sum(act, tile)), (6, lengths), (0, lambda tile: g.diagonal(act, tile)),
                            (5, square), (9, unit)])

        @block.tensor
        def _(pe):
            further = Further(pe, keep, s.m.name)
            sweep(pe, NT, [(3, lambda tile: g.convolve(pe, tile)), (1, lambda tile: g.sums(pe, tile, further))])


def build_gcn_second(nc, keep, dram, ins):
    with ExitStack() as ctx:
        s = WindowSweep(nc, ctx, keep, dram, ins, "gcn2", dram["z1"], DW)
        g = GcnFront(s, keep["w2"])
        p = Projection(s, keep["wc"], FILT, 2)
        m = s.m
        x1 = m.sb("x1", [TN, 8, D])
        v = m.sb("v", [TN, 8, D])
        g.own_loads = 2
        block = m.block()

        @block.gpsimd
        def _(pool):
            s.gather(pool)

        @block.sync
        def _(sp):
            further = Further(sp, keep, s.m.name)

            def load(tile):
                if tile.slot8 % 2:
                    return
                slot, _ = tile.ring(8)
                if tile.from_(8):
                    sp.wait_ge(s.w_ready, tile.t - 6)
                sp.dma_start(g.own[:, slot:slot + 2, :], node_rows(dram["z1"], tile, DW)).then_inc(g.own_loaded[slot // 2], 16)
                sp.dma_start(x1[:, slot:slot + 2, :], node_rows(dram["x1"], tile)).then_inc(g.own_loaded[slot // 2], 16)

            sweep(sp, NT, [(0, load), (0, lambda tile: s.load_chunks(sp, further, tile)),
                           (14, lambda tile: p.store(sp, tile, dram["x2"], (dram["h2"], 0, FILT)))])
            p.stores_done(sp)

        @block.vector
        def _(dve):
            further = Further(dve, keep, s.m.name)

            def scale_and_bias(tile):
                slot, _ = tile.ring(8)
                dve.wait_ge(g.conv_done, tile.t + 1)
                nc.vector.scalar_tensor_tensor(out=v[:, slot, :], in0=g.conv_ps[slot % 2][0:TN, 0:D], scalar=g.own[:, slot, D:DW],
                                               in1=keep["b2"][0:TN, :], op0=ALU.mult, op1=ALU.add).then_inc(g.conv_used, 1)

            def residual(tile):
                slot, _ = tile.ring(8)
                dve.wait_ge(g.conv_used, tile.t + 1)
                if tile.from_(8):
                    dve.wait_ge(p.out_ready, tile.t - 7)
                nc.vector.scalar_tensor_tensor(out=s.w[:, slot, :], in0=x1[:, slot, :], scalar=2.0, in1=v[:, slot, :],
                                               op0=ALU.mult, op1=ALU.add).then_inc(s.w_ready, 1)

            sweep(dve, NT, [(7, lambda tile: s.factor(dve, tile)), (5, lambda tile: s.row_stats(dve, tile)), (4, scale_and_bias),
                            (13, lambda tile: p.copy_projected(dve, tile)), (0, lambda tile: g.select(dve, tile, further)),
                            (5, lambda tile: s.moments(dve, tile)), (4, residual), (7, lambda tile: s.offset(dve, tile))])

        @block.scalar
        def _(act):
            sweep(act, NT, [(2, lambda tile: g.copy_sum(act, tile)), (0, lambda tile: g.diagonal(act, tile)),
                            (11, lambda tile: p.copy_turned(act, tile)), (6, lambda tile: s.deviation(act, tile)),
                            (9, lambda tile: p.normal(act, tile))])

        @block.tensor
        def _(pe):
            further = Further(pe, keep, s.m.name)
            sweep(pe, NT, [(12, lambda tile: p.project(pe, tile)), (10, lambda tile: p.turn(pe, tile)),
                           (3, lambda tile: g.convolve(pe, tile)), (1, lambda tile: g.sums(pe, tile, further))])


def build_filter(nc, keep, dram, ins):
    with ExitStack() as ctx:
        s = WindowSweep(nc, ctx, keep, dram, ins, "filter", dram["h2"], FILT, values=(dram["cut_f"],),
                        columns=((ins["radial_flat"].rearrange("(r e) -> r e", r=RAD), RAD),))
        p = Projection(s, keep["w3"], HW, 1)
        p.proj_stores = 2
        m = s.m
        x2 = m.sb("x2", [TN, 8, D])
        radial = m.sb("radial", [RAD, 8, W])
        message = m.sb("message", [P, 8, FILT])
        x_message = m.sb("x_message", [P, FILT])
        agg_t = m.sb("agg_t", [FILT + 1, 8, TN])
        radial_ps = m.ps("radial_ps", [P, 8, FILT])
        agg_ps = [m.ps(f"agg_ps{i}", [P, 512]) for i in range(2)]
        out_ps = [m.ps(f"out_ps{i}", [P, 512]) for i in range(2)]
        loaded = m.sems("loaded", 4)
        ones_ready, radial_done, message_ready, x_radial_done, x_message_ready, agg_ready, out_done = (
            m.sem(n) for n in ("ones_ready", "radial_done", "message_ready", "x_radial_done", "x_message_ready", "agg_ready",
                               "out_done"))
        block = m.block()

        @block.gpsimd
        def _(pool):
            s.gather(pool, rows_free=message_ready)

        @block.sync
        def _(sp):
            further = Further(sp, keep, s.m.name)

            def load(tile):
                if tile.slot8 % 2:
                    return
                slot, _ = tile.ring(8)
                if tile.from_(8):
                    sp.wait_ge(s.w_ready, tile.t - 6)
                sp.dma_start(x2[:, slot:slot + 2, :], node_rows(dram["x2"], tile)).then_inc(loaded[slot // 2], 16)
                sp.dma_start(radial[:, slot:slot + 2, :], dram["radial"][bass.ds(tile.t, 2), :, :].rearrange(
                    "k r e -> r k e")).then_inc(loaded[slot // 2], 16)

            sweep(sp, NT, [(0, load), (1, lambda tile: s.load_chunks(sp, further, tile)),
                           (16, lambda tile: p.store(sp, tile, dram["x3"], (dram["h3"], 0, HW), (dram["a_src"], D, HW)))])
            p.stores_done(sp)

        @block.vector
        def _(dve):
            further = Further(dve, keep, s.m.name)
            nc.vector.memset(agg_t[FILT:FILT + 1, :, :], 1.0).then_inc(ones_ready, 1)

            def messages(tile):
                slot, round8 = tile.ring(8)
                dve.wait_ge(s.gathered[slot], (round8 + 1) * 16)
                dve.wait_ge(radial_done, tile.t + 1)
                nc.vector.tensor_tensor(message[:, slot, :], s.rows[:, slot, :], radial_ps[:, 0, :], ALU.mult).then_inc(
                    message_ready, 1)
                s.select(dve, tile, scale=lambda slot_, tile_: keep["cut"][:, bass.ds(tile_.t, 1)])

                def chunk(k, n):
                    dve.wait_ge(x_radial_done, n)
                    dve.wait_ge(s.x_gathered, n * 16)
                    nc.vector.tensor_tensor(x_message[:], s.x_rows[:], radial_ps[:, 1, :], ALU.mult).then_inc(x_message_ready, 1)
                    s.select_chunk(dve, tile, n, scale=s.x_values[:, 0:1])

                further.chunks(tile, chunk)

            def residual(tile):
                slot, _ = tile.ring(8)
                dve.wait_ge(out_done, tile.t + 1)
                if tile.from_(8):
                    dve.wait_ge(p.out_ready, tile.t - 7)
                nc.vector.tensor_tensor(s.w[:, slot, :], out_ps[slot % 2][0:TN, 0:D], x2[:, slot, :], ALU.add).then_inc(s.w_ready, 1)

            sweep(dve, NT, [(8, lambda tile: s.factor(dve, tile)), (6, lambda tile: s.row_stats(dve, tile)), (5, residual),
                            (13, lambda tile: p.copy_projected(dve, tile)), (1, messages),
                            (6, lambda tile: s.moments(dve, tile)), (8, lambda tile: s.offset(dve, tile))])

        @block.scalar
        def _(act):
            def copy_sum(tile):
                slot, _ = tile.ring(8)
                act.wait_ge(s.summed, tile.t + 1)
                nc.scalar.copy(agg_t[0:FILT, slot, :], agg_ps[slot % 2][0:FILT, 0:TN]).then_inc(agg_ready, 1)

            sweep(act, NT, [(3, copy_sum), (12, lambda tile: p.copy_turned(act, tile)), (7, lambda tile: s.deviation(act, tile)),
                            (10, lambda tile: p.normal(act, tile))])

        @block.tensor
        def _(pe):
            further = Further(pe, keep, s.m.name)
            pe.wait_ge(ones_ready, 1)

            def filters(tile):
                slot, round8 = tile.ring(8)
                if slot % 2 == 0:
                    pe.wait_ge(loaded[slot // 2], (round8 + 1) * 32)
                if tile.from_(1):
                    pe.wait_ge(message_ready, tile.t)
                nc.tensor.matmul(radial_ps[:, 0, :], radial[:, slot, :], keep["wrad"][:], start=True, stop=True).then_inc(radial_done, 1)

            def sums(tile):
                slot, _ = tile.ring(8)
                pe.wait_ge(message_ready, tile.t + 1)
                pe.wait_ge(s.sel_ready, tile.t + 1)
                ps = agg_ps[slot % 2][0:FILT, :]
                half = TN // 2

                def add(msg, sel, a, b, start=False):
                    return nc.tensor.matmul(ps[:, a:b], msg, sel[:, a:b], start=start, stop=True, skip_group_check=True)

                add(message[:, slot, :], s.sel[:, slot, :], 0, half, start=True)

                def chunk(k, n):
                    pe.wait_ge(s.x_loaded, n * (16 * s.x_loads))
                    nc.tensor.matmul(radial_ps[:, 1, :], s.x_cols[0:RAD, :], keep["wrad"][:], start=True, stop=True).then_inc(
                        x_radial_done, 1)
                    pe.wait_ge(s.x_sel_ready, n)
                    pe.wait_ge(x_message_ready, n)
                    add(x_message[:], s.x_sel[:], 0, TN).then_inc(s.x_summed, 1)

                further.chunks(tile, chunk)
                add(message[:, slot, :], s.sel[:, slot, :], half, TN).then_inc(s.summed, 1)

            def output(tile):
                slot, _ = tile.ring(8)
                pe.wait_ge(agg_ready, tile.t + 1)
                if tile.from_(2):
                    pe.wait_ge(s.w_ready, tile.t - 1)
                nc.tensor.matmul(out_ps[slot % 2][0:TN, 0:D], agg_t[:, slot, :], keep["m2"][:], start=True, stop=True).then_inc(out_done, 1)

            sweep(pe, NT, [(13, lambda tile: p.project(pe, tile)), (11, lambda tile: p.turn(pe, tile)), (4, output), (2, sums),
                           (0, filters)])


def build_scores(nc, keep, dram, ins):
    with ExitStack() as ctx:
        m = Memory(nc, ctx, "score")
        index = m.sb("index", [P, 2, 8], I32)
        rows = m.sb("rows", [P, 8, HW])
        src_score = m.sb("src_score", [P, 8, H])
        attr = m.sb("attr", [4, 8, W])
        factor = m.sb("factor", [P, 8, D])
        prod = m.sb("prod", [P, 8, D])
        dot = m.sb("dot", [P, 8, H])
        total = m.sb("total", [P, 8, H])
        leaky = m.sb("leaky", [P, 8, H])
        alpha_t = m.sb("alpha_t", [H, 8, W])
        enc_ps = [m.ps(f"enc_ps{i}", [P, 512]) for i in range(2)]
        alpha_ps = [m.ps(f"alpha_ps{i}", [P, 512]) for i in range(2)]
        index_ready, passed = m.sem("index_ready"), m.sem("passed")
        gathered, loaded, stored = m.sems("gathered", 8), m.sems("loaded", 4), m.sems("stored", 4)
        enc_done, factor_ready, prod_ready, dot_ready, total_ready, leaky_ready, turned, alpha_ready = (
            m.sem(n) for n in ("enc_done", "factor_ready", "prod_ready", "dot_ready", "total_ready", "leaky_ready", "turned",
                               "alpha_ready"))
        block = m.block()

        @block.gpsimd
        def _(pool):
            def gather(tile):
                slot, round_ = tile.ring(8)
                if slot % 4 == 0:
                    if tile.from_(8):
                        pool.wait_ge(total_ready, tile.t - 4)
                    for k, name in enumerate(("dst_e", "src_e")):
                        last = nc.gpsimd.tensor_copy(index[:, k, slot:slot + 4], keep[name][:, bass.ds(tile.t, 4)])
                    last.then_inc(index_ready, 1)
                    wait_apart(pool, index_ready, round_ * 2 + slot // 4 + 1, passed)
                pool.indirect_dma_start(out=rows[:, slot, :], out_offset=None, in_=dram["h3"],
                                        in_offset=bass.IndirectOffsetOnAxis(ap=index[:, 0, slot:slot + 1], axis=0)).then_inc(gathered[slot], 16)
                pool.indirect_dma_start(out=src_score[:, slot, :], out_offset=None, in_=dram["a_src"],
                                        in_offset=bass.IndirectOffsetOnAxis(ap=index[:, 1, slot:slot + 1], axis=0)).then_inc(gathered[slot], 16)

            sweep(pool, ET, [(0, gather)])

        @block.sync
        def _(sp):
            def load(tile):
                if tile.slot8 % 2:
                    return
                slot, _ = tile.ring(8)
                if tile.from_(8):
                    sp.wait_ge(enc_done, tile.t - 6)
                sp.dma_start(attr[:, slot:slot + 2, :], ins["attr3t"][:, bass.ds(tile.t * W, 2 * W)].rearrange(
                    "r (k e) -> r k e", k=2)).then_inc(loaded[slot // 2], 16)

            def store(tile):
                if tile.slot8 % 2:
                    return
                slot, _ = tile.ring(8)
                sp.wait_ge(alpha_ready, tile.t + 2)
                sp.dma_start(dram["alpha"][:, bass.ds(tile.t * W, 2 * W)].rearrange("h (k e) -> h k e", k=2),
                             alpha_t[:, slot:slot + 2, :]).then_inc(stored[slot // 2], 16)

            sweep(sp, ET, [(0, load), (8, store)])
            for q in stored:
                sp.wait_ge(q, 16 * (ET // 8))

        @block.tensor
        def _(pe):
            def encode(tile):
                slot, round8 = tile.ring(8)
                if slot % 2 == 0:
                    pe.wait_ge(loaded[slot // 2], (round8 + 1) * 16)
                if tile.from_(2):
                    pe.wait_ge(factor_ready, tile.t - 1)
                nc.tensor.matmul(enc_ps[slot % 2][:, 0:D], attr[:, slot, :], keep["wedge"][:], start=True, stop=True).then_inc(enc_done, 1)

            def turn(tile):
                slot, _ = tile.ring(8)
                pe.wait_ge(leaky_ready, tile.t + 1)
                if tile.from_(2):
                    pe.wait_ge(alpha_ready, tile.t - 1)
                nc.tensor.transpose(alpha_ps[slot % 2][0:H, 0:W], leaky[:, slot, :], keep["ident"][:]).then_inc(turned, 1)

            sweep(pe, ET, [(0, encode), (5, turn)])

        @block.vector
        def _(dve):
            def factors(tile):
                slot, _ = tile.ring(8)
                dve.wait_ge(enc_done, tile.t + 1)
                nc.vector.scalar_tensor_tensor(out=factor[:, slot, :], in0=enc_ps[slot % 2][:, 0:D], scalar=0.0, in1=keep["adst"][:],
                                               op0=ALU.max, op1=ALU.add).then_inc(factor_ready, 1)

            def products(tile):
                slot, round8 = tile.ring(8)
                dve.wait_ge(gathered[slot], (round8 + 1) * 32)
                dve.wait_ge(factor_ready, tile.t + 1)
                nc.vector.tensor_tensor(prod[:, slot, :], factor[:, slot, :], rows[:, slot, 0:D], ALU.mult).then_inc(prod_ready, 1)

            def dots(tile):
                slot, _ = tile.ring(8)
                dve.wait_ge(prod_ready, tile.t + 1)
                nc.vector.tensor_reduce(dot[:, slot, :], prod[:, slot, :].rearrange("p (h d) -> p h d", h=H), AX_X, ALU.add).then_inc(dot_ready, 1)

            def totals(tile):
                slot, _ = tile.ring(8)
                dve.wait_ge(dot_ready, tile.t + 1)
                nc.vector.tensor_tensor(total[:, slot, :], dot[:, slot, :], src_score[:, slot, :], ALU.add).then_inc(total_ready, 1)

            def slopes(tile):
                slot, _ = tile.ring(8)
                dve.wait_ge(total_ready, tile.t + 1)
                if tile.from_(8):
                    dve.wait_ge(turned, tile.t - 7)
                nc.vector.scalar_tensor_tensor(out=leaky[:, slot, :], in0=total[:, slot, :], scalar=0.2, in1=total[:, slot, :],
                                               op0=ALU.mult, op1=ALU.max).then_inc(leaky_ready, 1)

            sweep(dve, ET, [(1, factors), (4, slopes), (2, products), (3, totals), (2, dots)])

        @block.scalar
        def _(act):
            def copy_alpha(tile):
                slot, round8 = tile.ring(8)
                act.wait_ge(turned, tile.t + 1)
                if tile.from_(8):
                    act.wait_ge(stored[slot // 2], round8 * 16)
                nc.scalar.copy(alpha_t[:, slot, :], alpha_ps[slot % 2][0:H, 0:W]).then_inc(alpha_ready, 1)

            sweep(act, ET, [(6, copy_alpha)])


def build_softmax(nc, keep, dram, ins):
    with ExitStack() as ctx:
        m = Memory(nc, ctx, "softmax")
        alpha = m.sb("alpha", [P, SQ])
        dst = m.sb("dst", [P, SQ + 2], I32)
        start = m.sb("start", [P, SQ])
        inside = m.sb("inside", [P, SQ])
        reset = m.sb("reset", [P, SQ])
        end = m.sb("end", [P, SQ])
        before_end = m.sb("before_end", [P, SQ])
        run = m.sb("run", [P, SQ])
        last = m.sb("last", [P, SQ])
        seg = m.sb("seg", [P, SQ])
        col = m.sb("col", [P, 5])
        flags = m.sb("flags", [H, 2, SEG])
        no_start, no_end, start_reset = m.sb("no_start", [H, SEG]), m.sb("no_end", [H, SEG]), m.sb("start_reset", [H, SEG])
        piece = m.sb("piece", [H, SEG])
        piece_sum = m.sb("piece_sum", [H, SEG])
        carry = m.sb("carry", [H, SEG])
        carry_in = m.sb("carry_in", [P, 1])
        windows = m.sb("windows", [P, NJ, H, W])
        loaded, chain_sem, exp_ready, shifted = m.sem("loaded"), m.sem("chain"), m.sem("exp_ready"), m.sem("shifted")
        flags_ready, flags_out, flags_back = m.sem("flags_ready"), m.sem("flags_out"), m.sem("flags_back")
        outcome_ready, outcome_out, outcome_back = m.sem("outcome_ready"), m.sem("outcome_out"), m.sem("outcome_back")
        carry_ready, carry_out, carry_back = m.sem("carry_ready"), m.sem("carry_out"), m.sem("carry_back")
        attn_ready, attn_out = m.sem("attn_ready"), m.sem("attn_out")
        window_in, window_out = m.sems("window_in", NJ), m.sem("window_out")
        flat = lambda t: t.rearrange("h (s q) -> (h s) q", s=SEG)
        SCANS = 4
        block = m.block()

        @block.sync
        def _(sp):
            sp.dma_start(alpha[:], flat(dram["alpha"])).then_inc(loaded, 16)
            for h in range(H):
                sp.dma_start(dst[h * SEG:(h + 1) * SEG, :], bass.AP(tensor=ins["dst_ext"].tensor, offset=0,
                             ap=[[SQ, SEG], [1, SQ + 2]])).then_inc(loaded, 16)
            carry_d = dram["carry"]
            sp.wait_ge(flags_ready, 1)
            for k in range(2):
                sp.dma_start(carry_d[k].unsqueeze(1), col[:, k:k + 1]).then_inc(flags_out, 16)
            sp.wait_ge(flags_out, 32)
            for k in range(2):
                sp.dma_start(flags[:, k, :], carry_d[k].rearrange("(h s) -> h s", h=H)).then_inc(flags_back, 16)
            for n in range(SCANS):
                sp.wait_ge(outcome_ready, n + 1)
                sp.dma_start(carry_d[2].unsqueeze(1), col[:, 2:3]).then_inc(outcome_out, 16)
                sp.wait_ge(outcome_out, 16 * (n + 1))
                sp.dma_start(piece[:], carry_d[2].rearrange("(h s) -> h s", h=H)).then_inc(outcome_back, 16)
                sp.wait_ge(carry_ready, n + 1)
                sp.dma_start(carry_d[3].rearrange("(h s) -> h s", h=H), carry[:]).then_inc(carry_out, 16)
                sp.wait_ge(carry_out, 16 * (n + 1))
                sp.dma_start(carry_in[:], carry_d[3].unsqueeze(1)).then_inc(carry_back, 16)
            sp.wait_ge(attn_ready, 1)
            sp.dma_start(flat(dram["attn"]), seg[:]).then_inc(attn_out, 16)
            for j in range(NJ):
                sp.wait_ge(window_in[j], 16 * H)
                sp.dma_start(dram["attn_windows"][j * P:(j + 1) * P, :, :], windows[:, j, :, :]).then_inc(window_out, 16)
            sp.wait_ge(window_out, 16 * NJ)

        @block.gpsimd
        def _(pool):
            pool.wait_ge(attn_out, 16)
            attn = dram["attn"].rearrange("h e -> (h e)").unsqueeze(1)
            for j in range(NJ):
                for h in range(H):
                    pool.indirect_dma_start(out=windows[:, j, h, :], out_offset=None, in_=attn,
                                            in_offset=bass.IndirectOffsetOnAxis(ap=keep["start_cols"][:, h, j:j + 1], axis=0),
                                            ).then_inc(window_in[j], 16)

        @block.scalar
        def _(act):
            act.wait_ge(shifted, 1)
            nc.scalar.activation(alpha[:], alpha[:], ACT.Exp).then_inc(exp_ready, 1)

        @block.vector
        def _(dve):
            chain = Chained(dve, chain_sem)
            dve.wait_ge(loaded, 16 * (H + 1))
            chain(nc.vector.tensor_tensor(start[:], dst[:, 1:SQ + 1], dst[:, 0:SQ], ALU.not_equal))
            chain(nc.vector.tensor_tensor(end[:], dst[:, 1:SQ + 1], dst[:, 2:SQ + 2], ALU.not_equal))
            chain(nc.vector.tensor_scalar(inside[:], start[:], -1.0, 1.0, ALU.mult, ALU.add))
            chain(nc.vector.tensor_scalar(reset[:], start[:], -BIG, None, ALU.mult))
            chain(nc.vector.tensor_scalar(before_end[:], end[:], -1.0, 1.0, ALU.mult, ALU.add))
            chain(nc.vector.tensor_reduce(col[:, 0:1], start[:], AX_X, ALU.max))
            chain(nc.vector.tensor_reduce(col[:, 1:2], end[:], AX_X, ALU.max))
            dve.sem_inc(flags_ready, 1)
            dve.wait_ge(flags_back, 32)
            chain(nc.vector.tensor_scalar(no_start[:], flags[:, 0, :], -1.0, 1.0, ALU.mult, ALU.add))
            chain(nc.vector.tensor_scalar(no_end[:], flags[:, 1, :], -1.0, 1.0, ALU.mult, ALU.add))
            chain(nc.vector.tensor_scalar(start_reset[:], flags[:, 0, :], -BIG, None, ALU.mult))
            scans = [0]

            def carried_scan(out, keep_, add, ops, piece_keep, empty, backward=False):
                flip = (lambda t: t[:, ::-1]) if backward else (lambda t: t[:, :])
                final = out[:, 0:1] if backward else out[:, SQ - 1:SQ]
                n = scans[0] = scans[0] + 1
                chain(nc.vector.tensor_tensor_scan(flip(out), flip(keep_), flip(add), empty, ops[0], ops[1]))
                chain(nc.vector.tensor_copy(col[:, 2:3], final))
                dve.sem_inc(outcome_ready, 1)
                dve.wait_ge(outcome_back, 16 * n)
                chain(nc.vector.tensor_tensor_scan(flip(piece_sum), flip(piece_keep), flip(piece), empty, ops[0], ops[1]))
                chain(nc.vector.memset(carry[:], empty))
                to, of = (carry[:, 0:SEG - 1], piece_sum[:, 1:SEG]) if backward else (carry[:, 1:SEG], piece_sum[:, 0:SEG - 1])
                chain(nc.vector.tensor_copy(to, of))
                dve.sem_inc(carry_ready, 1)
                dve.wait_ge(carry_back, 16 * n)
                chain(nc.vector.tensor_tensor_scan(flip(out), flip(keep_), flip(add), carry_in[:, 0:1], ops[0], ops[1]))

            def spread_last(out, value):
                chain(nc.vector.tensor_tensor(last[:], value[:], end[:], ALU.mult))
                carried_scan(out, before_end, last, (ALU.mult, ALU.add), no_end, 0.0, backward=True)

            carried_scan(run, reset, alpha, (ALU.add, ALU.max), start_reset, -BIG)
            spread_last(seg, run)
            nc.vector.tensor_tensor(alpha[:], alpha[:], seg[:], ALU.subtract).then_inc(shifted, 1)
            dve.wait_ge(exp_ready, 1)
            carried_scan(run, inside, alpha, (ALU.mult, ALU.add), no_start, 0.0)
            spread_last(seg, run)
            chain(nc.vector.tensor_scalar(seg[:], seg[:], 1e-10, None, ALU.max))
            chain(nc.vector.reciprocal(seg[:], seg[:]))
            nc.vector.tensor_tensor(seg[:], seg[:], alpha[:], ALU.mult).then_inc(attn_ready, 1)


def build_gat(nc, keep, dram, ins, out):
    with ExitStack() as ctx:
        s = WindowSweep(nc, ctx, keep, dram, ins, "gat", dram["h3"], HW, columns=((dram["attn"], H),))
        m = s.m
        x3 = m.sb("x3", [TN, 8, D])
        attn = m.sb("attn", [H, 8, W])
        message = m.sb("message", [P, 8, D])
        x_message = m.sb("x_message", [P, D])
        normed = m.sb("normed", [TN, 8, D])
        attn_ps = [m.ps(f"attn_ps{i}", [P, 512]) for i in range(2)]
        x_attn_ps = m.ps("x_attn_ps", [P, 512])
        sum_ps = [m.ps(f"sum_ps{i}", [P, 512]) for i in range(2)]
        loaded, stored = m.sems("loaded", 4), m.sems("stored", 4)
        turned, message_ready, x_turned, x_message_ready, out_ready = (
            m.sem(n) for n in ("turned", "message_ready", "x_turned", "x_message_ready", "out_ready"))
        block = m.block()

        @block.gpsimd
        def _(pool):
            s.gather(pool, rows_free=message_ready)

        @block.sync
        def _(sp):
            further = Further(sp, keep, s.m.name)

            def load(tile):
                if tile.slot8 % 2:
                    return
                slot, _ = tile.ring(8)
                if tile.from_(8):
                    sp.wait_ge(s.w_ready, tile.t - 6)
                sp.dma_start(x3[:, slot:slot + 2, :], node_rows(dram["x3"], tile)).then_inc(loaded[slot // 2], 16)
                sp.dma_start(attn[:, slot:slot + 2, :], dram["attn_windows"][bass.ds(tile.t, 2), :, :].rearrange(
                    "k h e -> h k e")).then_inc(loaded[slot // 2], 16)

            def store(tile):
                if tile.slot8 % 2:
                    return
                slot, _ = tile.ring(8)
                sp.wait_ge(out_ready, tile.t + 2)
                sp.dma_start(node_rows(out, tile), normed[:, slot:slot + 2, :]).then_inc(stored[slot // 2], 16)

            sweep(sp, NT, [(0, load), (1, lambda tile: s.load_chunks(sp, further, tile)), (10, store)])
            for q in stored:
                sp.wait_ge(q, 16 * (NT // 8))

        @block.vector
        def _(dve):
            further = Further(dve, keep, s.m.name)
            heads = lambda rows: rows[:, 0:D].rearrange("p (h d) -> p h d", h=H)
            weights = lambda ps: ps[:, 0:H].unsqueeze(2).broadcast_to([P, H, HD])

            def messages(tile):
                slot, round8 = tile.ring(8)
                dve.wait_ge(s.gathered[slot], (round8 + 1) * 16)
                dve.wait_ge(turned, tile.t + 1)
                nc.vector.tensor_tensor(heads(message[:, slot, :]), heads(s.rows[:, slot, :]), weights(attn_ps[slot % 2]),
                                        ALU.mult).then_inc(message_ready, 1)
                s.select(dve, tile)

                def chunk(k, n):
                    dve.wait_ge(x_turned, n)
                    dve.wait_ge(s.x_gathered, n * 16)
                    nc.vector.tensor_tensor(heads(x_message[:]), heads(s.x_rows[:]), weights(x_attn_ps), ALU.mult).then_inc(x_message_ready, 1)
                    s.select_chunk(dve, tile, n)

                further.chunks(tile, chunk)

            def residual(tile):
                slot, _ = tile.ring(8)
                dve.wait_ge(s.summed, tile.t + 1)
                if tile.from_(8):
                    dve.wait_ge(out_ready, tile.t - 7)
                nc.vector.tensor_tensor(s.w[:, slot, :], sum_ps[slot % 2][0:TN, 0:D], x3[:, slot, :], ALU.add).then_inc(s.w_ready, 1)

            sweep(dve, NT, [(6, lambda tile: s.factor(dve, tile)), (4, lambda tile: s.row_stats(dve, tile)), (3, residual),
                            (1, messages), (4, lambda tile: s.moments(dve, tile)), (6, lambda tile: s.offset(dve, tile))])

        @block.scalar
        def _(act):
            def normal(tile):
                slot, round8 = tile.ring(8)
                act.wait_ge(s.shift_ready, tile.t + 1)
                if tile.from_(8):
                    act.wait_ge(stored[slot // 2], round8 * 16)
                nc.scalar.activation(normed[:, slot, :], s.w[:, slot, :], ACT.Identity, bias=s.shift[:, slot, :],
                                     scale=s.rstd[:, slot, :]).then_inc(out_ready, 1)

            sweep(act, NT, [(5, lambda tile: s.deviation(act, tile)), (8, normal)])

        @block.tensor
        def _(pe):
            further = Further(pe, keep, s.m.name)

            def turn(tile):
                slot, round8 = tile.ring(8)
                if slot % 2 == 0:
                    wait_apart(pe, loaded[slot // 2], (round8 + 1) * 32, s.passed[3])
                nc.tensor.transpose(attn_ps[slot % 2][:, 0:H], attn[:, slot, :], keep["ident"][0:H, 0:H]).then_inc(turned, 1)

            def sums(tile):
                slot, _ = tile.ring(8)
                ps = sum_ps[slot % 2][0:TN, 0:D]
                if tile.from_(2):
                    wait_apart(pe, s.w_ready, tile.t - 1, s.passed[3])
                nc.tensor.matmul(ps, keep["ones"][0:1, 0:TN], keep["bias3"][:], start=True, stop=True, skip_group_check=True)

                def chunk(k, n):
                    wait_apart(pe, s.x_loaded, n * (16 * s.x_loads), s.passed[3])
                    nc.tensor.transpose(x_attn_ps[:, 0:H], s.x_cols[0:H, :], keep["ident"][0:H, 0:H]).then_inc(x_turned, 1)
                    pe.wait_ge(s.x_sel_ready, n)
                    pe.wait_ge(x_message_ready, n)
                    nc.tensor.matmul(ps, s.x_sel[:], x_message[:], start=False, stop=True, skip_group_check=True).then_inc(s.x_summed, 1)

                further.chunks(tile, chunk)
                pe.wait_ge(message_ready, tile.t + 1)
                pe.wait_ge(s.sel_ready, tile.t + 1)
                nc.tensor.matmul(ps, s.sel[:, slot, :], message[:, slot, :], start=False, stop=True, skip_group_check=True).then_inc(
                    s.summed, 1)

            sweep(pe, NT, [(2, sums), (0, turn)])


def build(nc, ins, out, last="gat"):
    def scratch(name, shape):
        return nc.dram_tensor(name, shape, F32, kind="Internal").ap()

    dram = {
        "dst_f": scratch("dst_f", [EP]), "src_f": scratch("src_f", [EP]), "cut_f": scratch("cut_f", [EP]),
        "cnt_f": scratch("cnt_f", [EP]), "icnt_f": scratch("icnt_f", [EP]),
        "starts": nc.dram_tensor("tile_starts", [NJ * P], I32, kind="Internal").ap(),
        "radial": scratch("radial_windows", [NJ * P, RAD, W]),
        "x1": scratch("x1", [NP, DW]), "z1": scratch("z1", [NP, DW]), "x2": scratch("x2", [NP, D]),
        "h2": scratch("h2", [NP, FILT]), "x3": scratch("x3", [NP, D]), "h3": scratch("h3", [NP, HW]),
        "a_src": scratch("a_src_h", [NP, H]), "alpha": scratch("alpha", [H, EP]), "attn": scratch("attn", [H, EP]),
        "attn_windows": scratch("attn_windows", [NJ * P, H, W]), "carry": scratch("carry", [4, P]),
    }
    with ExitStack() as ctx:
        m = Memory(nc, ctx, "keep")
        keep = {
            "wl": m.sb("wl", [P, KC, D]), "wr": m.sb("wr", [P, KC, D]), "wln": m.sb("wln", [P, KC, D]),
            "w1": m.sb("w1", [P, KC, D]), "w2": m.sb("w2", [P, KC, D]), "w3": m.sb("w3", [P, KC, HW]),
            "bl": m.sb("bl", [P, KC]), "wrad": m.sb("wrad", [RAD, FILT]), "wedge": m.sb("wedge", [4, D]),
            "b1": m.sb("b1", [P, D]), "b2": m.sb("b2", [P, D]), "bias3": m.sb("bias3", [1, D]), "adst": m.sb("adst", [P, D]),
            "wc": m.sb("wc", [P, KC, FILT]), "m2": m.sb("m2", [FILT + 1, D]),
            "ident": m.sb("ident", [P, P]), "ones": m.sb("ones", [P, P]), "eps": m.sb("eps", [P, 1]),
            "iota": m.sb("iota", [P, TN]), "base": m.sb("base", [P, NT]),
            "src_e": m.sb("src_e", [P, ET], I32), "dst_e": m.sb("dst_e", [P, ET], I32),
            "src": m.sb("src", [P, NT], I32), "drel": m.sb("drel", [P, NT]), "cut": m.sb("cut", [P, NT]),
            "cnt": m.sb("cnt", [P, NT]), "icnt": m.sb("icnt", [P, NT]),
            "starts": m.sb("starts", [1, NT], I32), "over": m.sb("over", [1, NT + 1], I32),
            "start_cols": m.sb("start_cols", [P, RAD, NJ], I32),
        }
        build_setup(nc, keep, dram, ins)
        build_sage(nc, keep, dram, ins)
        if last == "sage":
            return
        build_gcn_first(nc, keep, dram, ins)
        if last == "gcn1":
            return
        build_gcn_second(nc, keep, dram, ins)
        if last == "gcn2":
            return
        build_filter(nc, keep, dram, ins)
        if last == "filter":
            return
        build_scores(nc, keep, dram, ins)
        build_softmax(nc, keep, dram, ins)
        if last == "softmax":
            return
        build_gat(nc, keep, dram, ins, out)


def layouts(inputs):
    import numpy as np

    a = {k: np.asarray(v) for k, v in inputs.items()}
    rows = lambda v, n: np.concatenate([v, np.zeros((n - v.shape[0],) + v.shape[1:], v.dtype)])
    x = rows(a["x"], NP)
    src, dst = rows(a["src"], EP), np.concatenate([a["dst"], np.full(EP - E, PAD_DST, a["dst"].dtype)])
    attr3 = np.concatenate([rows(a["edge_attr_3"], EP), np.ones((EP, 1), a["edge_attr_3"].dtype)], axis=1)
    radial = np.ascontiguousarray(rows(a["edge_attr_12"], EP).T)
    column = lambda v: np.ascontiguousarray(v.reshape(KC, P).T)
    t = lambda name: np.ascontiguousarray(a[name].T)
    return {
        "x": x, "xt": np.ascontiguousarray(x.T), "src_flat": src,
        "dst_ext": np.concatenate([np.full(1, -1, dst.dtype), dst, np.full(1, -1, dst.dtype)]),
        "src_by_tile": np.ascontiguousarray(src.reshape(ET, W).T), "dst_by_tile": np.ascontiguousarray(dst.reshape(ET, W).T),
        "dist_flat": rows(a["edge_weight"], EP), "radial_flat": radial.reshape(-1),
        "attr3t": np.ascontiguousarray(attr3.T),
        "L0_wlt": t("L0_gnn_W_l"), "L0_wrt": t("L0_gnn_W_r"), "L0_wlnt": t("L0_gnn_W_ln"), "L0_bl": column(a["L0_gnn_b_l"]),
        "L1_w1": a["L1_gnn_W1"], "L1_w2": a["L1_gnn_W2"], "L1_b1": a["L1_gnn_b1"], "L1_b2": a["L1_gnn_b2"],
        "L2_wn": a["L2_gnn_W_node_to_message"], "L2_wradt": t("L2_gnn_W_radial_to_message"), "L2_lin1t": t("L2_gnn_W_lin1"),
        "L2_lin2b": np.concatenate([a["L2_gnn_W_lin2"], a["L2_gnn_b_lin2"][:, None]], axis=1),
        "L2_mnt": t("L2_gnn_W_message_to_node"),
        "L3_wt": t("L3_gnn_W"), "L3_w": a["L3_gnn_W"], "L3_asrc": column(a["L3_gnn_a_src"].reshape(-1)),
        "L3_adst": a["L3_gnn_a_dst"].reshape(-1), "L3_bias": a["L3_gnn_bias"],
        "L3_wedge": np.concatenate([t("L3_gnn_edge_W"), a["L3_gnn_edge_b"][None]], axis=0),
    }


def kernel(**inputs):
    import numpy as np
    import concourse.bacc as bacc
    from concourse.bass_utils import run_bass_kernel_spmd

    nc = bacc.Bacc("TRN2", target_bir_lowering=False, num_devices=1)
    arrays = layouts(inputs)
    ins = {k: nc.dram_tensor(f"in_{k}", v.shape, mybir.dt.from_np(v.dtype), kind="ExternalInput").ap() for k, v in arrays.items()}
    out = nc.dram_tensor("out", (NP, D), F32, kind="ExternalOutput").ap()
    build(nc, ins, out)
    r = run_bass_kernel_spmd(nc, [{f"in_{k}": v for k, v in arrays.items()}], core_ids=[0])
    return r.results[0]["out"][:N]
```

```python
from contextlib import ExitStack

import concourse.bass as bass
from concourse import mybir

F32 = mybir.dt.float32
I32 = mybir.dt.int32
BF16 = mybir.dt.bfloat16
ALU = mybir.AluOpType
ACT = mybir.ActivationFunctionType
AX_X = mybir.AxisListType.X

N = 50000
E = 50000
D = 256
P = 128
KC = D // P
TN = 96
UNROLL = 8
NT = -(-N // (TN * UNROLL)) * UNROLL
NP = NT * TN
W = 128
ET = -(-(E + W) // (W * UNROLL)) * UNROLL
EP = ET * W
EC = EP // P
PAD_DST = 60000
H, HD = 8, 32
FILT = 64
RAD = 12
HW = D + H
DW = D + 1
TG = 24
NG = NT // TG
NJ = -(-NT // P)
SEG = P // H
SQ = EP // SEG
BIG = 1e30
EPS = 1e-5

assert NG * TG == NT and NT * TN >= N and EC * P == EP and PAD_DST >= NP


class Tile:

    def __init__(self, round8, slot8):
        self.round8, self.slot8 = round8, slot8
        self.t = round8 * 8 + slot8
        self.peeled = isinstance(round8, int)

    def from_(self, n):
        return not self.peeled or self.t >= n

    def ring(self, n):
        return self.slot8 % n, self.round8 * (8 // n) + self.slot8 // n


def sweep(eng, count, stages, further=None):
    if further:
        for further.wanted in (True, False):
            with eng.If(further.any_over > 0 if further.wanted else further.any_over < 1):
                sweep(eng, count, stages)
        return

    def step(round8, slot8, only=lambda t: True):
        for lag, stage in stages:
            tile = Tile(round8 + (slot8 - lag) // 8, (slot8 - lag) % 8)
            if not tile.peeled or only(tile.t):
                stage(tile)

    longest = max(lag for lag, _ in stages)
    first = 1 + -(-longest // UNROLL)
    for r in range(first):
        for s in range(UNROLL):
            step(r, s, lambda t: t >= 0)
    with eng.Fori(first, count // UNROLL) as r:
        for s in range(UNROLL):
            step(r, s)
    for s in range(longest):
        step(count // UNROLL, s, lambda t: t < count)


class Memory:

    def __init__(self, nc, ctx, name):
        self.nc, self.ctx, self.name, self.semaphores = nc, ctx, name, []

    def sb(self, name, shape, dt=F32):
        return self.ctx.enter_context(self.nc.sbuf_tensor(f"{self.name}_{name}", shape, dt))

    def ps(self, name, shape):
        return self.ctx.enter_context(self.nc.psum_tensor(f"{self.name}_{name}", shape, F32))

    def sem(self, name):
        self.semaphores.append(self.nc.alloc_semaphore(f"{self.name}_{name}"))
        return self.semaphores[-1]

    def sems(self, name, n):
        return [self.sem(f"{name}{i}") for i in range(n)]

    def block(self):
        self.ctx.callback(self.free_semaphores)
        return self.ctx.enter_context(self.nc.Block())

    def free_semaphores(self):
        self.nc.clear_and_free_semaphores(self.semaphores)
        self.nc.all_engine_barrier()


def wait_apart(eng, sem, value, passed):
    eng.wait_ge(sem, value)
    eng.sem_inc(passed, 1)


class Chained:

    def __init__(self, eng, sem):
        self.eng, self.sem, self.n = eng, sem, 0

    def __call__(self, instruction, by=1):
        instruction.then_inc(self.sem, by)
        self.n += by
        self.eng.wait_ge(self.sem, self.n)


def build_setup(nc, keep, dram, ins):
    with ExitStack() as ctx:
        m = Memory(nc, ctx, "setup")
        wn = m.sb("wn", [FILT, D])
        lin1t = m.sb("lin1t", [FILT, FILT])
        lin2b = m.sb("lin2b", [FILT, FILT + 1])
        mnt = m.sb("mnt", [FILT, D])
        w3 = m.sb("w3", [P, KC, D])
        asrc = m.sb("asrc", [P, KC])
        hsel = m.sb("hsel", [P, KC, H])
        ahead = m.sb("ahead", [P, KC, H])
        dst_x = m.sb("dst_x", [P, EC + 2], I32)
        src_i = m.sb("src_i", [P, EC], I32)
        dist = m.sb("dist", [P, EC])
        dstf = m.sb("dstf", [P, EC])
        srcf = m.sb("srcf", [P, EC])
        wraps = m.sb("wraps", [P, EC])
        half_pi = m.sb("half_pi", [P, 1])
        bias = m.sb("bias", [3, D])
        part_b = m.sb("part_b", [3, D], BF16)
        part_f = m.sb("part_f", [3, D])
        bias_rest = m.sb("bias_rest", [3, D])
        bias_rows = m.sb("bias_rows", [3, D])
        ones_e = m.sb("ones_e", [P, EC])
        same = m.sb("same", [P, EC])
        run = m.sb("run", [P, EC])
        count_e = m.sb("count_e", [P, EC])
        count_inv = m.sb("count_inv", [P, EC])
        piece_col = m.sb("piece_col", [P, 2])
        piece_row = m.sb("piece_row", [1, 2, P])
        piece_run = m.sb("piece_run", [1, P])
        carry_row = m.sb("carry_row", [1, P])
        carry_in = m.sb("carry_in", [P, 1])
        dst_e = m.sb("dst_e", [P, ET], I32)
        group_start = m.sb("group_start", [P, NG + 1])
        tile_start = m.sb("tile_start", [P, TG + 1])
        past_group = m.sb("past_group", [P, EC, NG + 1], BF16)
        in_group = m.sb("in_group", [P, EC, NG], BF16)
        group_no = m.sb("group_no", [P, EC])
        rest = m.sb("rest", [P, EC])
        before_tile = m.sb("before_tile", [P, EC, TG + 1], BF16)
        radial_rows = m.sb("radial_rows", [P, NJ, RAD, W])
        iota_g = m.sb("iota_g", [NG, NG])
        part_g = m.sb("part_g", [NG, 1])
        earlier = m.sb("earlier", [NG, NG])
        within = m.sb("within", [NG, TG + 1])
        starts = m.sb("starts", [NG, TG])
        starts_i = m.sb("starts_i", [NG, TG], I32)
        zero_i = m.sb("zero_i", [1, NJ * P], I32)
        row = m.sb("row", [1, NT], I32)
        rowf = m.sb("rowf", [1, NT])
        cnt = m.sb("cnt", [1, NT])
        cnt_i = m.sb("cnt_i", [1, NT], I32)
        over_i = m.sb("over_i", [1, NT], I32)
        start_cols = m.sb("start_cols", [P, NJ], I32)
        window_rows = m.sb("window_rows", [P, 4, NJ, W])
        ident = keep["ident"]
        ps_fold = m.ps("ps_fold", [P, 512])
        ps_fold2 = m.ps("ps_fold2", [P, 512])
        ps_cnt = m.ps("ps_cnt", [P, 512])
        ps_base = m.ps("ps_base", [P, 512])
        ps_win = [m.ps(f"ps_win{i}", [P, W]) for i in range(2)]

        weights_in, edges_in = m.sem("weights_in"), m.sem("edges_in")
        kept_in = m.sem("kept_in")
        iotas_done, consts_done = m.sem("iotas_done"), m.sem("consts_done")
        dve_chain, act_chain = m.sem("dve_chain"), m.sem("act_chain")
        heads_ready, fold1, fold2, folds_copied = (m.sem(x) for x in ("heads_ready", "fold1", "fold2", "folds_copied"))
        wraps_ready, cutoff_ready = m.sem("wraps_ready"), m.sem("cutoff_ready")
        flat_ready, flat_out = m.sem("flat_ready"), m.sem("flat_out")
        onehots_ready, counted, within_ready, based = (m.sem(x) for x in ("onehots_ready", "counted", "within_ready", "based"))
        starts_ready, starts_out, starts_back = m.sem("starts_ready"), m.sem("starts_out"), m.sem("starts_back")
        index_ready, windows_in = m.sem("index_ready"), m.sem("windows_in")
        radial_in, radial_out = m.sems("radial_in", NJ), m.sem("radial_out")
        piece_ready, piece_turned, carry_ready, carry_turned = (m.sem(x) for x in ("piece_ready", "piece_turned", "carry_ready", "carry_turned"))
        count_ready, count_out, counts_in = m.sem("count_ready"), m.sem("count_out"), m.sem("counts_in")
        ident_zeroed, ident_ready = m.sem("ident_zeroed"), m.sem("ident_ready")
        turned, turned_used = m.sem("turned"), m.sem("turned_used")

        turns = [(j, k) for j in range(NJ) for k in range(3)] + [(j, 3) for j in range(NJ)]
        block = m.block()

        @block.sync
        def _(sp):
            n = 0
            for name, src in (("wl", "L0_wlt"), ("wr", "L0_wrt"), ("wln", "L0_wlnt"), ("w1", "L1_w1"), ("w2", "L1_w2")):
                sp.dma_start(keep[name][:], ins[src].rearrange("(c p) o -> p c o", p=P)).then_inc(kept_in, 16)
                n += 1
            sp.dma_start(keep["w3"][:, :, 0:D], ins["L3_wt"].rearrange("(c p) o -> p c o", p=P)).then_inc(kept_in, 16)
            sp.dma_start(keep["bl"][:], ins["L0_bl"]).then_inc(kept_in, 16)
            sp.dma_start(keep["wrad"][:], ins["L2_wradt"]).then_inc(kept_in, 16)
            sp.dma_start(keep["wedge"][:], ins["L3_wedge"]).then_inc(kept_in, 16)
            for name, src in (("b1", "L1_b1"), ("b2", "L1_b2"), ("adst", "L3_adst")):
                sp.dma_start(keep[name][:], ins[src].partition_broadcast(P)).then_inc(kept_in, 16)
            sp.dma_start(bias[:], ins["L3_bias"].partition_broadcast(3)).then_inc(kept_in, 16)
            sp.dma_start(keep["src_e"][:], ins["src_by_tile"]).then_inc(kept_in, 16)
            for dst_, src in ((wn, "L2_wn"), (lin1t, "L2_lin1t"), (lin2b, "L2_lin2b"), (mnt, "L2_mnt")):
                sp.dma_start(dst_[:], ins[src]).then_inc(weights_in, 16)
            sp.dma_start(w3[:], ins["L3_w"].rearrange("(c p) k -> p c k", p=P)).then_inc(weights_in, 16)
            sp.dma_start(asrc[:], ins["L3_asrc"]).then_inc(weights_in, 16)
            sp.wait_ge(flat_ready, 3)
            sp.wait_ge(cutoff_ready, 1)
            sp.dma_start(dram["dst_f"].rearrange("(p c) -> p c", p=P), dstf[:]).then_inc(flat_out, 16)
            sp.dma_start(dram["src_f"].rearrange("(p c) -> p c", p=P), srcf[:]).then_inc(flat_out, 16)
            sp.dma_start(dram["cut_f"].rearrange("(p c) -> p c", p=P), dist[:]).then_inc(flat_out, 16)
            sp.wait_ge(starts_ready, 1)
            sp.dma_start(dram["starts"][0:NT].rearrange("(g t) -> g t", t=TG), starts_i[:]).then_inc(starts_out, 16)
            sp.dma_start(dram["starts"][NT:NJ * P].unsqueeze(0), zero_i[:, NT:NJ * P]).then_inc(starts_out, 16)
            sp.wait_ge(starts_out, 32)
            sp.dma_start(keep["starts"][:], dram["starts"][0:NT].unsqueeze(0)).then_inc(starts_back, 16)
            sp.dma_start(row[:], dram["starts"][0:NT].unsqueeze(0)).then_inc(starts_back, 16)
            sp.dma_start(start_cols[:], dram["starts"].rearrange("(j p) -> p j", p=P),
                         allow_slow_non_contiguous=True).then_inc(starts_back, 16)
            sp.wait_ge(count_ready, 1)
            sp.dma_start(dram["icnt_f"].rearrange("(p c) -> p c", p=P), count_inv[:]).then_inc(count_out, 16)
            for j in range(NJ):
                sp.wait_ge(radial_in[j], 16 * RAD)
                sp.dma_start(dram["radial"][j * P:(j + 1) * P, :, :], radial_rows[:, j, :, :]).then_inc(radial_out, 16)
            sp.wait_ge(radial_out, NJ * 16)
            sp.wait_ge(count_out, 16)
            sp.wait_ge(flat_out, 3 * 16)
            sp.wait_ge(kept_in, 14 * 16)

        @block.scalar
        def _(act):
            act.dma_start(dst_x[:], bass.AP(tensor=ins["dst_ext"].tensor, offset=0, ap=[[EC, P], [1, EC + 2]])).then_inc(edges_in, 16)
            act.dma_start(src_i[:], ins["src_flat"].rearrange("(p c) -> p c", p=P)).then_inc(edges_in, 16)
            act.dma_start(dist[:], ins["dist_flat"].rearrange("(p c) -> p c", p=P)).then_inc(edges_in, 16)
            act.dma_start(dst_e[:], ins["dst_by_tile"]).then_inc(edges_in, 16)
            chain = Chained(act, act_chain)
            act.wait_ge(wraps_ready, 1)
            act.wait_ge(consts_done, 1)
            chain(nc.scalar.activation(wraps[:], wraps[:], ACT.Sin, bias=half_pi[:], scale=-3.14159265358979))
            nc.scalar.activation(dist[:], wraps[:], ACT.Square).then_inc(cutoff_ready, 1)

        @block.gpsimd
        def _(pool):
            nc.gpsimd.iota(keep["iota"][:], pattern=[[1, TN]], base=0, channel_multiplier=0,
                           allow_small_or_imprecise_dtypes=True).then_inc(iotas_done, 1)
            nc.gpsimd.iota(keep["base"][:], pattern=[[TN, NT]], base=0, channel_multiplier=0,
                           allow_small_or_imprecise_dtypes=True).then_inc(iotas_done, 1)
            nc.gpsimd.iota(group_start[:], pattern=[[TN * TG, NG + 1]], base=0, channel_multiplier=0,
                           allow_small_or_imprecise_dtypes=True).then_inc(iotas_done, 1)
            nc.gpsimd.iota(tile_start[:], pattern=[[TN, TG + 1]], base=0, channel_multiplier=0,
                           allow_small_or_imprecise_dtypes=True).then_inc(iotas_done, 1)
            nc.gpsimd.iota(iota_g[:], pattern=[[1, NG]], base=0, channel_multiplier=0,
                           allow_small_or_imprecise_dtypes=True).then_inc(iotas_done, 1)
            nc.gpsimd.iota(part_g[:], pattern=[[0, 1]], base=0, channel_multiplier=1,
                           allow_small_or_imprecise_dtypes=True).then_inc(iotas_done, 1)
            nc.gpsimd.memset(ident[:], 0.0).then_inc(ident_zeroed, 1)
            pool.wait_ge(ident_zeroed, 1)
            nc.gpsimd.affine_select(out=ident[:], in_=ident[:], compare_op=ALU.not_equal, fill=1.0, base=0,
                                    pattern=[[-1, P]], channel_multiplier=1).then_inc(ident_ready, 1)
            pool.wait_ge(index_ready, 1)
            pool.wait_ge(flat_out, 3 * 16)
            for j in range(NJ):
                for k, name in enumerate(("dst_f", "src_f", "cut_f")):
                    pool.indirect_dma_start(
                        out=window_rows[:, k, j, :], out_offset=None, in_=dram[name].unsqueeze(1),
                        in_offset=bass.IndirectOffsetOnAxis(ap=start_cols[:, j:j + 1], axis=0)).then_inc(windows_in, 16)
            for j in range(NJ):
                for k in range(RAD):
                    pool.indirect_dma_start(
                        out=radial_rows[:, j, k, :], out_offset=None, in_=ins["radial_flat"].unsqueeze(1),
                        in_offset=bass.IndirectOffsetOnAxis(ap=keep["start_cols"][:, k, j:j + 1], axis=0),
                    ).then_inc(radial_in[j], 16)
            pool.wait_ge(count_out, 16)
            for j in range(NJ):
                pool.indirect_dma_start(
                    out=window_rows[:, 3, j, :], out_offset=None, in_=dram["icnt_f"].unsqueeze(1),
                    in_offset=bass.IndirectOffsetOnAxis(ap=start_cols[:, j:j + 1], axis=0)).then_inc(counts_in, 16)

        @block.vector
        def _(dve):
            chain = Chained(dve, dve_chain)
            nc.vector.memset(half_pi[:], 1.5707963267949).then_inc(consts_done, 1)
            chain(nc.vector.memset(keep["eps"][:], EPS))
            chain(nc.vector.memset(keep["ones"][:], 1.0))
            chain(nc.vector.memset(keep["ones_b"][:], 1.0))
            chain(nc.vector.memset(zero_i[:], 0))
            chain(nc.vector.memset(ones_e[:], 1.0))
            dve.wait_ge(edges_in, 4 * 16)
            nc.vector.tensor_copy(srcf[:], src_i[:]).then_inc(flat_ready, 1)
            nc.vector.tensor_scalar(keep["dst_e"][:], dst_e[:], float(N - 1), None, ALU.min).then_inc(flat_ready, 1)
            chain(nc.vector.tensor_scalar(rest[:], dist[:], 0.1, None, ALU.mult))
            chain(nc.vector.tensor_scalar(wraps[:], rest[:], 12582912.0, None, ALU.add))
            chain(nc.vector.tensor_scalar(wraps[:], wraps[:], 12582912.0, None, ALU.subtract))
            chain(nc.vector.tensor_tensor(wraps[:], rest[:], wraps[:], ALU.subtract))
            nc.vector.scalar_tensor_tensor(out=wraps[:], in0=wraps[:], scalar=-1.0, in1=wraps[:],
                                           op0=ALU.mult, op1=ALU.max).then_inc(wraps_ready, 1)
            dve.wait_ge(wraps_ready, 1)
            chain(nc.vector.tensor_copy(dstf[:], dst_x[:, 1:EC + 1]))
            dve.sem_inc(flat_ready, 1)
            dve.wait_ge(iotas_done, 6)
            chain(nc.vector.tensor_tensor(
                past_group[:], dstf[:].unsqueeze(2).broadcast_to([P, EC, NG + 1]),
                group_start[:].unsqueeze(1).broadcast_to([P, EC, NG + 1]), ALU.is_ge))
            chain(nc.vector.tensor_tensor(in_group[:], past_group[:, :, 0:NG], past_group[:, :, 1:NG + 1], ALU.subtract))
            chain(nc.vector.tensor_reduce(group_no[:], past_group[:, :, 1:NG + 1], AX_X, ALU.add))
            chain(nc.vector.scalar_tensor_tensor(rest[:], group_no[:], -float(TN * TG), dstf[:], ALU.mult, ALU.add))
            nc.vector.tensor_tensor(
                before_tile[:], rest[:].unsqueeze(2).broadcast_to([P, EC, TG + 1]),
                tile_start[:].unsqueeze(1).broadcast_to([P, EC, TG + 1]), ALU.is_lt).then_inc(onehots_ready, 1)
            chain(nc.vector.tensor_scalar(earlier[:], iota_g[:], part_g[:], None, ALU.is_gt))
            dve.wait_ge(weights_in, 6 * 16)
            chain(nc.vector.memset(hsel[:], 0.0))
            for c in range(KC):
                for g in range(P // HD):
                    h = c * (P // HD) + g
                    chain(nc.vector.memset(hsel[g * HD:(g + 1) * HD, c, h:h + 1], 1.0))
            for c in range(KC):
                nc.vector.tensor_scalar(ahead[:, c, :], hsel[:, c, :], asrc[:, c:c + 1], None, ALU.mult).then_inc(heads_ready, 1)
            dve.wait_ge(fold1, 1)
            chain(nc.vector.tensor_copy(keep["wc"][:], ps_fold[:, 0:KC * FILT].rearrange("p (c o) -> p c o", c=KC)))
            chain(nc.vector.tensor_copy(keep["w3"][:, :, D:HW], ps_fold[:, 128:128 + KC * H].rearrange("p (c o) -> p c o", c=KC)))
            chain(nc.vector.tensor_copy(keep["m2"][:], ps_fold2[0:FILT + 1, 0:D]))
            dve.wait_ge(counted, 1)
            nc.vector.tensor_copy(within[:], ps_cnt[0:NG, 0:TG + 1]).then_inc(within_ready, 1)
            dve.wait_ge(based, 1)
            dve.wait_ge(within_ready, 1)
            chain(nc.vector.tensor_scalar(starts[:], within[:, 0:TG], ps_base[0:NG, 0:1], None, ALU.add))
            nc.vector.tensor_copy(starts_i[:], starts[:]).then_inc(starts_ready, 1)
            dve.wait_ge(starts_back, 48)
            chain(nc.vector.tensor_copy(rowf[:], row[:]))
            chain(nc.vector.memset(cnt[:], 0.0))
            chain(nc.vector.tensor_tensor(cnt[:, 0:NT - 1], rowf[:, 1:NT], rowf[:, 0:NT - 1], ALU.subtract))
            chain(nc.vector.tensor_scalar(cnt_i[:], cnt[:], -1.0, 0.0, ALU.add, ALU.max))
            chain(nc.vector.tensor_scalar(over_i[:], cnt_i[:], 7, None, ALU.arith_shift_right))
            chain(nc.vector.tensor_copy(keep["over"][:, 0:NT], over_i[:]))
            chain(nc.vector.tensor_reduce(cnt[:, 0:1], over_i[:], AX_X, ALU.max))
            chain(nc.vector.tensor_copy(keep["over"][:, NT:NT + 1], cnt[:, 0:1]))
            for k in range(RAD):
                chain(nc.vector.tensor_scalar(keep["start_cols"][:, k, :], start_cols[:], float(k * EP), None, ALU.add))
            dve.sem_inc(index_ready, 1)

            def carried_scan(n, out, add, backward):
                flip = (lambda t: t[:, ::-1]) if backward else (lambda t: t[:, :])
                final = out[:, 0:1] if backward else out[:, EC - 1:EC]
                chain(nc.vector.tensor_tensor_scan(flip(out), flip(same), flip(add), 0.0, ALU.mult, ALU.add))
                chain(nc.vector.tensor_copy(piece_col[:, 0:1], final))
                nc.vector.tensor_reduce(piece_col[:, 1:2], same[:], AX_X, ALU.min).then_inc(piece_ready, 1)
                dve.wait_ge(piece_turned, n)
                chain(nc.vector.tensor_copy(piece_row[:], ps_base[0:1, 128:128 + 2 * P].rearrange("p (k c) -> p k c", k=2)))
                chain(nc.vector.tensor_tensor_scan(flip(piece_run), flip(piece_row[:, 1, :]), flip(piece_row[:, 0, :]), 0.0,
                                                   ALU.mult, ALU.add))
                chain(nc.vector.memset(carry_row[:], 0.0))
                to, of = ((carry_row[:, 0:P - 1], piece_run[:, 1:P]) if backward else
                          (carry_row[:, 1:P], piece_run[:, 0:P - 1]))
                nc.vector.tensor_copy(to, of).then_inc(carry_ready, 1)
                dve.wait_ge(carry_turned, n)
                chain(nc.vector.tensor_copy(carry_in[:], ps_base[:, 64:65]))
                chain(nc.vector.tensor_tensor_scan(flip(out), flip(same), flip(add), carry_in[:, 0:1], ALU.mult, ALU.add))

            chain(nc.vector.tensor_tensor(same[:], dst_x[:, 1:EC + 1], dst_x[:, 0:EC], ALU.is_equal))
            carried_scan(1, run, ones_e, backward=False)
            chain(nc.vector.tensor_tensor(same[:], dst_x[:, 1:EC + 1], dst_x[:, 2:EC + 2], ALU.is_equal))
            chain(nc.vector.tensor_tensor(rest[:], run[:], same[:], ALU.mult))
            chain(nc.vector.tensor_tensor(run[:], run[:], rest[:], ALU.subtract))
            carried_scan(2, count_e, run, backward=True)
            nc.vector.reciprocal(count_inv[:], count_e[:]).then_inc(count_ready, 1)
            dve.wait_ge(kept_in, 14 * 16)
            dve.wait_ge(ident_ready, 1)
            chain(nc.vector.tensor_copy(bias_rest[:], bias[:]))
            chain(nc.vector.memset(bias_rows[:], 0.0))
            for k in range(3):
                chain(nc.vector.tensor_copy(part_b[:], bias_rest[:]))
                chain(nc.vector.tensor_copy(part_f[:], part_b[:]))
                chain(nc.vector.tensor_tensor(bias_rest[:], bias_rest[:], part_f[:], ALU.subtract))
                chain(nc.vector.scalar_tensor_tensor(out=bias_rows[:], in0=part_f[:], scalar=ident[0:3, k:k + 1], in1=bias_rows[:],
                                                     op0=ALU.mult, op1=ALU.add))
            chain(nc.vector.tensor_copy(keep["bias3"][:], bias_rows[:]))
            for n, (j, k) in enumerate(turns):
                w = min(P, NT - j * P)
                at = slice(j * P, j * P + w)
                dve.wait_ge(turned, n + 1)
                if k == 0:
                    op = nc.vector.tensor_tensor(keep["drel"][:, at], ps_win[n % 2][:, 0:w], keep["base"][:, at], ALU.subtract)
                else:
                    op = nc.vector.tensor_copy(keep[("src", "cut", "icnt")[k - 1]][:, at], ps_win[n % 2][:, 0:w])
                op.then_inc(turned_used, 1)
            dve.wait_ge(turned_used, len(turns))

        @block.tensor
        def _(pe):
            pe.wait_ge(weights_in, 6 * 16)
            for c in range(KC):
                nc.tensor.matmul(ps_fold[:, c * FILT:(c + 1) * FILT], wn[:, c * P:(c + 1) * P], lin1t[:], start=True, stop=True)
            pe.wait_ge(heads_ready, KC)
            for c in range(KC):
                for o in range(KC):
                    nc.tensor.matmul(ps_fold[:, 128 + c * H:128 + (c + 1) * H], w3[:, o, c * P:(c + 1) * P], ahead[:, o, :],
                                     start=(o == 0), stop=(o == KC - 1))
            nc.tensor.matmul(ps_fold2[0:FILT + 1, 0:D], lin2b[:], mnt[:], start=True, stop=True).then_inc(fold1, 1)
            pe.wait_ge(onehots_ready, 1)
            for c in range(EC):
                last = nc.tensor.matmul(ps_cnt[0:NG, 0:TG + 1], in_group[:, c, :], before_tile[:, c, :],
                                        start=(c == 0), stop=(c == EC - 1))
            last.then_inc(counted, 1)
            pe.wait_ge(within_ready, 1)
            nc.tensor.matmul(ps_base[0:NG, 0:1], earlier[:], within[:, TG:TG + 1], start=True, stop=True).then_inc(based, 1)
            pe.wait_ge(ident_ready, 1)
            for n in range(1, 3):
                pe.wait_ge(piece_ready, n)
                for k in range(2):
                    last = nc.tensor.transpose(ps_base[0:1, 128 + k * P:128 + (k + 1) * P], piece_col[:, k:k + 1], ident[:])
                last.then_inc(piece_turned, 1)
                pe.wait_ge(carry_ready, n)
                nc.tensor.matmul(ps_base[:, 64:65], carry_row[:], keep["ones"][0:1, 0:1], start=True, stop=True).then_inc(
                    carry_turned, 1)
            for n, (j, k) in enumerate(turns):
                pe.wait_ge(windows_in if k < 3 else counts_in, 16 * NJ * (3 if k < 3 else 1))
                if n >= 2:
                    pe.wait_ge(turned_used, n - 1)
                nc.tensor.transpose(ps_win[n % 2][:, 0:W], window_rows[:, k, j, :], ident[:]).then_inc(turned, 1)


class Further:

    def __init__(self, eng, keep, name):
        self.eng, self.keep, self.wanted = eng, keep, True
        self.any_over = eng.value_load(keep["over"][0:1, NT:NT + 1], min_val=0, max_val=ET)
        self.done = eng.alloc_register(f"{name}_chunks_done")
        eng.reg_mov(self.done, 0)

    def chunks(self, tile, body):
        eng = self.eng
        if self.wanted:
            count = eng.value_load(self.keep["over"][0:1, bass.ds(tile.t, 1)], min_val=0, max_val=ET)
            with eng.If(count > 0):
                with eng.Fori(0, count) as k:
                    eng.reg_add(self.done, self.done, 1)
                    body(k, eng.snap(self.done, min_val=1, max_val=60000))


class WindowSweep:

    def __init__(self, nc, ctx, keep, dram, ins, name, table, width, values=(), columns=()):
        self.nc, self.keep, self.dram, self.ins = nc, keep, dram, ins
        self.table, self.width, self.values, self.columns = table, width, values, columns
        m = self.m = Memory(nc, ctx, name)
        self.index = m.sb("index", [P, 8], I32)
        self.rows = m.sb("rows", [P, 8, width])
        self.sel = m.sb("sel", [P, 8, TN])
        self.index_ready = m.sem("index_ready")
        self.gathered = m.sems("gathered", 8)
        self.sel_ready = m.sem("sel_ready")
        self.summed = m.sem("summed")
        self.x_src = m.sb("x_src", [P, 1], I32)
        self.x_dst = m.sb("x_dst", [P, 1])
        self.x_values = m.sb("x_values", [P, 2])
        self.x_rel = m.sb("x_rel", [P, 1])
        self.x_rows = m.sb("x_rows", [P, width])
        self.x_sel = m.sb("x_sel", [P, TN])
        self.x_cols = m.sb("x_cols", [16, W])
        self.x_loaded = m.sem("x_loaded")
        self.x_gathered = m.sem("x_gathered")
        self.x_rel_ready = m.sem("x_rel_ready")
        self.x_sel_ready = m.sem("x_sel_ready")
        self.x_summed = m.sem("x_summed")
        self.passed = m.sems("passed", 4)
        self.x_loads = 2 + len(values) + len(columns)
        self.w = m.sb("w", [TN, 8, D])
        self.stats = m.sb("stats", [TN, 8, 6])
        self.mv = m.sb("mv", [TN, 8, 2])
        self.sd = m.sb("sd", [TN, 8, 1])
        self.rstd = m.sb("rstd", [TN, 8, 1])
        self.shift = m.sb("shift", [TN, 8, 1])
        self.w_ready, self.stats_ready, self.mv_ready, self.sd_ready, self.rstd_ready, self.shift_ready = (
            m.sem(x) for x in ("w_ready", "stats_ready", "mv_ready", "sd_ready", "rstd_ready", "shift_ready"))

    def gather(self, pool, rows_free=None):
        further = Further(pool, self.keep, self.m.name)
        rows_free = rows_free or self.summed

        def stage(tile):
            slot, round_ = tile.ring(8)
            if slot % 4 == 0:
                if tile.from_(8):
                    pool.wait_ge(rows_free, tile.t - 4)
                self.nc.gpsimd.tensor_copy(self.index[:, slot:slot + 4], self.keep["src"][:, bass.ds(tile.t, 4)]).then_inc(
                    self.index_ready, 1)
                wait_apart(pool, self.index_ready, round_ * 2 + slot // 4 + 1, self.passed[1])
            pool.indirect_dma_start(
                out=self.rows[:, slot, :], out_offset=None, in_=self.table,
                in_offset=bass.IndirectOffsetOnAxis(ap=self.index[:, slot:slot + 1], axis=0)).then_inc(self.gathered[slot], 16)

            def chunk(k, n):
                wait_apart(pool, self.x_loaded, n * (16 * self.x_loads), self.passed[1])
                pool.indirect_dma_start(
                    out=self.x_rows[:], out_offset=None, in_=self.table,
                    in_offset=bass.IndirectOffsetOnAxis(ap=self.x_src[:, 0:1], axis=0)).then_inc(self.x_gathered, 16)

            further.chunks(tile, chunk)

        sweep(pool, NT, [(0, stage)], further)

    def load_chunks(self, sp, further, tile):
        def chunk(k, n):
            start = sp.value_load(self.keep["starts"][0:1, bass.ds(tile.t, 1)], min_val=0, max_val=N)
            at = self.nc.s_assert_within(start + k * W + W, 0, N)
            sp.dma_start(self.x_src[:], self.ins["src_flat"][bass.ds(at, W)].unsqueeze(1)).then_inc(self.x_loaded, 16)
            sp.dma_start(self.x_dst[:], self.dram["dst_f"][bass.ds(at, W)].unsqueeze(1)).then_inc(self.x_loaded, 16)
            for i, value in enumerate(self.values):
                sp.dma_start(self.x_values[:, i:i + 1], value[bass.ds(at, W)].unsqueeze(1)).then_inc(self.x_loaded, 16)
            for source, n_rows in self.columns:
                sp.dma_start(self.x_cols[0:n_rows, :], source[:, bass.ds(at, W)]).then_inc(self.x_loaded, 16)
            wait_apart(sp, self.x_summed, n, self.passed[2])

        further.chunks(tile, chunk)

    def select(self, dve, tile, scale=None):
        slot, _ = tile.ring(8)
        s2, op1 = (scale(slot, tile), ALU.mult) if scale else (None, ALU.bypass)
        self.nc.vector.tensor_scalar(self.sel[:, slot, :], self.keep["iota"][:], self.keep["drel"][:, bass.ds(tile.t, 1)],
                                     s2, ALU.is_equal, op1).then_inc(self.sel_ready, 1)

    def select_chunk(self, dve, tile, n, scale=None):
        dve.wait_ge(self.x_gathered, n * 16)
        self.nc.vector.tensor_tensor(self.x_rel[:], self.x_dst[:], self.keep["base"][:, bass.ds(tile.t, 1)],
                                     ALU.subtract).then_inc(self.x_rel_ready, 1)
        dve.wait_ge(self.x_rel_ready, n)
        s2, op1 = (scale, ALU.mult) if scale is not None else (None, ALU.bypass)
        self.nc.vector.tensor_scalar(self.x_sel[:], self.keep["iota"][:], self.x_rel[:, 0:1], s2,
                                     ALU.is_equal, op1).then_inc(self.x_sel_ready, 1)

    def row_stats(self, dve, tile):
        slot, _ = tile.ring(8)
        dve.wait_ge(self.w_ready, tile.t + 1)
        self.nc.vector.bn_stats(self.stats[:, slot, :], self.w[:, slot, :]).then_inc(self.stats_ready, 1)

    def moments(self, dve, tile):
        slot, _ = tile.ring(8)
        wait_apart(dve, self.stats_ready, tile.t + 1, self.passed[0])
        self.nc.vector.bn_aggr(self.mv[:, slot, :], self.stats[:, slot, :]).then_inc(self.mv_ready, 1)

    def deviation(self, act, tile):
        if tile.slot8 % 2:
            pair = slice(tile.slot8 - 1, tile.slot8 + 1)
            act.wait_ge(self.mv_ready, tile.t + 1)
            self.nc.scalar.activation(self.sd[:, pair, :], self.mv[:, pair, 1:2], ACT.Sqrt,
                                      bias=self.keep["eps"][0:TN, :]).then_inc(self.sd_ready, 2)

    def factor(self, dve, tile):
        if tile.slot8 % 2:
            pair = slice(tile.slot8 - 1, tile.slot8 + 1)
            dve.wait_ge(self.sd_ready, tile.t + 1)
            self.nc.vector.reciprocal(self.rstd[:, pair, :], self.sd[:, pair, :]).then_inc(self.rstd_ready, 2)

    def offset(self, dve, tile):
        if tile.slot8 % 2:
            pair = slice(tile.slot8 - 1, tile.slot8 + 1)
            dve.wait_ge(self.rstd_ready, tile.t + 1)
            self.nc.vector.scalar_tensor_tensor(out=self.shift[:, pair, :], in0=self.mv[:, pair, 0:1], scalar=-1.0,
                                                in1=self.rstd[:, pair, :], op0=ALU.mult, op1=ALU.mult).then_inc(self.shift_ready, 2)


def node_rows(table, tile, width=D, count=2):
    return table[bass.ds(tile.t * TN, count * TN), 0:width].rearrange("(k p) f -> p k f", p=TN)


def build_sage(nc, keep, dram, ins):
    with ExitStack() as ctx:
        s = WindowSweep(nc, ctx, keep, dram, ins, "sage", ins["x"], D, values=(dram["icnt_f"],))
        m = s.m
        edge_of = m.sb("edge_of", [P, 8, TN], BF16)
        x_edge_of = m.sb("x_edge_of", [P, TN], BF16)
        x = m.sb("x", [TN, 8, D])
        xt = m.sb("xt", [P, 4, KC, 2 * TN])
        mean_t = m.sb("mean_t", [P, 4, KC, 2 * TN])
        hid_t = m.sb("hid_t", [P, 4, KC, 2 * TN])
        deg_root = m.sb("deg_root", [TN, 8, 1])
        dinv = m.sb("dinv", [TN, 8, 1])
        y = m.sb("y", [TN, 8, D])
        factor_s = m.sb("factor_s", [TN, 8, 1])
        shift_s = m.sb("shift_s", [TN, 8, 1])
        out = m.sb("out", [TN, 8, D])
        out_s = m.sb("out_s", [TN, 8, DW])
        sum_ps = [m.ps(f"sum_ps{i}", [P, 512]) for i in range(2)]
        hid_ps = [m.ps(f"hid_ps{i}", [P, 512]) for i in range(2)]
        out_ps = [m.ps(f"out_ps{i}", [P, 512]) for i in range(4)]
        loaded, stored = m.sems("loaded", 4), m.sems("stored", 4)
        mean_ready, inverted, scaled_ready, hid_summed, hid_ready, out_summed, y_ready, out_ready = (
            m.sem(n) for n in ("mean_ready", "inverted", "scaled_ready", "hid_summed", "hid_ready", "out_summed", "y_ready", "out_ready"))
        CNT = KC * TN
        block = m.block()

        @block.gpsimd
        def _(pool):
            s.gather(pool)

        @block.sync
        def _(sp):
            further = Further(sp, keep, s.m.name)

            def load(tile):
                if tile.slot8 % 2:
                    return
                pair = tile.slot8 // 2
                if tile.from_(8):
                    sp.wait_ge(s.w_ready, tile.t - 6)
                sp.dma_start(x[:, 2 * pair:2 * pair + 2, :], node_rows(ins["x"], tile)).then_inc(loaded[pair], 16)
                sp.dma_start(xt[:, pair, :, :], ins["xt"][:, bass.ds(tile.t * TN, 2 * TN)].rearrange(
                    "(c p) n -> p c n", p=P)).then_inc(loaded[pair], 16)

            def store(tile):
                if tile.slot8 % 2:
                    return
                slot, _ = tile.ring(8)
                sp.wait_ge(out_ready, tile.t + 2)
                sp.dma_start(node_rows(dram["x1"], tile), out[:, slot:slot + 2, :]).then_inc(stored[slot // 2], 16)
                sp.dma_start(node_rows(dram["x1_s"], tile, DW), out_s[:, slot:slot + 2, :]).then_inc(stored[slot // 2], 16)

            sweep(sp, NT, [(0, load), (0, lambda tile: s.load_chunks(sp, further, tile)), (18, store)], further)
            for q in stored:
                sp.wait_ge(q, 32 * (NT // 8))

        @block.vector
        def _(dve):
            further = Further(dve, keep, s.m.name)

            def select(tile):
                slot, _ = tile.ring(8)
                nc.vector.tensor_scalar(edge_of[:, slot, :], keep["iota"][:], keep["drel"][:, bass.ds(tile.t, 1)], None, ALU.is_equal)
                s.select(dve, tile, scale=lambda slot, tile_: keep["icnt"][:, bass.ds(tile_.t, 1)])

                def chunk(k, n):
                    dve.wait_ge(s.x_gathered, n * 16)
                    nc.vector.tensor_tensor(s.x_rel[:], s.x_dst[:], keep["base"][:, bass.ds(tile.t, 1)],
                                            ALU.subtract).then_inc(s.x_rel_ready, 1)
                    dve.wait_ge(s.x_rel_ready, n)
                    nc.vector.tensor_scalar(x_edge_of[:], keep["iota"][:], s.x_rel[:, 0:1], None, ALU.is_equal)
                    nc.vector.tensor_scalar(s.x_sel[:], keep["iota"][:], s.x_rel[:, 0:1], s.x_values[:, 0:1],
                                            ALU.is_equal, ALU.mult).then_inc(s.x_sel_ready, 1)

                further.chunks(tile, chunk)

            def skip(tile):
                slot, _ = tile.ring(8)
                dve.wait_ge(out_summed, tile.t + 1)
                nc.vector.tensor_tensor(y[:, slot, :], out_ps[slot % 4][0:TN, 0:D], x[:, slot, :], ALU.add).then_inc(y_ready, 1)

            def residual(tile):
                slot, _ = tile.ring(8)
                dve.wait_ge(y_ready, tile.t + 1)
                if tile.from_(8):
                    dve.wait_ge(out_ready, tile.t - 7)
                nc.vector.scalar_tensor_tensor(out=s.w[:, slot, :], in0=y[:, slot, :], scalar=0.0, in1=x[:, slot, :],
                                               op0=ALU.max, op1=ALU.add).then_inc(s.w_ready, 1)

            def degrees(tile):
                if tile.slot8 % 2:
                    pair = slice(tile.slot8 - 1, tile.slot8 + 1)
                    dve.wait_ge(mean_ready, tile.t + 1)
                    nc.vector.reciprocal(dinv[:, pair, :], deg_root[:, pair, :]).then_inc(inverted, 2)

            def scaled_factors(tile):
                if tile.slot8 % 2:
                    pair = slice(tile.slot8 - 1, tile.slot8 + 1)
                    if tile.from_(8):
                        dve.wait_ge(stored[tile.slot8 // 2], tile.round8 * 32)
                    dve.wait_ge(s.shift_ready, tile.t + 1)
                    nc.vector.tensor_copy(out_s[:, pair, D:DW], dinv[:, pair, :])
                    nc.vector.tensor_tensor(factor_s[:, pair, :], s.rstd[:, pair, :], dinv[:, pair, :], ALU.mult)
                    nc.vector.tensor_tensor(shift_s[:, pair, :], s.shift[:, pair, :], dinv[:, pair, :], ALU.mult).then_inc(scaled_ready, 2)

            sweep(dve, NT, [(10, lambda tile: s.factor(dve, tile)), (7, skip), (8, lambda tile: s.row_stats(dve, tile)),
                            (7, residual), (11, scaled_factors), (4, degrees), (0, select), (8, lambda tile: s.moments(dve, tile)),
                            (10, lambda tile: s.offset(dve, tile))], further)

        @block.scalar
        def _(act):
            def means(tile):
                slot, _ = tile.ring(8)
                ps = sum_ps[slot % 2]
                at = slice(slot % 2 * TN, slot % 2 * TN + TN)
                act.wait_ge(s.summed, tile.t + 1)
                nc.scalar.activation(deg_root[:, slot, :], ps[0:TN, CNT:CNT + 1], ACT.Sqrt, bias=keep["ones"][0:TN, 0:1])
                nc.scalar.copy(mean_t[:, slot // 2, :, at], ps[:, 0:CNT].rearrange("p (c n) -> p c n", c=KC)).then_inc(mean_ready, 1)

            def hidden(tile):
                if tile.slot8 % 2:
                    pair = tile.slot8 // 2
                    act.wait_ge(hid_summed, tile.t + 1)
                    for o in range(KC):
                        last = nc.scalar.activation(hid_t[:, pair, o, :], hid_ps[pair % 2][:, o * 2 * TN:(o + 1) * 2 * TN], ACT.Relu,
                                                    bias=keep["bl"][:, o:o + 1])
                    last.then_inc(hid_ready, 2)

            def normal(tile):
                slot, round8 = tile.ring(8)
                act.wait_ge(s.shift_ready, tile.t + 1)
                if tile.from_(8):
                    act.wait_ge(stored[slot // 2], round8 * 32)
                nc.scalar.activation(out[:, slot, :], s.w[:, slot, :], ACT.Identity, bias=s.shift[:, slot, :],
                                     scale=s.rstd[:, slot, :])

            def normal_scaled(tile):
                slot, _ = tile.ring(8)
                act.wait_ge(scaled_ready, tile.t + 1)
                nc.scalar.activation(out_s[:, slot, 0:D], s.w[:, slot, :], ACT.Identity, bias=shift_s[:, slot, :],
                                     scale=factor_s[:, slot, :]).then_inc(out_ready, 1)

            sweep(act, NT, [(5, hidden), (2, means), (9, lambda tile: s.deviation(act, tile)), (12, normal), (13, normal_scaled)])

        @block.tensor
        def _(pe):
            further = Further(pe, keep, s.m.name)

            def sums(tile):
                slot, round8 = tile.ring(8)
                ps = sum_ps[slot % 2]
                if tile.from_(2):
                    pe.wait_ge(mean_ready, tile.t - 1)
                pe.wait_ge(s.sel_ready, tile.t + 1)
                pe.wait_ge(s.gathered[slot], (round8 + 1) * 16)

                def add(rows, sel, edge_of, part, start=False):
                    if part < KC:
                        return nc.tensor.matmul(ps[:, part * TN:(part + 1) * TN], rows[:, part * P:(part + 1) * P], sel,
                                                start=start, stop=True, skip_group_check=True)
                    return nc.tensor.matmul(ps[0:TN, CNT:CNT + 1], edge_of, keep["ones_b"][:, 0:1], start=False, stop=True, skip_group_check=True)

                window = (s.rows[:, slot, :], s.sel[:, slot, :], edge_of[:, slot, :])
                add(*window, 0, start=True)

                def chunk(k, n):
                    pe.wait_ge(s.x_sel_ready, n)
                    for part in range(KC + 1):
                        last = add(s.x_rows[:], s.x_sel[:], x_edge_of[:], part)
                    last.then_inc(s.x_summed, 1)

                further.chunks(tile, chunk)
                for part in range(1, KC + 1):
                    last = add(*window, part)
                last.then_inc(s.summed, 1)

            def hidden(tile):
                if tile.slot8 % 2 == 0:
                    return
                pair = tile.slot8 // 2
                ps = hid_ps[pair % 2]
                pe.wait_ge(loaded[pair], (tile.round8 + 1) * 32)

                def multiply(weight, rows, first):
                    for o in range(KC):
                        for c in range(KC):
                            last = nc.tensor.matmul(ps[:, o * 2 * TN:(o + 1) * 2 * TN], keep[weight][:, c, o * P:(o + 1) * P],
                                                    rows[:, pair, c, :], start=(first and o == 0 and c == 0), stop=True,
                                                    skip_group_check=True)
                    return last

                multiply("wr", xt, True)
                pe.wait_ge(mean_ready, tile.t + 1)
                multiply("wl", mean_t, False).then_inc(hid_summed, 2)

            def output(tile):
                slot, _ = tile.ring(8)
                pair, half = slot // 2, slot % 2
                if half == 0:
                    pe.wait_ge(hid_ready, tile.t + 2)
                if tile.from_(4):
                    pe.wait_ge(y_ready, tile.t - 3)
                for c in range(KC):
                    last = nc.tensor.matmul(out_ps[slot % 4][0:TN, 0:D], hid_t[:, pair, c, half * TN:(half + 1) * TN],
                                            keep["wln"][:, c, :], start=(c == 0), stop=(c == KC - 1))
                last.then_inc(out_summed, 1)

            sweep(pe, NT, [(4, hidden), (1, sums), (6, output)], further)


class Projection:

    def __init__(self, s, matrix, width, proj_banks):
        self.s, self.nc, self.matrix, self.width = s, s.nc, matrix, width
        m = s.m
        self.out = m.sb("out", [TN, 8, D])
        self.turned = m.sb("turned", [P, 8, KC * TN])
        self.proj = m.sb("proj", [TN, 8, width])
        self.turn_ps = [m.ps(f"turn_ps{i}", [P, 512]) for i in range(2)]
        self.proj_ps = [m.ps(f"proj_ps{i}", [P, 512]) for i in range(proj_banks)]
        self.out_ready, self.turn_done, self.turned_ready, self.proj_done, self.proj_ready = (
            m.sem(n) for n in ("out_ready", "turn_done", "turned_ready", "proj_done", "proj_ready"))
        self.stored, self.proj_stored = m.sems("stored", 4), m.sems("proj_stored", 4)
        self.proj_stores = 1

    def normal(self, act, tile):
        s = self.s
        slot, round8 = tile.ring(8)
        act.wait_ge(s.shift_ready, tile.t + 1)
        if tile.from_(8):
            act.wait_ge(self.stored[slot // 2], round8 * 16)
        self.nc.scalar.activation(self.out[:, slot, :], s.w[:, slot, :], ACT.Identity, bias=s.shift[:, slot, :],
                                  scale=s.rstd[:, slot, :]).then_inc(self.out_ready, 1)

    def turn(self, pe, tile):
        slot, _ = tile.ring(8)
        pe.wait_ge(self.out_ready, tile.t + 1)
        if tile.from_(2):
            pe.wait_ge(self.turned_ready, tile.t - 1)
        for c in range(KC):
            last = self.nc.tensor.transpose(self.turn_ps[slot % 2][:, c * TN:(c + 1) * TN],
                                            self.out[:, slot, c * P:(c + 1) * P], self.s.keep["ident"][0:TN, 0:TN])
        last.then_inc(self.turn_done, 1)

    def copy_turned(self, act, tile):
        slot, _ = tile.ring(8)
        act.wait_ge(self.turn_done, tile.t + 1)
        if tile.from_(8):
            act.wait_ge(self.proj_done, tile.t - 7)
        self.nc.scalar.copy(self.turned[:, slot, :], self.turn_ps[slot % 2][:, 0:KC * TN]).then_inc(self.turned_ready, 1)

    def project(self, pe, tile):
        slot, _ = tile.ring(8)
        banks = len(self.proj_ps)
        pe.wait_ge(self.turned_ready, tile.t + 1)
        if tile.from_(banks):
            pe.wait_ge(self.proj_ready, tile.t + 1 - banks)
        for c in range(KC):
            last = self.nc.tensor.matmul(self.proj_ps[slot % len(self.proj_ps)][0:TN, 0:self.width],
                                         self.turned[:, slot, c * TN:(c + 1) * TN], self.matrix[:, c, :],
                                         start=(c == 0), stop=(c == KC - 1))
        last.then_inc(self.proj_done, 1)

    def copy_projected(self, act, tile):
        slot, round8 = tile.ring(8)
        act.wait_ge(self.proj_done, tile.t + 1)
        if tile.from_(8):
            act.wait_ge(self.proj_stored[slot // 2], round8 * 16 * self.proj_stores)
        self.nc.scalar.copy(self.proj[:, slot, :], self.proj_ps[slot % len(self.proj_ps)][0:TN, 0:self.width]).then_inc(
            self.proj_ready, 1)

    def store_rows(self, sp, tile, table):
        if tile.slot8 % 2:
            return
        slot, _ = tile.ring(8)
        sp.wait_ge(self.out_ready, tile.t + 2)
        sp.dma_start(node_rows(table, tile), self.out[:, slot:slot + 2, :]).then_inc(self.stored[slot // 2], 16)

    def store_projected(self, sp, tile, *proj_tables):
        if tile.slot8 % 2:
            return
        slot, _ = tile.ring(8)
        sp.wait_ge(self.proj_ready, tile.t + 2)
        for table, a, b in proj_tables:
            sp.dma_start(node_rows(table, tile, b - a), self.proj[:, slot:slot + 2, a:b]).then_inc(
                self.proj_stored[slot // 2], 16)

    def stores_done(self, sp):
        for q in range(4):
            sp.wait_ge(self.stored[q], 16 * (NT // 8))
            sp.wait_ge(self.proj_stored[q], 16 * self.proj_stores * (NT // 8))


class GcnFront:

    def __init__(self, s, weight, banks):
        self.s, self.nc, self.weight, self.banks = s, s.nc, weight, banks
        m = s.m
        self.own = m.sb("own", [TN, 8, DW])
        self.sum_t = m.sb("sum_t", [P, 8, KC * TN])
        self.sum_ps = [m.ps(f"sum_ps{i}", [P, 512]) for i in range(banks)]
        self.conv_ps = [m.ps(f"conv_ps{i}", [P, 512]) for i in range(banks)]
        self.own_loaded = m.sems("own_loaded", 4)
        self.dinv = m.sb("dinv", [TN, 8, 1])
        self.dinv_kept = m.sem("dinv_kept")
        self.own_t = m.sb("own_t", [P, 8, KC * TN])
        self.own_ready, self.sum_ready, self.conv_done, self.conv_used = (
            m.sem(n) for n in ("own_ready", "sum_ready", "conv_done", "conv_used"))

    def load_own(self, sp, tile):
        if tile.slot8 % 2 == 0:
            slot = tile.slot8
            if tile.from_(8):
                sp.wait_ge(self.s.summed, tile.t - 6)
                sp.wait_ge(self.dinv_kept, tile.t - 6)
            sp.dma_start(self.own[:, slot:slot + 2, :], node_rows(self.s.table, tile, DW)).then_inc(self.own_loaded[slot // 2], 16)

    def keep_dinv(self, dve, tile, used=None):
        if tile.slot8 % 2:
            if used and tile.from_(8):
                dve.wait_ge(used, tile.t - 7)
            pair = slice(tile.slot8 - 1, tile.slot8 + 1)
            dve.wait_ge(self.own_loaded[tile.slot8 // 2], (tile.round8 + 1) * 16)
            self.nc.vector.tensor_copy(self.dinv[:, pair, :], self.own[:, pair, D:DW]).then_inc(self.dinv_kept, 2)

    def select(self, dve, tile, further):
        s = self.s
        s.select(dve, tile)
        further.chunks(tile, lambda k, n: s.select_chunk(dve, tile, n))

    def sums(self, pe, tile, further):
        s = self.s
        slot, round8 = tile.ring(8)
        ps = self.sum_ps[slot % self.banks]
        if slot % 2 == 0:
            pe.wait_ge(self.own_loaded[slot // 2], (round8 + 1) * 16)
        if tile.from_(self.banks):
            pe.wait_ge(self.sum_ready, tile.t + 1 - self.banks)
        for c in range(KC):
            self.nc.tensor.transpose(ps[:, (KC + c) * TN:(KC + c + 1) * TN], self.own[:, slot, c * P:(c + 1) * P],
                                     s.keep["ident"][0:TN, 0:TN])

        def add(rows, sel, c, start=False):
            return self.nc.tensor.matmul(ps[:, c * TN:(c + 1) * TN], rows[:, c * P:(c + 1) * P], sel, start=start, stop=True,
                                         skip_group_check=True)

        pe.wait_ge(s.gathered[slot], (round8 + 1) * 16)
        pe.wait_ge(s.sel_ready, tile.t + 1)
        add(s.rows[:, slot, :], s.sel[:, slot, :], 0, start=True)

        def chunk(k, n):
            pe.wait_ge(s.x_sel_ready, n)
            for c in range(KC):
                last = add(s.x_rows[:], s.x_sel[:], c)
            last.then_inc(s.x_summed, 1)

        further.chunks(tile, chunk)
        add(s.rows[:, slot, :], s.sel[:, slot, :], 1).then_inc(s.summed, 1)

    def copy_own(self, act, tile):
        slot, _ = tile.ring(8)
        act.wait_ge(self.s.summed, tile.t + 1)
        self.nc.scalar.copy(self.own_t[:, slot, :], self.sum_ps[slot % self.banks][:, KC * TN:2 * KC * TN]).then_inc(self.own_ready, 1)

    def add_own(self, dve, tile):
        slot, _ = tile.ring(8)
        dve.wait_ge(self.own_ready, tile.t + 1)
        self.nc.vector.tensor_tensor(self.sum_t[:, slot, :], self.sum_ps[slot % self.banks][:, 0:KC * TN],
                                     self.own_t[:, slot, :], ALU.add).then_inc(self.sum_ready, 1)

    def convolve(self, pe, tile):
        slot, _ = tile.ring(8)
        pe.wait_ge(self.sum_ready, tile.t + 1)
        if tile.from_(self.banks):
            pe.wait_ge(self.conv_used, tile.t + 1 - self.banks)
        for c in range(KC):
            last = self.nc.tensor.matmul(self.conv_ps[slot % self.banks][0:TN, 0:D], self.sum_t[:, slot, c * TN:(c + 1) * TN],
                                         self.weight[:, c, :], start=(c == 0), stop=(c == KC - 1))
        last.then_inc(self.conv_done, 1)


def build_gcn_first(nc, keep, dram, ins):
    with ExitStack() as ctx:
        s = WindowSweep(nc, ctx, keep, dram, ins, "gcn1", dram["x1_s"], DW)
        g = GcnFront(s, keep["w1"], 4)
        m = s.m
        z = m.sb("z", [TN, 8, D])
        square_rows = m.sb("square_rows", [TN, 8, D])
        squares = m.sb("squares", [TN, 8, 1])
        length = m.sb("length", [TN, 8, 1])
        inverse = m.sb("inverse", [TN, 8, 1])
        factor_s = m.sb("factor_s", [TN, 8, 1])
        out = m.sb("out", [TN, 8, DW])
        stored = m.sems("stored", 4)
        squares_ready, length_ready, clamped, inverse_ready, scaled_ready, out_ready = (
            m.sem(n) for n in ("squares_ready", "length_ready", "clamped", "inverse_ready", "scaled_ready", "out_ready"))
        block = m.block()

        @block.gpsimd
        def _(pool):
            s.gather(pool)

        @block.sync
        def _(sp):
            further = Further(sp, keep, s.m.name)

            def store(tile):
                if tile.slot8 % 2:
                    return
                slot, _ = tile.ring(8)
                sp.wait_ge(out_ready, tile.t + 2)
                sp.dma_start(node_rows(dram["z1_s"], tile, DW), out[:, slot:slot + 2, :]).then_inc(stored[slot // 2], 16)

            sweep(sp, NT, [(0, lambda tile: g.load_own(sp, tile)), (0, lambda tile: s.load_chunks(sp, further, tile)), (16, store)],
                  further)
            for q in stored:
                sp.wait_ge(q, 16 * (NT // 8))

        @block.vector
        def _(dve):
            further = Further(dve, keep, s.m.name)

            def scale_and_bias(tile):
                slot, _ = tile.ring(8)
                dve.wait_ge(g.conv_done, tile.t + 1)
                if tile.from_(8):
                    dve.wait_ge(out_ready, tile.t - 7)
                nc.vector.scalar_tensor_tensor(out=z[:, slot, :], in0=g.conv_ps[slot % g.banks][0:TN, 0:D], scalar=g.dinv[:, slot, :],
                                               in1=keep["b1"][0:TN, :], op0=ALU.mult, op1=ALU.add).then_inc(g.conv_used, 1)

            def clamp(tile):
                if tile.slot8 % 2:
                    pair = slice(tile.slot8 - 1, tile.slot8 + 1)
                    dve.wait_ge(length_ready, tile.t + 1)
                    nc.vector.tensor_scalar(length[:, pair, :], length[:, pair, :], 1e-12, None, ALU.max).then_inc(clamped, 2)

            def invert(tile):
                if tile.slot8 % 2:
                    pair = slice(tile.slot8 - 1, tile.slot8 + 1)
                    dve.wait_ge(clamped, tile.t + 1)
                    nc.vector.reciprocal(inverse[:, pair, :], length[:, pair, :]).then_inc(inverse_ready, 2)

            def scaled_factors(tile):
                if tile.slot8 % 2:
                    pair = slice(tile.slot8 - 1, tile.slot8 + 1)
                    dve.wait_ge(inverse_ready, tile.t + 1)
                    if tile.from_(8):
                        dve.wait_ge(stored[tile.slot8 // 2], tile.round8 * 16)
                    nc.vector.tensor_copy(out[:, pair, D:DW], g.dinv[:, pair, :])
                    nc.vector.tensor_tensor(factor_s[:, pair, :], inverse[:, pair, :], g.dinv[:, pair, :], ALU.mult).then_inc(scaled_ready, 2)

            sweep(dve, NT, [(9, scaled_factors), (8, clamp), (1, lambda tile: g.keep_dinv(dve, tile, scaled_ready)),
                            (5, scale_and_bias), (2, lambda tile: g.add_own(dve, tile)),
                            (0, lambda tile: g.select(dve, tile, further)), (8, invert)], further)

        @block.scalar
        def _(act):
            def square(tile):
                slot, _ = tile.ring(8)
                act.wait_ge(g.conv_used, tile.t + 1)
                nc.scalar.activation(square_rows[:, slot, :], z[:, slot, :], ACT.Square, accum_out=squares[:, slot, :]).then_inc(squares_ready, 1)

            def lengths(tile):
                if tile.slot8 % 2:
                    pair = slice(tile.slot8 - 1, tile.slot8 + 1)
                    act.wait_ge(squares_ready, tile.t + 1)
                    nc.scalar.activation(length[:, pair, :], squares[:, pair, :], ACT.Sqrt).then_inc(length_ready, 2)

            def unit(tile):
                slot, round8 = tile.ring(8)
                act.wait_ge(scaled_ready, tile.t + 1)
                if tile.from_(8):
                    act.wait_ge(stored[slot // 2], round8 * 16)
                nc.scalar.activation(out[:, slot, 0:D], z[:, slot, :], ACT.Identity, scale=factor_s[:, slot, :]).then_inc(out_ready, 1)

            sweep(act, NT, [(2, lambda tile: g.copy_own(act, tile)), (7, lengths), (6, square), (11, unit)])

        @block.tensor
        def _(pe):
            further = Further(pe, keep, s.m.name)
            sweep(pe, NT, [(4, lambda tile: g.convolve(pe, tile)), (1, lambda tile: g.sums(pe, tile, further))], further)


def build_gcn_second(nc, keep, dram, ins):
    with ExitStack() as ctx:
        s = WindowSweep(nc, ctx, keep, dram, ins, "gcn2", dram["z1_s"], DW)
        g = GcnFront(s, keep["w2"], 2)
        p = Projection(s, keep["wc"], FILT, 2)
        m = s.m
        x1 = m.sb("x1", [TN, 8, D])
        v = m.sb("v", [TN, 8, D])
        x1_loaded = m.sems("x1_loaded", 4)
        block = m.block()

        @block.gpsimd
        def _(pool):
            s.gather(pool)

        @block.sync
        def _(sp):
            further = Further(sp, keep, s.m.name)

            def load_residual(tile):
                if tile.slot8 % 2 == 0:
                    slot = tile.slot8
                    if tile.from_(8):
                        sp.wait_ge(s.w_ready, tile.t - 6)
                    sp.dma_start(x1[:, slot:slot + 2, :], node_rows(dram["x1"], tile)).then_inc(x1_loaded[slot // 2], 16)

            sweep(sp, NT, [(0, lambda tile: g.load_own(sp, tile)), (2, load_residual),
                           (0, lambda tile: s.load_chunks(sp, further, tile)), (15, lambda tile: p.store_rows(sp, tile, dram["x2"])),
                           (19, lambda tile: p.store_projected(sp, tile, (dram["h2"], 0, FILT)))], further)
            p.stores_done(sp)

        @block.vector
        def _(dve):
            further = Further(dve, keep, s.m.name)

            def scale_and_bias(tile):
                slot, _ = tile.ring(8)
                dve.wait_ge(g.conv_done, tile.t + 1)
                nc.vector.scalar_tensor_tensor(out=v[:, slot, :], in0=g.conv_ps[slot % g.banks][0:TN, 0:D], scalar=g.dinv[:, slot, :],
                                               in1=keep["b2"][0:TN, :], op0=ALU.mult, op1=ALU.add).then_inc(g.conv_used, 1)

            def residual(tile):
                slot, round8 = tile.ring(8)
                if slot % 2 == 0:
                    dve.wait_ge(x1_loaded[slot // 2], (round8 + 1) * 16)
                dve.wait_ge(g.conv_used, tile.t + 1)
                if tile.from_(8):
                    dve.wait_ge(p.out_ready, tile.t - 7)
                nc.vector.scalar_tensor_tensor(out=s.w[:, slot, :], in0=x1[:, slot, :], scalar=2.0, in1=v[:, slot, :],
                                               op0=ALU.mult, op1=ALU.add).then_inc(s.w_ready, 1)

            sweep(dve, NT, [(1, lambda tile: g.keep_dinv(dve, tile)), (8, lambda tile: s.factor(dve, tile)),
                            (6, lambda tile: s.row_stats(dve, tile)), (5, scale_and_bias),
                            (2, lambda tile: g.add_own(dve, tile)),
                            (0, lambda tile: g.select(dve, tile, further)),
                            (6, lambda tile: s.moments(dve, tile)), (5, residual), (8, lambda tile: s.offset(dve, tile))], further)

        @block.scalar
        def _(act):
            sweep(act, NT, [(2, lambda tile: g.copy_own(act, tile)), (12, lambda tile: p.copy_turned(act, tile)), (7, lambda tile: s.deviation(act, tile)),
                            (14, lambda tile: p.copy_projected(act, tile)), (10, lambda tile: p.normal(act, tile))])

        @block.tensor
        def _(pe):
            further = Further(pe, keep, s.m.name)
            sweep(pe, NT, [(13, lambda tile: p.project(pe, tile)), (11, lambda tile: p.turn(pe, tile)),
                           (4, lambda tile: g.convolve(pe, tile)), (1, lambda tile: g.sums(pe, tile, further))], further)


def build_filter(nc, keep, dram, ins):
    with ExitStack() as ctx:
        s = WindowSweep(nc, ctx, keep, dram, ins, "filter", dram["h2"], FILT, values=(dram["cut_f"],),
                        columns=((ins["radial_flat"].rearrange("(r e) -> r e", r=RAD), RAD),))
        p = Projection(s, keep["w3"], HW, 1)
        p.proj_stores = 2
        m = s.m
        x2 = m.sb("x2", [TN, 8, D])
        radial = m.sb("radial", [RAD, 8, W])
        message = m.sb("message", [P, 8, FILT])
        x_message = m.sb("x_message", [P, FILT])
        agg_t = m.sb("agg_t", [FILT + 1, 8, TN])
        radial_ps = m.ps("radial_ps", [P, 8, FILT])
        x2_loaded = m.sems("x2_loaded", 4)
        agg_ps = [m.ps(f"agg_ps{i}", [P, 512]) for i in range(2)]
        out_ps = [m.ps(f"out_ps{i}", [P, 512]) for i in range(2)]
        loaded = m.sems("loaded", 4)
        ones_ready, radial_done, message_ready, x_radial_done, x_message_ready, agg_ready, out_done = (
            m.sem(n) for n in ("ones_ready", "radial_done", "message_ready", "x_radial_done", "x_message_ready", "agg_ready",
                               "out_done"))
        block = m.block()

        @block.gpsimd
        def _(pool):
            s.gather(pool, rows_free=message_ready)

        @block.sync
        def _(sp):
            further = Further(sp, keep, s.m.name)

            def load(tile):
                if tile.slot8 % 2:
                    return
                slot, _ = tile.ring(8)
                if tile.from_(8):
                    sp.wait_ge(radial_done, tile.t - 6)
                sp.dma_start(radial[:, slot:slot + 2, :], dram["radial"][bass.ds(tile.t, 2), :, :].rearrange(
                    "k r e -> r k e")).then_inc(loaded[slot // 2], 16)

            def load_residual(tile):
                if tile.slot8 % 2 == 0:
                    slot = tile.slot8
                    if tile.from_(8):
                        sp.wait_ge(s.w_ready, tile.t - 6)
                    sp.dma_start(x2[:, slot:slot + 2, :], node_rows(dram["x2"], tile)).then_inc(x2_loaded[slot // 2], 16)

            sweep(sp, NT, [(0, load), (2, load_residual), (1, lambda tile: s.load_chunks(sp, further, tile)),
                           (15, lambda tile: p.store_rows(sp, tile, dram["x3"])),
                           (18, lambda tile: p.store_projected(sp, tile, (dram["h3"], 0, HW), (dram["a_src"], D, HW)))], further)
            p.stores_done(sp)

        @block.vector
        def _(dve):
            further = Further(dve, keep, s.m.name)
            nc.vector.memset(agg_t[FILT:FILT + 1, :, :], 1.0).then_inc(ones_ready, 1)

            def messages(tile):
                slot, round8 = tile.ring(8)
                dve.wait_ge(s.gathered[slot], (round8 + 1) * 16)
                dve.wait_ge(radial_done, tile.t + 1)
                nc.vector.tensor_tensor(message[:, slot, :], s.rows[:, slot, :], radial_ps[:, 0, :], ALU.mult).then_inc(
                    message_ready, 1)
                s.select(dve, tile, scale=lambda slot_, tile_: keep["cut"][:, bass.ds(tile_.t, 1)])

                def chunk(k, n):
                    dve.wait_ge(x_radial_done, n)
                    dve.wait_ge(s.x_gathered, n * 16)
                    nc.vector.tensor_tensor(x_message[:], s.x_rows[:], radial_ps[:, 1, :], ALU.mult).then_inc(x_message_ready, 1)
                    s.select_chunk(dve, tile, n, scale=s.x_values[:, 0:1])

                further.chunks(tile, chunk)

            def residual(tile):
                slot, round8 = tile.ring(8)
                dve.wait_ge(out_done, tile.t + 1)
                if slot % 2 == 0:
                    dve.wait_ge(x2_loaded[slot // 2], (round8 + 1) * 16)
                if tile.from_(8):
                    dve.wait_ge(p.out_ready, tile.t - 7)
                nc.vector.tensor_tensor(s.w[:, slot, :], out_ps[slot % 2][0:TN, 0:D], x2[:, slot, :], ALU.add).then_inc(s.w_ready, 1)

            sweep(dve, NT, [(8, lambda tile: s.factor(dve, tile)), (6, lambda tile: s.row_stats(dve, tile)), (5, residual),
                            (1, messages),
                            (6, lambda tile: s.moments(dve, tile)), (8, lambda tile: s.offset(dve, tile))], further)

        @block.scalar
        def _(act):
            def copy_sum(tile):
                slot, _ = tile.ring(8)
                act.wait_ge(s.summed, tile.t + 1)
                nc.scalar.copy(agg_t[0:FILT, slot, :], agg_ps[slot % 2][0:FILT, 0:TN]).then_inc(agg_ready, 1)

            sweep(act, NT, [(3, copy_sum), (13, lambda tile: p.copy_projected(act, tile)),
                            (12, lambda tile: p.copy_turned(act, tile)), (7, lambda tile: s.deviation(act, tile)),
                            (10, lambda tile: p.normal(act, tile))])

        @block.tensor
        def _(pe):
            further = Further(pe, keep, s.m.name)
            pe.wait_ge(ones_ready, 1)

            def filters(tile):
                slot, round8 = tile.ring(8)
                if slot % 2 == 0:
                    pe.wait_ge(loaded[slot // 2], (round8 + 1) * 16)
                if tile.from_(1):
                    pe.wait_ge(message_ready, tile.t)
                nc.tensor.matmul(radial_ps[:, 0, :], radial[:, slot, :], keep["wrad"][:], start=True, stop=True).then_inc(radial_done, 1)

            def sums(tile):
                slot, _ = tile.ring(8)
                pe.wait_ge(message_ready, tile.t + 1)
                pe.wait_ge(s.sel_ready, tile.t + 1)
                ps = agg_ps[slot % 2][0:FILT, :]
                half = TN // 2

                def add(msg, sel, a, b, start=False):
                    return nc.tensor.matmul(ps[:, a:b], msg, sel[:, a:b], start=start, stop=True, skip_group_check=True)

                add(message[:, slot, :], s.sel[:, slot, :], 0, half, start=True)

                def chunk(k, n):
                    pe.wait_ge(s.x_loaded, n * (16 * s.x_loads))
                    nc.tensor.matmul(radial_ps[:, 1, :], s.x_cols[0:RAD, :], keep["wrad"][:], start=True, stop=True).then_inc(
                        x_radial_done, 1)
                    pe.wait_ge(s.x_sel_ready, n)
                    pe.wait_ge(x_message_ready, n)
                    add(x_message[:], s.x_sel[:], 0, TN).then_inc(s.x_summed, 1)

                further.chunks(tile, chunk)
                add(message[:, slot, :], s.sel[:, slot, :], half, TN).then_inc(s.summed, 1)

            def output(tile):
                slot, _ = tile.ring(8)
                pe.wait_ge(agg_ready, tile.t + 1)
                if tile.from_(2):
                    pe.wait_ge(s.w_ready, tile.t - 1)
                nc.tensor.matmul(out_ps[slot % 2][0:TN, 0:D], agg_t[:, slot, :], keep["m2"][:], start=True, stop=True).then_inc(out_done, 1)

            sweep(pe, NT, [(13, lambda tile: p.project(pe, tile)), (11, lambda tile: p.turn(pe, tile)), (4, output), (2, sums),
                           (0, filters)], further)


def build_scores(nc, keep, dram, ins):
    with ExitStack() as ctx:
        m = Memory(nc, ctx, "score")
        index = m.sb("index", [P, 2, 8], I32)
        rows = m.sb("rows", [P, 8, HW])
        src_score = m.sb("src_score", [P, 8, H])
        attr = m.sb("attr", [4, 8, W])
        factor = m.sb("factor", [P, 8, D])
        prod = m.sb("prod", [P, 8, D])
        dot = m.sb("dot", [P, 8, H])
        total = m.sb("total", [P, 8, H])
        leaky = m.sb("leaky", [P, 8, H])
        alpha_t = m.sb("alpha_t", [H, 8, W])
        enc_ps = [m.ps(f"enc_ps{i}", [P, 512]) for i in range(2)]
        alpha_ps = [m.ps(f"alpha_ps{i}", [P, 512]) for i in range(2)]
        index_ready, passed = m.sem("index_ready"), m.sem("passed")
        gathered, loaded, stored = m.sems("gathered", 8), m.sems("loaded", 4), m.sems("stored", 4)
        enc_done, factor_ready, prod_ready, dot_ready, total_ready, leaky_ready, turned, alpha_ready = (
            m.sem(n) for n in ("enc_done", "factor_ready", "prod_ready", "dot_ready", "total_ready", "leaky_ready", "turned",
                               "alpha_ready"))
        block = m.block()

        @block.gpsimd
        def _(pool):
            def gather(tile):
                slot, round_ = tile.ring(8)
                if slot % 4 == 0:
                    if tile.from_(8):
                        pool.wait_ge(total_ready, tile.t - 4)
                    for k, name in enumerate(("dst_e", "src_e")):
                        last = nc.gpsimd.tensor_copy(index[:, k, slot:slot + 4], keep[name][:, bass.ds(tile.t, 4)])
                    last.then_inc(index_ready, 1)
                    wait_apart(pool, index_ready, round_ * 2 + slot // 4 + 1, passed)
                pool.indirect_dma_start(out=rows[:, slot, :], out_offset=None, in_=dram["h3"],
                                        in_offset=bass.IndirectOffsetOnAxis(ap=index[:, 0, slot:slot + 1], axis=0)).then_inc(gathered[slot], 16)
                pool.indirect_dma_start(out=src_score[:, slot, :], out_offset=None, in_=dram["a_src"],
                                        in_offset=bass.IndirectOffsetOnAxis(ap=index[:, 1, slot:slot + 1], axis=0)).then_inc(gathered[slot], 16)

            sweep(pool, ET, [(0, gather)])

        @block.sync
        def _(sp):
            def load(tile):
                if tile.slot8 % 2:
                    return
                slot, _ = tile.ring(8)
                if tile.from_(8):
                    sp.wait_ge(enc_done, tile.t - 6)
                sp.dma_start(attr[:, slot:slot + 2, :], ins["attr3t"][:, bass.ds(tile.t * W, 2 * W)].rearrange(
                    "r (k e) -> r k e", k=2)).then_inc(loaded[slot // 2], 16)

            def store(tile):
                if tile.slot8 % 2:
                    return
                slot, _ = tile.ring(8)
                sp.wait_ge(alpha_ready, tile.t + 2)
                sp.dma_start(dram["alpha"][:, bass.ds(tile.t * W, 2 * W)].rearrange("h (k e) -> h k e", k=2),
                             alpha_t[:, slot:slot + 2, :]).then_inc(stored[slot // 2], 16)

            sweep(sp, ET, [(0, load), (11, store)])
            for q in stored:
                sp.wait_ge(q, 16 * (ET // 8))

        @block.tensor
        def _(pe):
            def encode(tile):
                slot, round8 = tile.ring(8)
                if slot % 2 == 0:
                    pe.wait_ge(loaded[slot // 2], (round8 + 1) * 16)
                if tile.from_(2):
                    pe.wait_ge(factor_ready, tile.t - 1)
                nc.tensor.matmul(enc_ps[slot % 2][:, 0:D], attr[:, slot, :], keep["wedge"][:], start=True, stop=True).then_inc(enc_done, 1)

            def turn(tile):
                slot, _ = tile.ring(8)
                pe.wait_ge(leaky_ready, tile.t + 1)
                if tile.from_(2):
                    pe.wait_ge(alpha_ready, tile.t - 1)
                nc.tensor.transpose(alpha_ps[slot % 2][0:H, 0:W], leaky[:, slot, :], keep["ident"][:]).then_inc(turned, 1)

            sweep(pe, ET, [(0, encode), (5, turn)])

        @block.vector
        def _(dve):
            def factors(tile):
                slot, _ = tile.ring(8)
                dve.wait_ge(enc_done, tile.t + 1)
                nc.vector.scalar_tensor_tensor(out=factor[:, slot, :], in0=enc_ps[slot % 2][:, 0:D], scalar=0.0, in1=keep["adst"][:],
                                               op0=ALU.max, op1=ALU.add).then_inc(factor_ready, 1)

            def products(tile):
                slot, round8 = tile.ring(8)
                dve.wait_ge(gathered[slot], (round8 + 1) * 32)
                dve.wait_ge(factor_ready, tile.t + 1)
                nc.vector.tensor_tensor(prod[:, slot, :], factor[:, slot, :], rows[:, slot, 0:D], ALU.mult).then_inc(prod_ready, 1)

            def dots(tile):
                slot, _ = tile.ring(8)
                dve.wait_ge(prod_ready, tile.t + 1)
                nc.vector.tensor_reduce(dot[:, slot, :], prod[:, slot, :].rearrange("p (h d) -> p h d", h=H), AX_X, ALU.add).then_inc(dot_ready, 1)

            def totals(tile):
                slot, _ = tile.ring(8)
                dve.wait_ge(dot_ready, tile.t + 1)
                nc.vector.tensor_tensor(total[:, slot, :], dot[:, slot, :], src_score[:, slot, :], ALU.add).then_inc(total_ready, 1)

            def slopes(tile):
                slot, _ = tile.ring(8)
                dve.wait_ge(total_ready, tile.t + 1)
                if tile.from_(8):
                    dve.wait_ge(turned, tile.t - 7)
                nc.vector.scalar_tensor_tensor(out=leaky[:, slot, :], in0=total[:, slot, :], scalar=0.2, in1=total[:, slot, :],
                                               op0=ALU.mult, op1=ALU.max).then_inc(leaky_ready, 1)

            sweep(dve, ET, [(1, factors), (4, slopes), (2, products), (3, totals), (2, dots)])

        @block.scalar
        def _(act):
            def copy_alpha(tile):
                slot, round8 = tile.ring(8)
                act.wait_ge(turned, tile.t + 1)
                if tile.from_(8):
                    act.wait_ge(stored[slot // 2], round8 * 16)
                nc.scalar.copy(alpha_t[:, slot, :], alpha_ps[slot % 2][0:H, 0:W]).then_inc(alpha_ready, 1)

            sweep(act, ET, [(6, copy_alpha)])


def build_softmax(nc, keep, dram, ins):
    with ExitStack() as ctx:
        m = Memory(nc, ctx, "softmax")
        alpha = m.sb("alpha", [P, SQ])
        dst = m.sb("dst", [P, SQ + 2], I32)
        start = m.sb("start", [P, SQ])
        inside = m.sb("inside", [P, SQ])
        reset = m.sb("reset", [P, SQ])
        end = m.sb("end", [P, SQ])
        before_end = m.sb("before_end", [P, SQ])
        run = m.sb("run", [P, SQ])
        last = m.sb("last", [P, SQ])
        seg = m.sb("seg", [P, SQ])
        col = m.sb("col", [P, 5])
        flags = m.sb("flags", [H, 2, SEG])
        no_start, no_end, start_reset = m.sb("no_start", [H, SEG]), m.sb("no_end", [H, SEG]), m.sb("start_reset", [H, SEG])
        piece = m.sb("piece", [H, SEG])
        piece_sum = m.sb("piece_sum", [H, SEG])
        carry = m.sb("carry", [H, SEG])
        carry_in = m.sb("carry_in", [P, 1])
        windows = m.sb("windows", [P, NJ, H, W])
        loaded, chain_sem, exp_ready, shifted = m.sem("loaded"), m.sem("chain"), m.sem("exp_ready"), m.sem("shifted")
        flags_ready, flags_out, flags_back = m.sem("flags_ready"), m.sem("flags_out"), m.sem("flags_back")
        outcome_ready, outcome_out, outcome_back = m.sem("outcome_ready"), m.sem("outcome_out"), m.sem("outcome_back")
        carry_ready, carry_out, carry_back = m.sem("carry_ready"), m.sem("carry_out"), m.sem("carry_back")
        attn_ready, attn_out = m.sem("attn_ready"), m.sem("attn_out")
        window_in, window_out = m.sems("window_in", NJ), m.sem("window_out")
        flat = lambda t: t.rearrange("h (s q) -> (h s) q", s=SEG)
        SCANS = 4
        block = m.block()

        @block.sync
        def _(sp):
            sp.dma_start(alpha[:], flat(dram["alpha"])).then_inc(loaded, 16)
            for h in range(H):
                sp.dma_start(dst[h * SEG:(h + 1) * SEG, :], bass.AP(tensor=ins["dst_ext"].tensor, offset=0,
                             ap=[[SQ, SEG], [1, SQ + 2]])).then_inc(loaded, 16)
            carry_d = dram["carry"]
            sp.wait_ge(flags_ready, 1)
            for k in range(2):
                sp.dma_start(carry_d[k].unsqueeze(1), col[:, k:k + 1]).then_inc(flags_out, 16)
            sp.wait_ge(flags_out, 32)
            for k in range(2):
                sp.dma_start(flags[:, k, :], carry_d[k].rearrange("(h s) -> h s", h=H)).then_inc(flags_back, 16)
            for n in range(SCANS):
                sp.wait_ge(outcome_ready, n + 1)
                sp.dma_start(carry_d[2].unsqueeze(1), col[:, 2:3]).then_inc(outcome_out, 16)
                sp.wait_ge(outcome_out, 16 * (n + 1))
                sp.dma_start(piece[:], carry_d[2].rearrange("(h s) -> h s", h=H)).then_inc(outcome_back, 16)
                sp.wait_ge(carry_ready, n + 1)
                sp.dma_start(carry_d[3].rearrange("(h s) -> h s", h=H), carry[:]).then_inc(carry_out, 16)
                sp.wait_ge(carry_out, 16 * (n + 1))
                sp.dma_start(carry_in[:], carry_d[3].unsqueeze(1)).then_inc(carry_back, 16)
            sp.wait_ge(attn_ready, 1)
            sp.dma_start(flat(dram["attn"]), seg[:]).then_inc(attn_out, 16)
            for j in range(NJ):
                sp.wait_ge(window_in[j], 16 * H)
                sp.dma_start(dram["attn_windows"][j * P:(j + 1) * P, :, :], windows[:, j, :, :]).then_inc(window_out, 16)
            sp.wait_ge(window_out, 16 * NJ)

        @block.gpsimd
        def _(pool):
            pool.wait_ge(attn_out, 16)
            attn = dram["attn"].rearrange("h e -> (h e)").unsqueeze(1)
            for j in range(NJ):
                for h in range(H):
                    pool.indirect_dma_start(out=windows[:, j, h, :], out_offset=None, in_=attn,
                                            in_offset=bass.IndirectOffsetOnAxis(ap=keep["start_cols"][:, h, j:j + 1], axis=0),
                                            ).then_inc(window_in[j], 16)

        @block.scalar
        def _(act):
            act.wait_ge(shifted, 1)
            nc.scalar.activation(alpha[:], alpha[:], ACT.Exp).then_inc(exp_ready, 1)

        @block.vector
        def _(dve):
            chain = Chained(dve, chain_sem)
            dve.wait_ge(loaded, 16 * (H + 1))
            chain(nc.vector.tensor_tensor(start[:], dst[:, 1:SQ + 1], dst[:, 0:SQ], ALU.not_equal))
            chain(nc.vector.tensor_tensor(end[:], dst[:, 1:SQ + 1], dst[:, 2:SQ + 2], ALU.not_equal))
            chain(nc.vector.tensor_scalar(inside[:], start[:], -1.0, 1.0, ALU.mult, ALU.add))
            chain(nc.vector.tensor_scalar(reset[:], start[:], -BIG, None, ALU.mult))
            chain(nc.vector.tensor_scalar(before_end[:], end[:], -1.0, 1.0, ALU.mult, ALU.add))
            chain(nc.vector.tensor_reduce(col[:, 0:1], start[:], AX_X, ALU.max))
            chain(nc.vector.tensor_reduce(col[:, 1:2], end[:], AX_X, ALU.max))
            dve.sem_inc(flags_ready, 1)
            dve.wait_ge(flags_back, 32)
            chain(nc.vector.tensor_scalar(no_start[:], flags[:, 0, :], -1.0, 1.0, ALU.mult, ALU.add))
            chain(nc.vector.tensor_scalar(no_end[:], flags[:, 1, :], -1.0, 1.0, ALU.mult, ALU.add))
            chain(nc.vector.tensor_scalar(start_reset[:], flags[:, 0, :], -BIG, None, ALU.mult))
            scans = [0]

            def carried_scan(out, keep_, add, ops, piece_keep, empty, backward=False):
                flip = (lambda t: t[:, ::-1]) if backward else (lambda t: t[:, :])
                final = out[:, 0:1] if backward else out[:, SQ - 1:SQ]
                n = scans[0] = scans[0] + 1
                chain(nc.vector.tensor_tensor_scan(flip(out), flip(keep_), flip(add), empty, ops[0], ops[1]))
                chain(nc.vector.tensor_copy(col[:, 2:3], final))
                dve.sem_inc(outcome_ready, 1)
                dve.wait_ge(outcome_back, 16 * n)
                chain(nc.vector.tensor_tensor_scan(flip(piece_sum), flip(piece_keep), flip(piece), empty, ops[0], ops[1]))
                chain(nc.vector.memset(carry[:], empty))
                to, of = (carry[:, 0:SEG - 1], piece_sum[:, 1:SEG]) if backward else (carry[:, 1:SEG], piece_sum[:, 0:SEG - 1])
                chain(nc.vector.tensor_copy(to, of))
                dve.sem_inc(carry_ready, 1)
                dve.wait_ge(carry_back, 16 * n)
                chain(nc.vector.tensor_tensor_scan(flip(out), flip(keep_), flip(add), carry_in[:, 0:1], ops[0], ops[1]))

            def spread_last(out, value):
                chain(nc.vector.tensor_tensor(last[:], value[:], end[:], ALU.mult))
                carried_scan(out, before_end, last, (ALU.mult, ALU.add), no_end, 0.0, backward=True)

            carried_scan(run, reset, alpha, (ALU.add, ALU.max), start_reset, -BIG)
            spread_last(seg, run)
            nc.vector.tensor_tensor(alpha[:], alpha[:], seg[:], ALU.subtract).then_inc(shifted, 1)
            dve.wait_ge(exp_ready, 1)
            carried_scan(run, inside, alpha, (ALU.mult, ALU.add), no_start, 0.0)
            spread_last(seg, run)
            chain(nc.vector.tensor_scalar(seg[:], seg[:], 1e-10, None, ALU.max))
            chain(nc.vector.reciprocal(seg[:], seg[:]))
            nc.vector.tensor_tensor(seg[:], seg[:], alpha[:], ALU.mult).then_inc(attn_ready, 1)


def build_gat(nc, keep, dram, ins, out):
    with ExitStack() as ctx:
        s = WindowSweep(nc, ctx, keep, dram, ins, "gat", dram["h3"], HW, columns=((dram["attn"], H),))
        m = s.m
        x3 = m.sb("x3", [TN, 8, D])
        attn = m.sb("attn", [H, 8, W])
        message = m.sb("message", [P, 8, D])
        x_message = m.sb("x_message", [P, D])
        normed = m.sb("normed", [TN, 8, D])
        attn_ps = [m.ps(f"attn_ps{i}", [P, 512]) for i in range(2)]
        x_attn_ps = m.ps("x_attn_ps", [P, 512])
        sum_ps = [m.ps(f"sum_ps{i}", [P, 512]) for i in range(2)]
        loaded, x3_loaded, stored = m.sems("loaded", 4), m.sems("x3_loaded", 4), m.sems("stored", 4)
        turned, message_ready, x_turned, x_message_ready, out_ready = (
            m.sem(n) for n in ("turned", "message_ready", "x_turned", "x_message_ready", "out_ready"))
        block = m.block()

        @block.gpsimd
        def _(pool):
            s.gather(pool, rows_free=message_ready)

        @block.sync
        def _(sp):
            further = Further(sp, keep, s.m.name)

            def load(tile):
                if tile.slot8 % 2:
                    return
                slot, _ = tile.ring(8)
                if tile.from_(8):
                    sp.wait_ge(turned, tile.t - 6)
                sp.dma_start(attn[:, slot:slot + 2, :], dram["attn_windows"][bass.ds(tile.t, 2), :, :].rearrange(
                    "k h e -> h k e")).then_inc(loaded[slot // 2], 16)

            def load_residual(tile):
                if tile.slot8 % 2 == 0:
                    slot = tile.slot8
                    if tile.from_(8):
                        sp.wait_ge(s.w_ready, tile.t - 6)
                    sp.dma_start(x3[:, slot:slot + 2, :], node_rows(dram["x3"], tile)).then_inc(x3_loaded[slot // 2], 16)

            def store(tile):
                if tile.slot8 % 2:
                    return
                slot, _ = tile.ring(8)
                sp.wait_ge(out_ready, tile.t + 2)
                sp.dma_start(node_rows(out, tile), normed[:, slot:slot + 2, :]).then_inc(stored[slot // 2], 16)

            sweep(sp, NT, [(0, load), (0, load_residual), (1, lambda tile: s.load_chunks(sp, further, tile)), (13, store)], further)
            for q in stored:
                sp.wait_ge(q, 16 * (NT // 8))

        @block.vector
        def _(dve):
            further = Further(dve, keep, s.m.name)
            heads = lambda rows: rows[:, 0:D].rearrange("p (h d) -> p h d", h=H)
            weights = lambda ps: ps[:, 0:H].unsqueeze(2).broadcast_to([P, H, HD])

            def messages(tile):
                slot, round8 = tile.ring(8)
                dve.wait_ge(s.gathered[slot], (round8 + 1) * 16)
                dve.wait_ge(turned, tile.t + 1)
                nc.vector.tensor_tensor(heads(message[:, slot, :]), heads(s.rows[:, slot, :]), weights(attn_ps[slot % 2]),
                                        ALU.mult).then_inc(message_ready, 1)
                s.select(dve, tile)

                def chunk(k, n):
                    dve.wait_ge(x_turned, n)
                    dve.wait_ge(s.x_gathered, n * 16)
                    nc.vector.tensor_tensor(heads(x_message[:]), heads(s.x_rows[:]), weights(x_attn_ps), ALU.mult).then_inc(x_message_ready, 1)
                    s.select_chunk(dve, tile, n)

                further.chunks(tile, chunk)

            def residual(tile):
                slot, round8 = tile.ring(8)
                dve.wait_ge(s.summed, tile.t + 1)
                if slot % 2 == 0:
                    dve.wait_ge(x3_loaded[slot // 2], (round8 + 1) * 16)
                if tile.from_(8):
                    dve.wait_ge(out_ready, tile.t - 7)
                nc.vector.tensor_tensor(s.w[:, slot, :], sum_ps[slot % 2][0:TN, 0:D], x3[:, slot, :], ALU.add).then_inc(s.w_ready, 1)

            sweep(dve, NT, [(6, lambda tile: s.factor(dve, tile)), (4, lambda tile: s.row_stats(dve, tile)), (3, residual),
                            (1, messages), (4, lambda tile: s.moments(dve, tile)), (6, lambda tile: s.offset(dve, tile))], further)

        @block.scalar
        def _(act):
            def normal(tile):
                slot, round8 = tile.ring(8)
                act.wait_ge(s.shift_ready, tile.t + 1)
                if tile.from_(8):
                    act.wait_ge(stored[slot // 2], round8 * 16)
                nc.scalar.activation(normed[:, slot, :], s.w[:, slot, :], ACT.Identity, bias=s.shift[:, slot, :],
                                     scale=s.rstd[:, slot, :]).then_inc(out_ready, 1)

            sweep(act, NT, [(5, lambda tile: s.deviation(act, tile)), (8, normal)])

        @block.tensor
        def _(pe):
            further = Further(pe, keep, s.m.name)

            def turn(tile):
                slot, round8 = tile.ring(8)
                if slot % 2 == 0:
                    wait_apart(pe, loaded[slot // 2], (round8 + 1) * 16, s.passed[3])
                nc.tensor.transpose(attn_ps[slot % 2][:, 0:H], attn[:, slot, :], keep["ident"][0:H, 0:H]).then_inc(turned, 1)

            def sums(tile):
                slot, _ = tile.ring(8)
                ps = sum_ps[slot % 2][0:TN, 0:D]
                if tile.from_(2):
                    wait_apart(pe, s.w_ready, tile.t - 1, s.passed[3])
                nc.tensor.matmul(ps, keep["ones_b"][0:3, :], keep["bias3"][:], start=True, stop=True, skip_group_check=True)

                def chunk(k, n):
                    wait_apart(pe, s.x_loaded, n * (16 * s.x_loads), s.passed[3])
                    nc.tensor.transpose(x_attn_ps[:, 0:H], s.x_cols[0:H, :], keep["ident"][0:H, 0:H]).then_inc(x_turned, 1)
                    pe.wait_ge(s.x_sel_ready, n)
                    pe.wait_ge(x_message_ready, n)
                    nc.tensor.matmul(ps, s.x_sel[:], x_message[:], start=False, stop=True, skip_group_check=True).then_inc(s.x_summed, 1)

                further.chunks(tile, chunk)
                pe.wait_ge(message_ready, tile.t + 1)
                pe.wait_ge(s.sel_ready, tile.t + 1)
                nc.tensor.matmul(ps, s.sel[:, slot, :], message[:, slot, :], start=False, stop=True, skip_group_check=True).then_inc(
                    s.summed, 1)

            sweep(pe, NT, [(2, sums), (0, turn)], further)


def build(nc, ins, out):
    def scratch(name, shape):
        return nc.dram_tensor(name, shape, F32, kind="Internal").ap()

    dram = {
        "dst_f": scratch("dst_f", [EP]), "src_f": scratch("src_f", [EP]), "cut_f": scratch("cut_f", [EP]),
        "icnt_f": scratch("icnt_f", [EP]),
        "starts": nc.dram_tensor("tile_starts", [NJ * P], I32, kind="Internal").ap(),
        "radial": scratch("radial_windows", [NJ * P, RAD, W]),
        "x1": scratch("x1", [NP, D]), "x1_s": scratch("x1_s", [NP, DW]), "z1_s": scratch("z1_s", [NP, DW]), "x2": scratch("x2", [NP, D]),
        "h2": scratch("h2", [NP, FILT]), "x3": scratch("x3", [NP, D]), "h3": scratch("h3", [NP, HW]),
        "a_src": scratch("a_src_h", [NP, H]), "alpha": scratch("alpha", [H, EP]), "attn": scratch("attn", [H, EP]),
        "attn_windows": scratch("attn_windows", [NJ * P, H, W]), "carry": scratch("carry", [4, P]),
    }
    with ExitStack() as ctx:
        m = Memory(nc, ctx, "keep")
        keep = {
            "wl": m.sb("wl", [P, KC, D]), "wr": m.sb("wr", [P, KC, D]), "wln": m.sb("wln", [P, KC, D]),
            "w1": m.sb("w1", [P, KC, D]), "w2": m.sb("w2", [P, KC, D]), "w3": m.sb("w3", [P, KC, HW]),
            "bl": m.sb("bl", [P, KC]), "wrad": m.sb("wrad", [RAD, FILT]), "wedge": m.sb("wedge", [4, D]),
            "b1": m.sb("b1", [P, D]), "b2": m.sb("b2", [P, D]), "bias3": m.sb("bias3", [3, D], BF16), "adst": m.sb("adst", [P, D]),
            "wc": m.sb("wc", [P, KC, FILT]), "m2": m.sb("m2", [FILT + 1, D]),
            "ident": m.sb("ident", [P, P]), "ones": m.sb("ones", [P, P]), "eps": m.sb("eps", [P, 1]),
            "iota": m.sb("iota", [P, TN]), "base": m.sb("base", [P, NT]),
            "src_e": m.sb("src_e", [P, ET], I32), "dst_e": m.sb("dst_e", [P, ET], I32),
            "src": m.sb("src", [P, NT], I32), "drel": m.sb("drel", [P, NT]), "cut": m.sb("cut", [P, NT]),
            "ones_b": m.sb("ones_b", [P, TN], BF16), "icnt": m.sb("icnt", [P, NT]),
            "starts": m.sb("starts", [1, NT], I32), "over": m.sb("over", [1, NT + 1], I32),
            "start_cols": m.sb("start_cols", [P, RAD, NJ], I32),
        }
        build_setup(nc, keep, dram, ins)
        build_sage(nc, keep, dram, ins)
        build_gcn_first(nc, keep, dram, ins)
        build_gcn_second(nc, keep, dram, ins)
        build_filter(nc, keep, dram, ins)
        build_scores(nc, keep, dram, ins)
        build_softmax(nc, keep, dram, ins)
        build_gat(nc, keep, dram, ins, out)


def layouts(inputs):
    import numpy as np

    a = {k: np.asarray(v) for k, v in inputs.items()}
    rows = lambda v, n: np.concatenate([v, np.zeros((n - v.shape[0],) + v.shape[1:], v.dtype)])
    x = rows(a["x"], NP)
    src, dst = rows(a["src"], EP), np.concatenate([a["dst"], np.full(EP - E, PAD_DST, a["dst"].dtype)])
    attr3 = np.concatenate([rows(a["edge_attr_3"], EP), np.ones((EP, 1), a["edge_attr_3"].dtype)], axis=1)
    radial = np.ascontiguousarray(rows(a["edge_attr_12"], EP).T)
    column = lambda v: np.ascontiguousarray(v.reshape(KC, P).T)
    t = lambda name: np.ascontiguousarray(a[name].T)
    return {
        "x": x, "xt": np.ascontiguousarray(x.T), "src_flat": src,
        "dst_ext": np.concatenate([np.full(1, -1, dst.dtype), dst, np.full(1, -1, dst.dtype)]),
        "src_by_tile": np.ascontiguousarray(src.reshape(ET, W).T), "dst_by_tile": np.ascontiguousarray(dst.reshape(ET, W).T),
        "dist_flat": rows(a["edge_weight"], EP), "radial_flat": radial.reshape(-1),
        "attr3t": np.ascontiguousarray(attr3.T),
        "L0_wlt": t("L0_gnn_W_l"), "L0_wrt": t("L0_gnn_W_r"), "L0_wlnt": t("L0_gnn_W_ln"), "L0_bl": column(a["L0_gnn_b_l"]),
        "L1_w1": a["L1_gnn_W1"], "L1_w2": a["L1_gnn_W2"], "L1_b1": a["L1_gnn_b1"], "L1_b2": a["L1_gnn_b2"],
        "L2_wn": a["L2_gnn_W_node_to_message"], "L2_wradt": t("L2_gnn_W_radial_to_message"), "L2_lin1t": t("L2_gnn_W_lin1"),
        "L2_lin2b": np.concatenate([a["L2_gnn_W_lin2"], a["L2_gnn_b_lin2"][:, None]], axis=1),
        "L2_mnt": t("L2_gnn_W_message_to_node"),
        "L3_wt": t("L3_gnn_W"), "L3_w": a["L3_gnn_W"], "L3_asrc": column(a["L3_gnn_a_src"].reshape(-1)),
        "L3_adst": a["L3_gnn_a_dst"].reshape(-1), "L3_bias": a["L3_gnn_bias"],
        "L3_wedge": np.concatenate([t("L3_gnn_edge_W"), a["L3_gnn_edge_b"][None]], axis=0),
    }


def kernel(**inputs):
    import numpy as np
    import concourse.bacc as bacc
    from concourse.bass_utils import run_bass_kernel_spmd

    nc = bacc.Bacc("TRN2", target_bir_lowering=False, num_devices=1)
    arrays = layouts(inputs)
    ins = {k: nc.dram_tensor(f"in_{k}", v.shape, mybir.dt.from_np(v.dtype), kind="ExternalInput").ap() for k, v in arrays.items()}
    out = nc.dram_tensor("out", (NP, D), F32, kind="ExternalOutput").ap()
    build(nc, ins, out)
    r = run_bass_kernel_spmd(nc, [{f"in_{k}": v for k, v in arrays.items()}], core_ids=[0])
    return r.results[0]["out"][:N]
```
